# Optimizing a Trainium2 kernel written in Bass

```python
import numpy as np
import jax
import jax.numpy as jnp

def _softmax(x, axis=-1):
    return jax.nn.softmax(x, axis=axis)

def _gelu(x):
    return jax.nn.gelu(x, approximate=True)

def _silu(x):
    return jax.nn.silu(x)

def _sigmoid(x):
    return jax.nn.sigmoid(x)

def _layernorm(x, axis=-1, eps=1e-05):
    m = jnp.mean(x, axis=axis, keepdims=True)
    v = jnp.var(x, axis=axis, keepdims=True)
    return (x - m) / jnp.sqrt(v + eps)

def _scatter_add(tgt, idx, src, axis=0):
    return tgt.at[idx].add(src)

def _segment_sum(src, seg, n):
    return jax.ops.segment_sum(src, seg, n)
kernel_name = 'mk_adaln_d2_jaxref_r8_58d1b9'

def setup_inputs(seed: int=0):
    np.random.seed(seed)
    _w = jnp.asarray

    def _L0_attn_setup():
        import jax, jax.numpy as jnp
        import numpy as np
        H = 16
        KV = 4
        D = 128
        THETA = 10000.0
        MASK_NEG = -2.3819763e+38

        def rope(x):
            B, S, nh, Dd = x.shape
            half = Dd // 2
            freqs = 1.0 / THETA ** (jnp.arange(0, Dd, 2, dtype=jnp.float32) / Dd)
            ang = jnp.arange(S, dtype=jnp.float32)[:, None] * freqs[None, :]
            cos = jnp.cos(ang)[None, :, None, :]
            sin = jnp.sin(ang)[None, :, None, :]
            x1, x2 = (x[..., :half], x[..., half:])
            return jnp.concatenate([x1 * cos - x2 * sin, x1 * sin + x2 * cos], axis=-1).astype(x.dtype)
        key = jax.random.key(seed)
        k1, k2, k3 = jax.random.split(key, 3)
        B, S, dm = (2, 256, 256)
        x = jax.random.normal(k1, (B, S, dm), dtype=jnp.float32)
        lim_qkv = 1.0 / np.sqrt(dm)
        lim_o = 1.0 / np.sqrt(H * D)
        Wqkv = jax.random.uniform(k2, (dm, (H + 2 * KV) * D), dtype=jnp.float32, minval=-lim_qkv, maxval=lim_qkv)
        Wo = jax.random.uniform(k3, (H * D, dm), dtype=jnp.float32, minval=-lim_o, maxval=lim_o)
        return {'x': x, 'Wqkv': Wqkv, 'Wo': Wo}
    _L0_attn_in = _L0_attn_setup()

    def _L0_ffn_setup():
        import jax, jax.numpy as jnp
        import numpy as np

        def _sparsify_2to4(h):
            B, S, I = h.shape
            g = h.reshape(B, S, I // 4, 4)
            a = jnp.abs(g)
            _, idx = jax.lax.top_k(a, 2)
            pos = jnp.arange(4)
            mask = (pos == idx[..., 0:1]) | (pos == idx[..., 1:2])
            return (g * mask.astype(g.dtype)).reshape(B, S, I)
        key = jax.random.key(seed)
        k1, k2, k3, k4 = jax.random.split(key, 4)
        B, S, H, I = (4, 256, 256, 1024)
        x = jax.random.normal(k1, (B, S, H), dtype=jnp.float32)
        w_gate = jax.random.normal(k2, (H, I), dtype=jnp.float32) / np.sqrt(H)
        w_up = jax.random.normal(k3, (H, I), dtype=jnp.float32) / np.sqrt(H)
        w_down = jax.random.normal(k4, (I, H), dtype=jnp.float32) / np.sqrt(I)
        return {'x': x, 'w_gate': w_gate, 'w_up': w_up, 'w_down': w_down}
    _L0_ffn_in = _L0_ffn_setup()
    _L0_c = _w((lambda *s: np.random.randn(*s).astype(np.float32) * 0.05)(1, 256))
    _L0_wmod = _w((lambda *s: np.random.randn(*s).astype(np.float32) * 0.05)(256, 6 * 256) * 256 ** (-0.5))

    def _L1_attn_setup():
        import jax, jax.numpy as jnp
        import numpy as np
        DIMS = 256
        HEAD_DIM = 64
        NUM_HEADS = DIMS // HEAD_DIM
        GQA_HEADS = 2
        EPS = 1e-08
        key = jax.random.key(seed)
        ks = jax.random.split(key, 6)
        b, s = (2, 256)
        kv_dims = HEAD_DIM * GQA_HEADS
        x = jax.random.normal(ks[0], (b, s, DIMS), dtype=jnp.float32)
        Wq = jax.random.normal(ks[1], (DIMS, DIMS), dtype=jnp.float32) * 0.02
        Wk = jax.random.normal(ks[2], (kv_dims, DIMS), dtype=jnp.float32) * 0.02
        Wv = jax.random.normal(ks[3], (kv_dims, DIMS), dtype=jnp.float32) * 0.02
        Wo = jax.random.normal(ks[4], (DIMS, DIMS), dtype=jnp.float32) * 0.02
        norm_scale = jnp.ones((DIMS,), dtype=jnp.float32)
        split_scale = jnp.full((DIMS,), 0.1, dtype=jnp.float32)
        return {'x': x, 'norm_scale': norm_scale, 'split_scale': split_scale, 'Wq': Wq, 'Wk': Wk, 'Wv': Wv, 'Wo': Wo}
    _L1_attn_in = _L1_attn_setup()

    def _L1_ffn_setup():
        import jax, jax.numpy as jnp
        import numpy as np
        TOP_K = 2
        CAPACITY_FACTOR = 1.0

        def _ffn(x, w1, w2):
            h = x @ w1
            x1, x2 = jnp.split(h, 2, axis=-1)
            return x1 * jax.nn.silu(x2) @ w2
        key = jax.random.key(seed)
        ks = jax.random.split(key, 6)
        B, S, D, F, E_r, E_s = (4, 256, 256, 128, 7, 1)
        sc_in = 1.0 / np.sqrt(D)
        sc_mid = 1.0 / np.sqrt(F)
        return {'x': jax.random.normal(ks[0], (B, S, D), dtype=jnp.float32), 'gate_w': jax.random.normal(ks[1], (D, E_r), dtype=jnp.float32) * sc_in, 'expert_bias': jnp.zeros((E_r,), dtype=jnp.float32), 'shared_w1': jax.random.normal(ks[2], (E_s, D, 2 * F), dtype=jnp.float32) * sc_in, 'shared_w2': jax.random.normal(ks[3], (E_s, F, D), dtype=jnp.float32) * sc_mid, 'routed_w1': jax.random.normal(ks[4], (E_r, D, 2 * F), dtype=jnp.float32) * sc_in, 'routed_w2': jax.random.normal(ks[5], (E_r, F, D), dtype=jnp.float32) * sc_mid}
    _L1_ffn_in = _L1_ffn_setup()
    _L1_c = _w((lambda *s: np.random.randn(*s).astype(np.float32) * 0.05)(1, 256))
    _L1_wmod = _w((lambda *s: np.random.randn(*s).astype(np.float32) * 0.05)(256, 6 * 256) * 256 ** (-0.5))
    _d = {'L0_attn_x': _L0_attn_in['x'], 'L0_attn_Wqkv': _L0_attn_in['Wqkv'], 'L0_attn_Wo': _L0_attn_in['Wo'], 'L0_ffn_w_gate': _L0_ffn_in['w_gate'], 'L0_ffn_w_up': _L0_ffn_in['w_up'], 'L0_ffn_w_down': _L0_ffn_in['w_down'], 'L0_c': _L0_c, 'L0_wmod': _L0_wmod, 'L1_attn_norm_scale': _L1_attn_in['norm_scale'], 'L1_attn_split_scale': _L1_attn_in['split_scale'], 'L1_attn_Wq': _L1_attn_in['Wq'], 'L1_attn_Wk': _L1_attn_in['Wk'], 'L1_attn_Wv': _L1_attn_in['Wv'], 'L1_attn_Wo': _L1_attn_in['Wo'], 'L1_ffn_gate_w': _L1_ffn_in['gate_w'], 'L1_ffn_expert_bias': _L1_ffn_in['expert_bias'], 'L1_ffn_shared_w1': _L1_ffn_in['shared_w1'], 'L1_ffn_shared_w2': _L1_ffn_in['shared_w2'], 'L1_ffn_routed_w1': _L1_ffn_in['routed_w1'], 'L1_ffn_routed_w2': _L1_ffn_in['routed_w2'], 'L1_c': _L1_c, 'L1_wmod': _L1_wmod}
    _x0 = _d['L0_attn_x']
    _d['L0_attn_x'] = jax.random.normal(jax.random.fold_in(jax.random.key(seed), 1), (1, 1024, 256), dtype=_x0.dtype)
    del _x0
    return _d

def reference(L0_attn_x, L0_attn_Wqkv, L0_attn_Wo, L0_ffn_w_gate, L0_ffn_w_up, L0_ffn_w_down, L0_c, L0_wmod, L1_attn_norm_scale, L1_attn_split_scale, L1_attn_Wq, L1_attn_Wk, L1_attn_Wv, L1_attn_Wo, L1_ffn_gate_w, L1_ffn_expert_bias, L1_ffn_shared_w1, L1_ffn_shared_w2, L1_ffn_routed_w1, L1_ffn_routed_w2, L1_c, L1_wmod):

    def _L0_attn_ref(x, Wqkv, Wo):
        import jax, jax.numpy as jnp
        import numpy as np
        H = 16
        KV = 4
        D = 128
        THETA = 10000.0
        MASK_NEG = -2.3819763e+38

        def rope(x):
            B, S, nh, Dd = x.shape
            half = Dd // 2
            freqs = 1.0 / THETA ** (jnp.arange(0, Dd, 2, dtype=jnp.float32) / Dd)
            ang = jnp.arange(S, dtype=jnp.float32)[:, None] * freqs[None, :]
            cos = jnp.cos(ang)[None, :, None, :]
            sin = jnp.sin(ang)[None, :, None, :]
            x1, x2 = (x[..., :half], x[..., half:])
            return jnp.concatenate([x1 * cos - x2 * sin, x1 * sin + x2 * cos], axis=-1).astype(x.dtype)
        B, S, dm = x.shape
        q_size, kv_size = (H * D, KV * D)
        xqkv = x @ Wqkv
        xq = xqkv[..., :q_size].reshape(B, S, H, D)
        xk = xqkv[..., q_size:q_size + kv_size].reshape(B, S, KV, D)
        xv = xqkv[..., q_size + kv_size:].reshape(B, S, KV, D)
        xq = rope(xq)
        xk = rope(xk)
        G = H // KV
        xk = jnp.repeat(xk, G, axis=2)
        xv = jnp.repeat(xv, G, axis=2)
        q = xq.transpose(0, 2, 1, 3)
        k = xk.transpose(0, 2, 1, 3)
        v = xv.transpose(0, 2, 1, 3)
        scores = jnp.einsum('bhsd,bhtd->bhst', q, k) * D ** (-0.5)
        mask = jnp.triu(jnp.full((S, S), MASK_NEG, dtype=scores.dtype), 1)
        probs = jax.nn.softmax(scores + mask[None, None], axis=-1)
        att = jnp.einsum('bhst,bhtd->bshd', probs, v).reshape(B, S, H * D)
        return att @ Wo

    def _L0_ffn_ref(x, w_gate, w_up, w_down):
        import jax, jax.numpy as jnp
        import numpy as np

        def _sparsify_2to4(h):
            B, S, I = h.shape
            g = h.reshape(B, S, I // 4, 4)
            a = jnp.abs(g)
            _, idx = jax.lax.top_k(a, 2)
            pos = jnp.arange(4)
            mask = (pos == idx[..., 0:1]) | (pos == idx[..., 1:2])
            return (g * mask.astype(g.dtype)).reshape(B, S, I)
        h = jax.nn.silu(jnp.einsum('bsh,hi->bsi', x, w_gate)) * jnp.einsum('bsh,hi->bsi', x, w_up)
        h_sparse = _sparsify_2to4(h)
        return jnp.einsum('bsi,ih->bsh', h_sparse, w_down)

    def _L1_attn_ref(x, norm_scale, split_scale, Wq, Wk, Wv, Wo):
        import jax, jax.numpy as jnp
        import numpy as np
        DIMS = 256
        HEAD_DIM = 64
        NUM_HEADS = DIMS // HEAD_DIM
        GQA_HEADS = 2
        EPS = 1e-08
        b, s, d = x.shape
        H, G, dh = (NUM_HEADS, GQA_HEADS, HEAD_DIM)
        hpg = H // G
        nrm = jnp.linalg.norm(x, axis=-1, keepdims=True) * d ** (-0.5)
        h = norm_scale * x / (nrm + EPS) * split_scale
        q = (h @ Wq.T).reshape(b, s, H, dh)
        k = (h @ Wk.T).reshape(b, s, G, dh)
        v = (h @ Wv.T).reshape(b, s, G, dh)
        q = q.transpose(0, 2, 1, 3).reshape(b, G, hpg, s, dh)
        k = k.transpose(0, 2, 1, 3)
        v = v.transpose(0, 2, 1, 3)
        scores = jnp.einsum('bghsd,bgtd->bghst', q, k) / np.float32(np.sqrt(dh))
        attn = jax.nn.softmax(scores, axis=-1)
        out = jnp.einsum('bghst,bgtd->bghsd', attn, v)
        out = out.reshape(b, H, s, dh).transpose(0, 2, 1, 3).reshape(b, s, H * dh)
        return x + out @ Wo.T

    def _L1_ffn_ref(x, gate_w, expert_bias, shared_w1, shared_w2, routed_w1, routed_w2):
        import jax, jax.numpy as jnp
        import numpy as np
        TOP_K = 2
        CAPACITY_FACTOR = 1.0

        def _ffn(x, w1, w2):
            h = x @ w1
            x1, x2 = jnp.split(h, 2, axis=-1)
            return x1 * jax.nn.silu(x2) @ w2
        B, S, D = x.shape
        E_r = gate_w.shape[1]
        T = B * S
        capacity = max(1, int(CAPACITY_FACTOR * T / E_r))
        flat_x = x.reshape(T, D)
        shared_sum = jax.vmap(_ffn, in_axes=(None, 0, 0))(flat_x, shared_w1, shared_w2).sum(0)
        gate_logits = flat_x @ gate_w + expert_bias
        aff = jax.nn.sigmoid(gate_logits)
        _, topk_idx = jax.lax.top_k(aff, TOP_K)
        mask = (topk_idx[:, :, None] == jnp.arange(E_r)[None, None, :]).any(axis=1)
        score = jnp.where(mask, aff, -1.0).T
        _, sel_idx = jax.lax.top_k(score, capacity)
        kept = jnp.take_along_axis(mask.T, sel_idx, axis=1)
        w = jnp.where(kept, jnp.take_along_axis(aff.T, sel_idx, axis=1), 0.0)
        inp = flat_x[sel_idx]
        out = jax.vmap(_ffn)(inp, routed_w1, routed_w2)
        routed_sum = jnp.zeros_like(flat_x).at[sel_idx].add(out * w[:, :, None])
        return (shared_sum + routed_sum).reshape(B, S, D)
    x = L0_attn_x
    mod = (_silu(L0_c) @ L0_wmod).reshape(L0_c.shape[0], 6, 1, -1)
    sa, ca, ga, sb, cb, gb = (mod[:, 0], mod[:, 1], mod[:, 2], mod[:, 3], mod[:, 4], mod[:, 5])
    ga = (2 * (ga >= 0) - 1) * jnp.maximum(jnp.abs(ga), 0.25)
    gb = (2 * (gb >= 0) - 1) * jnp.maximum(jnp.abs(gb), 0.25)
    h = _layernorm(x, axis=-1) * (1 + ca) + sa
    x = x + ga * _L0_attn_ref(h, L0_attn_Wqkv, L0_attn_Wo)
    h = _layernorm(x, axis=-1) * (1 + cb) + sb
    x = x + gb * _L0_ffn_ref(h, L0_ffn_w_gate, L0_ffn_w_up, L0_ffn_w_down)
    mod = (_silu(L1_c) @ L1_wmod).reshape(L1_c.shape[0], 6, 1, -1)
    sa, ca, ga, sb, cb, gb = (mod[:, 0], mod[:, 1], mod[:, 2], mod[:, 3], mod[:, 4], mod[:, 5])
    ga = (2 * (ga >= 0) - 1) * jnp.maximum(jnp.abs(ga), 0.25)
    gb = (2 * (gb >= 0) - 1) * jnp.maximum(jnp.abs(gb), 0.25)
    h = _layernorm(x, axis=-1) * (1 + ca) + sa
    x = x + ga * _L1_attn_ref(h, L1_attn_norm_scale, L1_attn_split_scale, L1_attn_Wq, L1_attn_Wk, L1_attn_Wv, L1_attn_Wo)
    h = _layernorm(x, axis=-1) * (1 + cb) + sb
    x = x + gb * _L1_ffn_ref(h, L1_ffn_gate_w, L1_ffn_expert_bias, L1_ffn_shared_w1, L1_ffn_shared_w2, L1_ffn_routed_w1, L1_ffn_routed_w2)
    return x

_drawn_inputs = setup_inputs


def setup_inputs(seed=0):
    import zlib

    import numpy as np

    out = dict(_drawn_inputs(seed))
    spreads = {'L1_attn_norm_scale': (1.0, 0.6),
     'L1_attn_split_scale': (0.10000000149011612, 0.6),
     'L1_ffn_expert_bias': (0.0, 1.259)}
    factors = {'L0_attn_Wqkv': 5.244,
     'L0_attn_Wo': 4.979,
     'L1_attn_Wq': 36.932,
     'L1_attn_Wk': 38.708,
     'L1_attn_Wv': 28.578,
     'L1_attn_Wo': 30.126}
    for name, (base, spread) in spreads.items():
        noise = np.random.default_rng([zlib.crc32(name.encode()), seed]).standard_normal(out[name].shape)
        drawn = base * np.exp(spread * noise) if base else spread * noise
        out[name] = jnp.asarray(drawn.astype(out[name].dtype))
    for name, factor in factors.items():
        out[name] = (out[name] * factor).astype(out[name].dtype)
    return out
```

```python
from contextlib import ExitStack

import numpy as np

import concourse.bass as bass
from concourse import mybir

P = 128
S = 1024
DM = 256
NT = S // P
KD = DM // P
BANK = 512
EPS = 1e-5

H0, KV0, D0 = 16, 4, 128
PER_KV = H0 // KV0
I0 = 1024
H1, G1, D1 = 4, 2, 64
RMS_EPS = 1e-8
NE, FE, TOPK = 7, 128, 2
CAPACITY = S // NE
MASK_NEG = -2.3819763e+38

F32 = mybir.dt.float32
F32R = mybir.dt.float32r
BF16 = mybir.dt.bfloat16
ALU = mybir.AluOpType
ACT = mybir.ActivationFunctionType
AX = mybir.AxisListType


class Split:

    def __init__(self, hi, lo):
        self.hi, self.lo = hi, lo

    def __getitem__(self, index):
        return Split(self.hi[index], self.lo[index])

    def __call__(self, pattern, **sizes):
        return Split(self.hi.rearrange(pattern, **sizes), self.lo.rearrange(pattern, **sizes))


def product(pe, out, left, right, start, stop):
    pe.matmul(out, left.hi, right.hi, start=start, stop=False)
    pe.matmul(out, left.hi, right.lo, start=False, stop=False)
    return pe.matmul(out, left.lo, right.hi, start=False, stop=stop)


def as_f32(ap):
    return ap.bitcast(F32)


class Chain:

    def __init__(self, engine, sem, value=0):
        self.engine, self.sem, self.value = engine, sem, value

    def step(self, ins):
        ins.then_inc(self.sem, 1)
        self.value += 1
        return ins

    def settle(self):
        self.engine.wait_ge(self.sem, self.value)

    def run(self, ins):
        self.step(ins)
        self.settle()
        return ins


def build(nc, a):
    top = ExitStack()
    with top:
        def sb(name, shape, dt=F32, ctx=top):
            return ctx.enter_context(nc.sbuf_tensor(name, shape, dt))

        def split(name, shape, ctx=top):
            return Split(sb(name + "_hi", shape, F32R, ctx)[:], sb(name + "_lo", shape, F32R, ctx)[:])

        x = sb("x", [P, NT, DM])
        ident = sb("ident_sb", [P, P])
        identb = sb("identb_sb", [P, P], BF16)
        maskb = sb("maskb_sb", [P, P], BF16)
        ones = sb("ones", [P, P])
        modcol = sb("modcol", [P, 2, 12])
        gate = sb("gate", [P, 2, 2, DM])
        stats = sb("stats", [P, NT, 6])
        meanvar = sb("meanvar", [P, NT, 2])
        vareps = sb("vareps", [P, NT])
        rstd = sb("rstd", [P, NT])
        tiny = sb("tiny", [P, 2, NT])
        hT = split("hT", [P, KD, S])
        sems = Sems(nc, top)
        staging, staging1 = sb("staging", [P, 6144]), sb("staging1", [P, 2048])
        staged, staged1 = sems("staged"), sems("staged1")
        m = Shared(x, ident, identb, maskb, ones, modcol, gate, stats, meanvar, vareps, rstd, tiny, hT,
                   staging, staging1, staged, staged1)
        modulation(nc, a, m, sems, sb, split)
        attention0(nc, a, m, sems, sb, split)
        ffn0(nc, a, m, sems, sb, split)
        attention1(nc, a, m, sems, sb, split)
        ffn1(nc, a, m, sems, sb, split)


class Shared:
    def __init__(self, x, ident, identb, maskb, ones, modcol, gate, stats, meanvar, vareps, rstd, tiny, hT,
                 staging, staging1, staged, staged1):
        self.x, self.ident, self.identb, self.maskb, self.ones = x, ident, identb, maskb, ones
        self.modcol, self.gate, self.stats, self.meanvar = modcol, gate, stats, meanvar
        self.vareps, self.rstd, self.tiny, self.hT = vareps, rstd, tiny, hT
        self.staging, self.staging1, self.staged, self.staged1 = staging, staging1, staged, staged1


class Sems:

    def __init__(self, nc, ctx):
        self.nc, self.ctx = nc, ctx

    def __call__(self, name):
        return self.ctx.enter_context(self.nc.semaphore(name))


def row_stats(dve, m, chain, sqrt_in, sqrt_out):
    for n in range(NT):
        chain.step(dve.bn_stats(m.stats[:, n, :], m.x[:, n, :]))
    chain.settle()
    for n in range(NT):
        chain.step(dve.bn_aggr(m.meanvar[:, n, :], m.stats[:, n, :]))
    chain.settle()
    dve.tensor_scalar(m.vareps[:, :], m.meanvar[:, :, 1], EPS, None, ALU.add).then_inc(sqrt_in, 1)
    dve.wait_ge(sqrt_out, 1)
    chain.run(dve.reciprocal(m.rstd[:, :], m.tiny[:, 0, :]))
    chain.run(dve.tensor_tensor(m.tiny[:, 1, :], m.rstd[:, :], m.rstd[:, :], ALU.mult))
    chain.run(dve.tensor_tensor(m.tiny[:, 1, :], m.tiny[:, 1, :], m.vareps[:, :], ALU.mult))
    chain.run(dve.tensor_scalar(m.tiny[:, 1, :], m.tiny[:, 1, :], -0.5, 1.5, ALU.mult, ALU.add))
    chain.run(dve.tensor_tensor(m.rstd[:, :], m.rstd[:, :], m.tiny[:, 1, :], ALU.mult))


def row_stats_sqrt(act, m, sqrt_in, sqrt_out):
    act.wait_ge(sqrt_in, 1)
    act.activation(m.tiny[:, 0, :], m.vareps[:, :], ACT.Sqrt).then_inc(sqrt_out, 1)


def modulation(nc, a, m, sems, sb, split):
    with ExitStack() as ctx:
        wmod = sb("wmod", [P, 2, KD, 6 * DM], F32, ctx)
        craw = sb("craw", [P, 2, KD], F32, ctx)
        csil = sb("csil", [P, 2, KD], F32, ctx)
        cwide = sb("cwide", [P, 2, KD, P], F32, ctx)
        mask32 = sb("mask32", [P, P], F32, ctx)
        sgn = sb("sgn", [P, 2, 2, DM], F32, ctx)
        p_col = ctx.enter_context(nc.psum_tensor("p_col", [P, 2, 12], F32))
        p_gate = [ctx.enter_context(nc.psum_tensor(f"p_gate{n}", [P, 2, DM], F32)) for n in range(2)]
        c_in, const_in = sems("c_in"), sems("const_in")
        w_in = [sems(f"wmod_in{n}") for n in range(2)]
        c_silu, c_wide, mod_done, mod_read = sems("c_silu"), sems("c_wide"), sems("mod_done"), sems("mod_read")
        chain_sem = sems("mod_chain")
        with nc.Block() as block:
            @block.sync
            def _(sp):
                for n in range(2):
                    sp.dma_start(craw[:, n, :], a[f"L{n}_c"]).then_inc(c_in, 16)
                sp.dma_start(wmod[:, 0, :, :], a["L0_wmod"].rearrange("(k p) n -> p k n", p=P)).then_inc(w_in[0], 16)
                sp.dma_start(wmod[:, 1, :, :], a["L1_wmod"].rearrange("(k p) n -> p k n", p=P)).then_inc(w_in[1], 16)

            @block.scalar
            def _(act):
                act.dma_start(m.x[:, :, :], a["L0_attn_x"].rearrange("o (n p) d -> p (o n) d", p=P)).then_inc(const_in, 16)
                act.dma_start(m.ident[:, :], a["ident"]).then_inc(const_in, 16)
                act.dma_start(mask32[:, :], a["mask"]).then_inc(const_in, 16)
                act.wait_ge(c_in, 32)
                act.activation(csil[:, :, :], craw[:, :, :], ACT.Silu).then_inc(c_silu, 1)

            @block.tensor
            def _(pe):
                pe.wait_ge(c_wide, 1)
                for n in range(2):
                    pe.wait_ge(w_in[n], 16)
                    for j in range(12):
                        for k in range(KD):
                            pe.matmul(p_col[:, n, j:j + 1], wmod[:, n, k, j * P:(j + 1) * P], csil[:, n, k:k + 1],
                                      start=(k == 0), stop=(k == KD - 1))
                    for g, part in enumerate((2, 5)):
                        for k in range(KD):
                            mm = pe.matmul(p_gate[n][:, g, :], cwide[:, n, k, :],
                                           wmod[:, n, k, part * DM:(part + 1) * DM],
                                           start=(k == 0), stop=(k == KD - 1))
                mm.then_inc(mod_done, 1)

            @block.vector
            def _(dve):
                chain = Chain(dve, chain_sem)
                chain.run(dve.memset(m.ones[:, :], 1.0))
                dve.wait_ge(c_silu, 1)
                for n in range(2):
                    for k in range(KD):
                        w = dve.tensor_scalar(cwide[:, n, k, :], m.ones[:, :], csil[:, n, k:k + 1], None, ALU.mult)
                        if n == 1 and k == KD - 1:
                            w.then_inc(c_wide, 1)
                dve.wait_ge(const_in, 48)
                chain.run(dve.tensor_copy(m.identb[:, :], m.ident[:, :]))
                chain.run(dve.tensor_copy(m.maskb[:, :], mask32[:, :]))
                dve.wait_ge(mod_done, 1)
                chain.run(dve.tensor_copy(m.modcol[:, :, :], p_col[:, :, :]))
                for j in (2, 8):
                    chain.run(dve.tensor_scalar(m.modcol[:, :, j:j + 2], m.modcol[:, :, j:j + 2], 1.0, None, ALU.add))
                for n in range(2):
                    g, out = p_gate[n][:, :, :], m.gate[:, n, :, :]
                    chain.run(dve.tensor_scalar(sgn[:, n, :, :], g, 0.0, 2.0, ALU.is_ge, ALU.mult))
                    chain.run(dve.tensor_scalar(sgn[:, n, :, :], sgn[:, n, :, :], -1.0, None, ALU.add))
                    chain.run(dve.tensor_tensor(out, g, sgn[:, n, :, :], ALU.mult))
                    chain.run(dve.tensor_scalar(out, out, 0.25, None, ALU.max))
                    chain.run(dve.tensor_tensor(out, out, sgn[:, n, :, :], ALU.mult))


def transposed_rows(nc, m, sems, sb, layer, part, name, keep=None, more=None):
    with ExitStack() as ctx:
        xn = sb(name + "_xn", [P, NT, DM], F32, ctx)
        h32 = sb(name + "_h32", [P, KD, S], F32, ctx) if keep is None else keep
        banks = [ctx.enter_context(nc.psum_tensor(f"{name}_bank{n}", [P, BANK], F32)) for n in range(4)]
        sqrt_in, sqrt_out = sems(name + "_sqrt_in"), sems(name + "_sqrt_out")
        normed, turned, scaled, chain_sem = (sems(f"{name}_{s}") for s in ("normed", "turned", "scaled", "chain"))
        with nc.Block() as block:
            @block.vector
            def _(dve):
                chain = Chain(dve, chain_sem)
                row_stats(dve, m, chain, sqrt_in, sqrt_out)
                for n in range(NT):
                    dve.tensor_scalar(xn[:, n, :], m.x[:, n, :], m.meanvar[:, n, 0:1], m.rstd[:, n:n + 1],
                                      ALU.subtract, ALU.mult).then_inc(normed, 1)
                for q in range(4 if keep is None else 0):
                    k, cols = q % KD, slice(q // KD * BANK, (q // KD + 1) * BANK)
                    dve.wait_ge(scaled, q + 1)
                    chain.run(dve.tensor_copy(m.hT.hi[:, k, cols], h32[:, k, cols]))
                    chain.run(dve.tensor_tensor(m.hT.lo[:, k, cols], h32[:, k, cols], as_f32(m.hT.hi[:, k, cols]),
                                                ALU.subtract))

            @block.scalar
            def _(act):
                row_stats_sqrt(act, m, sqrt_in, sqrt_out)
                for q in range(4):
                    k, cols = q % KD, slice(q // KD * BANK, (q // KD + 1) * BANK)
                    act.wait_ge(turned, q + 1)
                    act.activation(h32[:, k, cols], banks[q][:, :], ACT.Identity,
                                   scale=m.modcol[:, layer, part + 2 + k:part + 3 + k],
                                   bias=m.modcol[:, layer, part + k:part + k + 1]).then_inc(scaled, 1)

            @block.tensor
            def _(pe):
                for q in range(4):
                    k, half = q % KD, q // KD
                    pe.wait_ge(normed, 4 * (half + 1))
                    for n in range(4):
                        mm = pe.transpose(banks[q][:, n * P:(n + 1) * P], xn[:, 4 * half + n, k * P:(k + 1) * P],
                                          m.ident[:, :])
                    mm.then_inc(turned, 1)


def attention0(nc, a, m, sems, sb, split):
    transposed_rows(nc, m, sems, sb, 0, 0, "ln0")
    UNITS = PER_KV * NT
    TGROUPS = 12
    CH = 2
    with ExitStack() as ctx:
        def buf(name, shape, dt=F32):
            return sb("at0_" + name, shape, dt, ctx)

        def pair(name, shape):
            return split("at0_" + name, shape, ctx)

        cos, sin = buf("cos", [P, S]), buf("sin", [P, S])
        wq_in, wkv_in, wo_in = buf("wq_in", [P, KD, P]), buf("wkv_in", [P, KD, 2, P]), buf("wo_in", [P, 2, DM])
        wq, wkv, wo = pair("wq", [P, KD, P]), pair("wkv", [P, KD, 2, P]), pair("wo", [P, 2, DM])
        kT, v = pair("kT", [P, S]), pair("v", [P, NT, D0])
        k_next = buf("k_next", [P, S])
        q = [pair(f"q{n}", [P, S]) for n in range(2)]
        swapped, turned = buf("swapped", [P, BANK]), buf("turned", [P, BANK])
        probs = buf("probs", [P, 4, S])
        negmax, rowsum, rinv = buf("negmax", [P, 4]), buf("rowsum", [P, 4]), buf("rinv", [P, 4])
        pT = [pair("pT0", [P, 4, BANK]), pair("pT1", [P, 8, BANK])]
        att = pair("att", [P, 2, S])
        p_scores = [ctx.enter_context(nc.psum_tensor(f"at0_scores{n}", [P, S], F32)) for n in range(2)]
        p_turn = [ctx.enter_context(nc.psum_tensor(f"at0_turn{n}", [P, 4, P], F32)) for n in range(2)]
        p_att = ctx.enter_context(nc.psum_tensor("at0_att", [P, BANK], F32))
        p_proj = ctx.enter_context(nc.psum_tensor("at0_proj", [P, BANK], F32))

        def sem(name):
            return sems("at0_" + name)

        tables_in, wq_loaded, wkv_loaded, wo_loaded = (sem(n) for n in ("tables_in", "wq_loaded", "wkv_loaded", "wo_loaded"))
        wq_ready, wkv_ready, wo_ready = sem("wq_ready"), sem("wkv_ready"), sem("wo_ready")
        rope_mm = sem("rope_mm")
        rope_swapped = sem("rope_swapped")
        rope_done = sem("rope_done")
        keys_ready = sem("keys_ready")
        v_mm, v_hi = sem("v_mm"), sem("v_hi")
        proj_free = sem("proj_free")
        scores_mm, max_done, exp_done, rinv_done, normed = (sem(n) for n in ("scores_mm", "max_done", "exp_done", "rinv_done", "normed"))
        turn_mm, turn_hi, turn_lo = sem("turn_mm"), sem("turn_hi"), sem("turn_lo")
        att_mm, att_hi, att_lo = sem("att_mm"), sem("att_hi"), sem("att_lo")
        out_mm, out_added = sem("out_mm"), sem("out_added")
        key_hi, w_hi, wo_gated, rope_sin, rope_sum, query_hi = (sem(n) for n in ("key_hi", "w_hi", "wo_gated", "rope_sin", "rope_sum", "query_hi"))

        JOBS, ROPES = 20, 10

        def tgroups_before(unit):
            h, i = divmod(unit, NT)
            return TGROUPS * h + (i if i < 4 else 4 + 2 * (i - 4))

        def blocks(i):
            return [(0, min(i + 1, 4))] + ([(4, i + 1)] if i >= 4 else [])

        def job_base(g, k):
            if isinstance(g, int) and g == 0:
                return 4 + k if k < 4 else k
            return JOBS * g + k

        def body(g, first, last, slot):
            for s in range(UNITS):
                slot(g, s, first, last)

        def groups(engine, slot):
            body(0, True, False, slot)
            with engine.Fori(1, KV0 - 1) as g:
                body(g, False, False, slot)
            body(KV0 - 1, False, True, slot)

        wqkv = a["L0_attn_Wqkv"].rearrange("(k p) n -> p k n", p=P)
        wo_rows = a["L0_attn_Wo"].rearrange("(h p) n -> p h n", p=P)
        with nc.Block() as block:
            @block.sync
            def _(sp):
                def load_q(head, n):
                    if not (isinstance(n, int) and n == 0):
                        sp.wait_ge(wq_ready, n)
                    sp.dma_start(wq_in[:, :, :], wqkv[:, :, bass.ds(head * P, P)]).then_inc(wq_loaded, 16)

                def load_kv(g):
                    if not (isinstance(g, int) and g == 0):
                        sp.wait_ge(wkv_ready, g)
                    for j in range(2):
                        sp.dma_start(wkv_in[:, :, j, :], wqkv[:, :, bass.ds(g * P + (H0 + j * KV0) * P, P)])\
                          .then_inc(wkv_loaded, 16)

                def load_o(n):
                    if not (isinstance(n, int) and n == 0):
                        sp.wait_ge(wo_ready, n)
                    sp.dma_start(wo_in[:, :, :], wo_rows[:, bass.ds(n * 2, 2), :]).then_inc(wo_loaded, 16)

                load_kv(0)
                load_q(0, 0)
                sp.dma_start(cos[:, :], a["cos"]).then_inc(tables_in, 16)
                sp.dma_start(sin[:, :], a["sin"]).then_inc(tables_in, 16)
                load_q(1, 1)
                for n, name in enumerate(("L0_ffn_w_gate", "L0_ffn_w_up")):
                    sp.dma_start(m.staging[:, n * 2048:(n + 1) * 2048].rearrange("p (k n) -> p k n", k=KD),
                                 a[name].rearrange("(k p) n -> p k n", p=P)).then_inc(m.staged, 16)
                sp.dma_start(m.staging[:, 4096:6144].rearrange("p (c d) -> p c d", d=DM),
                             a["L0_ffn_w_down"].rearrange("(c p) d -> p c d", p=P)).then_inc(m.staged, 16)

                at = 0
                for name in ("L1_attn_Wq", "L1_attn_Wk", "L1_attn_Wv"):
                    w = a[name]
                    n = KD * w.shape[1]
                    sp.dma_start(m.staging1[:, at:at + n].rearrange("p (k n) -> p k n", k=KD), w.rearrange("(k p) n -> p k n", p=P))\
                      .then_inc(m.staged1, 16)
                    at += n
                for half in range(2):
                    sp.dma_start(m.staging1[half * D1:(half + 1) * D1, at:].rearrange("p (h n) -> p h n", h=H1),
                                 a["L1_attn_Wo"].rearrange("(h p) n -> p h n", p=D1)).then_inc(m.staged1, 16)

                def group(g, last):
                    if not last:
                        load_kv(g + 1)
                    load_q(g * PER_KV + 2, g * PER_KV + 2)
                    load_o(g * 2)
                    load_q(g * PER_KV + 3, g * PER_KV + 3)
                    if not last:
                        load_q(g * PER_KV + 4, g * PER_KV + 4)
                    load_o(g * 2 + 1)
                    if not last:
                        load_q(g * PER_KV + 5, g * PER_KV + 5)

                group(0, False)
                with sp.Fori(1, KV0 - 1) as g:
                    group(g, False)
                group(KV0 - 1, True)

            @block.tensor
            def _(pe):
                def proj_bank(job):
                    if not (isinstance(job, int) and job == 0):
                        pe.wait_ge(proj_free, job)

                def rope_job(job, w, c):
                    proj_bank(job)
                    for k in range(KD):
                        mm = product(pe, p_proj[:, :], w[:, k, :], m.hT[:, k, c * BANK:(c + 1) * BANK], k == 0, k == KD - 1)
                    mm.then_inc(rope_mm, 1)

                def key_job(job, g, c):
                    pe.wait_ge(wkv_ready, g + 1)
                    rope_job(job, wkv[:, :, 0, :], c)

                def query_job(job, head, c):
                    pe.wait_ge(wq_ready, head + 1)
                    rope_job(job, wq, c)

                def value_job(job, g, c):
                    proj_bank(job)
                    for n in range(4):
                        rows = slice((4 * c + n) * P, (4 * c + n + 1) * P)
                        for k in range(KD):
                            mm = product(pe, p_proj[:, n * P:(n + 1) * P], m.hT[:, k, rows], wkv[:, k, 1, :], k == 0, k == KD - 1)
                    mm.then_inc(v_mm, 1)

                def out_job(job, pair_index, j):
                    proj_bank(job)
                    if j == 0:
                        pe.wait_ge(wo_ready, pair_index + 1)
                        pe.wait_ge(att_lo, pair_index * 4 + 4)
                    for n in range(2):
                        rows = slice((2 * j + n) * P, (2 * j + n + 1) * P)
                        for hh in range(2):
                            mm = product(pe, p_proj[:, n * DM:(n + 1) * DM], att[:, hh, rows], wo[:, hh, :], hh == 0, hh == 1)
                    mm.then_inc(out_mm, 1)

                def scores(g, s, first):
                    h, i = divmod(s, NT)
                    out, rows, width = p_scores[s % 2], slice(i * P, (i + 1) * P), (i + 1) * P
                    if i == 0:
                        if h == 0:
                            pe.wait_ge(keys_ready, g + 1)
                            pe.wait_ge(rope_done, g * ROPES + 4)
                        else:
                            pe.wait_ge(rope_done, g * ROPES + 4 + 2 * h)
                    if not (first and s < 2):
                        pe.wait_ge(exp_done, g * UNITS + s - 1)
                    for c0 in range(0, width, BANK):
                        c1 = min(c0 + BANK, width)
                        qs, ks = q[h % 2][:, rows], kT[:, c0:c1]
                        pe.matmul(out[:, c0:c1], qs.hi, ks.hi, start=True, stop=False)
                        if c1 == width:
                            pe.matmul(out[:, width - P:width], m.identb[:, :], m.maskb[:, :], start=False, stop=False)
                        pe.matmul(out[:, c0:c1], qs.hi, ks.lo, start=False, stop=False)
                        mm = pe.matmul(out[:, c0:c1], qs.lo, ks.hi, start=False, stop=True)
                    mm.then_inc(scores_mm, 1)

                def turn(g, s):
                    h, i = divmod(s, NT)
                    pe.wait_ge(normed, g * UNITS + s + 1)
                    for n, (b0, b1) in enumerate(blocks(i)):
                        t = tgroups_before(s) + n
                        if not (isinstance(g, int) and g == 0 and t < 2):
                            pe.wait_ge(turn_lo, g * PER_KV * TGROUPS + t - 1)
                        for b in range(b0, b1):
                            mm = pe.transpose(p_turn[t % 2][:, b - b0, :], probs[:, s % 4, b * P:(b + 1) * P], m.ident[:, :])
                        mm.then_inc(turn_mm, 1)

                def attend(g, h, c, t0, t1):
                    last_tile = 4 * c + 3
                    if t0 == 0:
                        pe.wait_ge(turn_lo, g * PER_KV * TGROUPS + h * TGROUPS + (4 if c == 0 else TGROUPS))
                        pe.wait_ge(proj_free, job_base(g, 2 + c) + 1)
                        if not (isinstance(g, int) and g == 0 and h == 0 and c == 0):
                            pe.wait_ge(att_lo, (g * PER_KV + h) * 2 + c)
                    for t in range(t0, t1):
                        c0 = max(0, t - 4 * c) * P
                        mm = product(pe, p_att[:, c0:BANK], v[:, t, :], pT[c][:, t, c0:BANK], t == 0, t == last_tile)
                    if t1 == last_tile + 1:
                        mm.then_inc(att_mm, 1)

                def slot(g, s, first, last):
                    h, i = divmod(s, NT)
                    scores(g, s, first)
                    if s >= 2:
                        turn(g, s - 2)
                    elif not first:
                        turn(g - 1, UNITS + s - 2)
                    prev = (g, h - 1) if h else (g - 1, PER_KV - 1)
                    if i in (2, 3) and not (first and h == 0):
                        attend(*prev, 1, 4 * (i - 2), 4 * (i - 1))
                    if i == 6:
                        attend(g, h, 0, 0, 4)
                    if h < PER_KV - 1 and i < 2:
                        query_job(job_base(g, (0, 8, 10)[h] + i), g * 4 + h + 1, i)
                    if h == PER_KV - 1 and i < 2 and not last:
                        query_job(job_base(g, 16 + i), g * 4 + 4, i)
                    if h == PER_KV - 1 and i in (4, 5) and not last:
                        key_job(job_base(g, 14 + i), g + 1, i - 4)
                    if h == 0 and i in (3, 4):
                        value_job(job_base(g, i - 1), g, i - 3)
                    if i >= 4 and h == 0 and not first:
                        out_job(job_base(g, i), g * 2 - 1, i - 4)
                    if i >= 4 and h == 2:
                        out_job(job_base(g, 8 + i), g * 2, i - 4)

                for c in range(CH):
                    key_job(c, 0, c)
                for c in range(CH):
                    query_job(2 + c, 0, c)
                groups(pe, slot)
                g = KV0 - 1
                turn(g, UNITS - 2)
                turn(g, UNITS - 1)
                attend(g, PER_KV - 1, 1, 0, 8)
                for j in range(4):
                    out_job(JOBS * KV0 - 4 + j, 2 * KV0 - 1, j)

            @block.scalar
            def _(act):
                def swap(r):
                    act.wait_ge(rope_mm, r + 1)
                    if not (isinstance(r, int) and r == 0):
                        act.wait_ge(rope_done, r)
                    half = P // 2
                    act.activation(swapped[0:half, :], p_proj[half:P, :], ACT.Copy)
                    act.activation(swapped[half:P, :], p_proj[0:half, :], ACT.Copy).then_inc(rope_swapped, 1)

                def value_hi(g, c):
                    act.wait_ge(v_mm, g * 2 + c + 1)
                    if not (isinstance(g, int) and g == 0):
                        act.wait_ge(att_mm, g * 2 * PER_KV)
                    act.activation(v.hi[:, 4 * c:4 * c + 4, :], p_proj[:, :].rearrange("p (n d) -> p n d", n=4), ACT.Copy)\
                       .then_inc(v_hi, 1)

                def probs_hi(g, s):
                    h, i = divmod(s, NT)
                    c = i // 4
                    if i % 4 == 0 and not (isinstance(g, int) and g == 0 and h == 0):
                        act.wait_ge(att_mm, (g * PER_KV + h) * 2 - 1 + c)
                    for n, (b0, b1) in enumerate(blocks(i)):
                        t = tgroups_before(s) + n
                        act.wait_ge(turn_mm, g * PER_KV * TGROUPS + t + 1)
                        act.activation(pT[c].hi[:, b0:b1, (i % 4) * P:(i % 4 + 1) * P], p_turn[t % 2][:, 0:b1 - b0, :], ACT.Copy)\
                           .then_inc(turn_hi, 1)

                def exp(g, s, first):
                    i = s % NT
                    width = (i + 1) * P
                    act.wait_ge(max_done, g * UNITS + s + 1)
                    if not (first and s < 4):
                        before = tgroups_before(s - 3) if s >= 3 else tgroups_before(UNITS + s - 3) - PER_KV * TGROUPS
                        act.wait_ge(turn_mm, g * PER_KV * TGROUPS + before)
                    act.activation(probs[:, s % 4, 0:width], p_scores[s % 2][:, 0:width], ACT.Exp,
                                   bias=negmax[:, s % 4:s % 4 + 1], accum_out=rowsum[:, s % 4:s % 4 + 1])\
                       .then_inc(exp_done, 1)

                def attended_hi(g, h, c):
                    n = (g * PER_KV + h) * 2 + c
                    act.wait_ge(att_mm, n + 1)
                    if h % 2 == 0 and c == 0 and not (isinstance(g, int) and g == 0 and h == 0):
                        act.wait_ge(out_mm, (g * 2 + h // 2) * 4)
                    act.activation(att.hi[:, h % 2, c * BANK:(c + 1) * BANK], p_att[:, :], ACT.Copy).then_inc(att_hi, 1)

                def slot(g, s, first, last):
                    h, i = divmod(s, NT)
                    if s >= 2:
                        probs_hi(g, s - 2)
                    elif not first:
                        probs_hi(g - 1, UNITS + s - 2)
                    exp(g, s, first)
                    if i == 3 and not (first and h == 0):
                        attended_hi(*((g, h - 1) if h else (g - 1, PER_KV - 1)), 1)
                    if i == 7:
                        attended_hi(g, h, 0)
                    if i < 2 and not (last and h == PER_KV - 1):
                        swap(g * ROPES + 4 + 2 * h + i)
                    if h == PER_KV - 1 and i in (4, 5) and not last:
                        swap(g * ROPES + 8 + i)
                    if h == 0 and i in (3, 4):
                        value_hi(g, i - 3)

                for r in range(4):
                    swap(r)
                groups(act, slot)
                g = KV0 - 1
                probs_hi(g, UNITS - 2)
                probs_hi(g, UNITS - 1)
                attended_hi(g, PER_KV - 1, 1)

            @block.vector
            def _(dve):
                def times_cos(r, c):
                    if not (isinstance(r, int) and r == 0):
                        dve.wait_ge(rope_done, r)
                    dve.wait_ge(rope_swapped, r + 1)
                    dve.tensor_tensor(turned[:, :], p_proj[:, :], cos[:, c * BANK:(c + 1) * BANK], ALU.mult)\
                       .then_inc(proj_free, 1)

                def split_keys(g, first):
                    dve.wait_ge(rope_done, g * ROPES + (2 if first else 4))
                    if not first:
                        dve.wait_ge(scores_mm, g * UNITS)
                    dve.tensor_copy(kT.hi[:, :], k_next[:, :]).then_inc(key_hi, 1)
                    dve.wait_ge(key_hi, g + 1)
                    dve.tensor_tensor(kT.lo[:, :], k_next[:, :], as_f32(kT.hi[:, :]), ALU.subtract).then_inc(keys_ready, 1)

                def value_lo(g, c):
                    dve.wait_ge(v_hi, g * 2 + c + 1)
                    out = v[:, 4 * c:4 * c + 4, :]
                    dve.tensor_tensor(out.lo, p_proj[:, :].rearrange("p (n d) -> p n d", n=4), as_f32(out.hi), ALU.subtract)\
                       .then_inc(proj_free, 1)

                def maximum(g, s):
                    i = s % NT
                    dve.wait_ge(scores_mm, g * UNITS + s + 1)
                    dve.tensor_reduce(negmax[:, s % 4:s % 4 + 1], p_scores[s % 2][:, 0:(i + 1) * P], AX.X, ALU.max, negate=True)\
                       .then_inc(max_done, 1)

                def inverse_sum(g, s):
                    dve.wait_ge(exp_done, g * UNITS + s + 1)
                    dve.reciprocal(rinv[:, s % 4:s % 4 + 1], rowsum[:, s % 4:s % 4 + 1]).then_inc(rinv_done, 1)

                def probs_lo(g, s):
                    h, i = divmod(s, NT)
                    for n, (b0, b1) in enumerate(blocks(i)):
                        t = tgroups_before(s) + n
                        out = pT[i // 4][:, b0:b1, (i % 4) * P:(i % 4 + 1) * P]
                        dve.wait_ge(turn_hi, g * PER_KV * TGROUPS + t + 1)
                        dve.tensor_tensor(out.lo, p_turn[t % 2][:, 0:b1 - b0, :], as_f32(out.hi), ALU.subtract).then_inc(turn_lo, 1)

                def attended_lo(g, h, c):
                    out = att[:, h % 2, c * BANK:(c + 1) * BANK]
                    dve.wait_ge(att_hi, (g * PER_KV + h) * 2 + c + 1)
                    dve.tensor_tensor(out.lo, p_att[:, :], as_f32(out.hi), ALU.subtract).then_inc(att_lo, 1)

                def add_out(pair_index, j):
                    dve.wait_ge(out_mm, pair_index * 4 + j + 1)
                    rows = m.x[:, 2 * j:2 * j + 2, :]
                    dve.tensor_tensor(rows, p_proj[:, :].rearrange("p (n d) -> p n d", n=2), rows, ALU.add)\
                       .then_inc(proj_free, 1)

                def slot(g, s, first, last):
                    h, i = divmod(s, NT)
                    if s == 0:
                        split_keys(g, first)
                    maximum(g, s)
                    if s:
                        inverse_sum(g, s - 1)
                    elif not first:
                        inverse_sum(g - 1, UNITS - 1)
                    if s >= 2:
                        probs_lo(g, s - 2)
                    elif not first:
                        probs_lo(g - 1, UNITS + s - 2)
                    if i == 3 and not (first and h == 0):
                        attended_lo(*((g, h - 1) if h else (g - 1, PER_KV - 1)), 1)
                    if i < 2 and not (last and h == PER_KV - 1):
                        times_cos(g * ROPES + 4 + 2 * h + i, i)
                    if h == PER_KV - 1 and i in (4, 5) and not last:
                        times_cos(g * ROPES + 8 + i, i - 4)
                    if h == 0 and i in (3, 4):
                        value_lo(g, i - 3)
                    if i >= 4 and h == 0 and not first:
                        add_out(g * 2 - 1, i - 4)
                    if i >= 4 and h == 2:
                        add_out(g * 2, i - 4)
                    if i == 7:
                        attended_lo(g, h, 0)

                dve.wait_ge(tables_in, 32)
                for r in range(4):
                    times_cos(r, r % CH)
                groups(dve, slot)
                g = KV0 - 1
                inverse_sum(g, UNITS - 1)
                probs_lo(g, UNITS - 2)
                probs_lo(g, UNITS - 1)
                attended_lo(g, PER_KV - 1, 1)
                for j in range(4):
                    add_out(2 * KV0 - 1, j)


            @block.gpsimd
            def _(pool):
                def alone():
                    pool.nop(nofuse=True)

                def turn_sum(r, job, c, dst):
                    pool.wait_ge(rope_swapped, r + 1)
                    pool.tensor_tensor(swapped[:, :], swapped[:, :], sin[:, c * BANK:(c + 1) * BANK], ALU.mult).then_inc(rope_sin, 1)
                    pool.wait_ge(proj_free, job + 1)
                    pool.wait_ge(rope_sin, r + 1)
                    return pool.tensor_tensor(dst, turned[:, :], swapped[:, :], ALU.add)

                def key_turn(r, job, g, c):
                    if not (isinstance(g, int) and g == 0):
                        pool.wait_ge(keys_ready, g)
                    turn_sum(r, job, c, k_next[:, c * BANK:(c + 1) * BANK]).then_inc(rope_done, 1)

                def query_turn(r, job, n, g, h, c, free=False):
                    turn_sum(r, job, c, turned[:, :]).then_inc(rope_sum, 1)
                    out = q[h % 2][:, c * BANK:(c + 1) * BANK]
                    if not free:
                        pool.wait_ge(scores_mm, g * UNITS + (h - 1) * NT)
                    pool.wait_ge(rope_sum, n + 1)
                    alone()
                    pool.tensor_scalar(out.hi, turned[:, :], 1.0, 1.0, ALU.mult, ALU.mult).then_inc(query_hi, 1)
                    pool.wait_ge(query_hi, n + 1)
                    pool.tensor_tensor(out.lo, turned[:, :], as_f32(out.hi), ALU.subtract).then_inc(rope_done, 1)

                def split_weights(n, staged, out, ready):
                    alone()
                    pool.tensor_scalar(out.hi, staged, 1.0, 1.0, ALU.mult, ALU.mult).then_inc(w_hi, 1)
                    pool.wait_ge(w_hi, n + 1)
                    pool.tensor_tensor(out.lo, staged, as_f32(out.hi), ALU.subtract).then_inc(ready, 1)

                def split_q(n, head, projected):
                    pool.wait_ge(wq_loaded, head * 16 + 16)
                    if projected is not None:
                        pool.wait_ge(rope_mm, projected)
                    split_weights(n, wq_in[:, :, :], wq, wq_ready)

                def split_kv(n, g):
                    pool.wait_ge(wkv_loaded, g * 32 + 32)
                    if not (isinstance(g, int) and g == 0):
                        pool.wait_ge(v_mm, g * 2)
                    split_weights(n, wkv_in[:, :, :, :], wkv, wkv_ready)

                def split_o(n, pair_index):
                    pool.wait_ge(wo_loaded, pair_index * 16 + 16)
                    for hh in range(2):
                        pool.tensor_tensor(wo_in[:, hh, :], wo_in[:, hh, :], m.gate[:, 0, 0, :], ALU.mult).then_inc(wo_gated, 1)
                    pool.wait_ge(wo_gated, pair_index * 2 + 2)
                    if not (isinstance(pair_index, int) and pair_index == 0):
                        pool.wait_ge(out_mm, pair_index * 4)
                    split_weights(n, wo_in[:, :, :], wo, wo_ready)

                def normalise(g, s):
                    width = (s % NT + 1) * P
                    pool.wait_ge(rinv_done, g * UNITS + s + 1)
                    alone()
                    pool.tensor_scalar(probs[:, s % 4, 0:width], probs[:, s % 4, 0:width], rinv[:, s % 4:s % 4 + 1], 1.0,
                                       ALU.mult, ALU.mult).then_inc(normed, 1)

                def slot(g, s, first, last):
                    h, i = divmod(s, NT)
                    if s:
                        normalise(g, s - 1)
                    elif not first:
                        normalise(g - 1, UNITS - 1)
                    r = g * ROPES + 4 + 2 * h + i
                    if i < 2 and h < PER_KV - 1:
                        query_turn(r, job_base(g, (0, 8, 10)[h] + i), g * 8 + 2 + 2 * h + i, g, h + 1, i, first and h == 0)
                    if i < 2 and h == PER_KV - 1 and not last:
                        query_turn(r, job_base(g, 16 + i), g * 8 + 8 + i, g + 1, 0, i)
                    if h == PER_KV - 1 and i in (4, 5) and not last:
                        key_turn(g * ROPES + 8 + i, job_base(g, 14 + i), g + 1, i - 4)
                    n = g * 7 + 3
                    if (h, i) == (0, 2):
                        split_q(n, g * PER_KV + 2, g * ROPES + 6)
                    if (h, i) == (1, 2):
                        split_q(n + 1, g * PER_KV + 3, g * ROPES + 8)
                    if (h, i) == (1, 4) and not last:
                        split_kv(n + 2, g + 1)
                    if (h, i) == (1, 5):
                        split_o(n + (2 if last else 3), g * 2)
                    if (h, i) == (2, 2) and not last:
                        split_q(n + 4, g * PER_KV + 4, g * ROPES + 10)
                    if (h, i) == (3, 2) and not last:
                        split_q(n + 5, g * PER_KV + 5, g * ROPES + 12)
                    if (h, i) == (3, 3):
                        split_o(n + (3 if last else 6), g * 2 + 1)

                split_kv(0, 0)
                split_q(1, 0, None)
                pool.wait_ge(tables_in, 32)
                for c in range(CH):
                    key_turn(c, c, 0, c)
                for c in range(CH):
                    query_turn(2 + c, 2 + c, c, 0, 0, c, True)
                split_q(2, 1, 4)
                groups(pool, slot)
                normalise(KV0 - 1, UNITS - 1)


def ffn0(nc, a, m, sems, sb, split):
    with ExitStack() as ctx:
        def buf(name, shape, dt=F32):
            return sb("ff0_" + name, shape, dt, ctx)

        def pair(name, shape):
            return split("ff0_" + name, shape, ctx)

        def sem(name):
            return sems("ff0_" + name)

        wg_in, wu_in, wd_in = (m.staging[:, n * 2048:(n + 1) * 2048] for n in range(3))
        wg, wu, wd = pair("wg", [P, KD, I0]), pair("wu", [P, KD, I0]), pair("wd", [P, I0 // P, DM])
        xn = [buf(f"xn{n}", [P, DM]) for n in range(2)]
        h32 = buf("h32", [P, KD, P])
        hx = [pair(f"hx{n}", [P, KD, P]) for n in range(2)]
        sg, absh = buf("sg", [P, I0]), buf("absh", [P, I0])
        h = [buf(f"h{n}", [P, I0]) for n in range(2)]
        cx, cy, cz, cs, ct = (buf(n, [P, 2, I0 // 4], BF16) for n in ("cx", "cy", "cz", "cs", "ct"))
        wins = buf("wins", [P, 4, I0 // 4], BF16)
        hsT = pair("hsT", [P, I0 // P, P])
        p_gate, p_up = (ctx.enter_context(nc.psum_tensor(f"ff0_{n}", [P, I0], F32)) for n in ("gate", "up"))
        p_turn = [ctx.enter_context(nc.psum_tensor(f"ff0_turn{n}", [P, 4, P], F32)) for n in range(2)]
        p_x = ctx.enter_context(nc.psum_tensor("ff0_x", [P, BANK], F32))
        p_y = ctx.enter_context(nc.psum_tensor("ff0_y", [P, BANK], F32))
        sqrt_in, sqrt_out, chain_sem = sem("sqrt_in"), sem("sqrt_out"), sem("chain")
        w_hi, wgu_ready, wd_gated, wd_hi, wd_ready = (sem(n) for n in ("w_hi", "wgu_ready", "wd_gated", "wd_hi", "wd_ready"))
        normed, x_mm, h32_done, hx_hi, hx_ready = (sem(n) for n in ("normed", "x_mm", "h32_done", "hx_hi", "hx_ready"))
        gate_mm, up_mm, silu_done, mul_done, abs_done = (sem(n) for n in ("gate_mm", "up_mm", "silu_done", "mul_done", "abs_done"))
        compared, summed, won, sparse = (sem(n) for n in ("compared", "summed", "won", "sparse"))
        turn_mm, turn_hi, turn_lo, down_mm, added = (sem(n) for n in ("turn_mm", "turn_hi", "turn_lo", "down_mm", "added"))

        OPEN = 1

        def zero(t):
            return isinstance(t, int) and t == 0

        def tiles(engine, step, between=lambda: None):
            step(0, 0, True, False)
            between()
            with engine.Fori(0, NT // 2 - 1) as r:
                step(r * 2 + 1, 1, False, False)
                step(r * 2 + 2, 0, False, False)
            step(NT - 1, 1, False, True)

        with nc.Block() as block:
            @block.tensor
            def _(pe):
                def turn_x(t, b):
                    pe.wait_ge(normed, t + 1)
                    if not zero(t):
                        pe.wait_ge(h32_done, t)
                    for k in range(KD):
                        mm = pe.transpose(p_x[:, k * P:(k + 1) * P], xn[b][:, k * P:(k + 1) * P], m.ident[:, :])
                    mm.then_inc(x_mm, 1)

                def gate_up(t, b):
                    pe.wait_ge(hx_ready, t + 1)
                    for w, out, free, done in ((wg, p_gate, silu_done, gate_mm), (wu, p_up, mul_done, up_mm)):
                        if not zero(t):
                            pe.wait_ge(free, t)
                        for c in range(I0 // BANK):
                            cols = slice(c * BANK, (c + 1) * BANK)
                            for k in range(KD):
                                mm = product(pe, out[:, cols], hx[b][:, k, :], w[:, k, cols], k == 0, k == KD - 1)
                        mm.then_inc(done, 1)

                def turn_h(t, b):
                    pe.wait_ge(sparse, t * 4 + 4)
                    pe.wait_ge(turn_lo, OPEN + t * 2)
                    for n in range(2):
                        for j in range(4):
                            c = 4 * n + j
                            mm = pe.transpose(p_turn[n][:, j, :], h[b][:, c * P:(c + 1) * P], m.ident[:, :])
                        mm.then_inc(turn_mm, 1)

                def down(t):
                    pe.wait_ge(added, OPEN + t)
                    for c in range(I0 // P):
                        if c % 4 == 0:
                            pe.wait_ge(turn_lo, OPEN + t * 2 + 1 + c // 4)
                        mm = product(pe, p_y[:, 0:DM], hsT[:, c, :], wd[:, c, :], c == 0, c == I0 // P - 1)
                    mm.then_inc(down_mm, 1)

                def step(t, b, first, last):
                    if not last:
                        turn_x(t + 1, 1 - b)
                    gate_up(t, b)
                    if not first:
                        turn_h(t - 1, 1 - b)
                        down(t - 1)

                pe.sem_inc(turn_mm, OPEN)
                pe.sem_inc(down_mm, OPEN)
                turn_x(0, 0)
                pe.wait_ge(wgu_ready, 4)
                tiles(pe, step, lambda: pe.wait_ge(wd_ready, 1))
                turn_h(NT - 1, 1)
                down(NT - 1)

            @block.scalar
            def _(act):
                for n, (w, w_in) in enumerate(((wg, wg_in), (wu, wu_in))):
                    act.wait_ge(m.staged, 16 * (n + 1))
                    for k in range(KD):
                        act.activation(w.hi[:, k, :], w_in[:, k * I0:(k + 1) * I0], ACT.Copy).then_inc(w_hi, 1)
                row_stats_sqrt(act, m, sqrt_in, sqrt_out)

                def scale_shift(t):
                    act.wait_ge(x_mm, t + 1)
                    if not zero(t):
                        act.wait_ge(hx_ready, t)
                    for k in range(KD):
                        ins = act.activation(h32[:, k, :], p_x[:, k * P:(k + 1) * P], ACT.Identity,
                                             scale=m.modcol[:, 0, 8 + k:9 + k], bias=m.modcol[:, 0, 6 + k:7 + k])
                    ins.then_inc(h32_done, 1)

                def silu(t):
                    act.wait_ge(gate_mm, t + 1)
                    if not zero(t):
                        act.wait_ge(mul_done, t)
                    act.activation(sg[:, :], p_gate[:, :], ACT.Silu).then_inc(silu_done, 1)

                def turned_hi(t):
                    for n in range(2):
                        act.wait_ge(turn_mm, OPEN + t * 2 + n + 1)
                        if n == 0:
                            act.wait_ge(down_mm, OPEN + t)
                        act.activation(hsT.hi[:, 4 * n:4 * n + 4, :], p_turn[n][:, :, :], ACT.Copy).then_inc(turn_hi, 1)

                def magnitude(t, b):
                    act.wait_ge(mul_done, t + 1)
                    if not zero(t):
                        act.wait_ge(compared, t * 3)
                    act.activation(absh[:, :], h[b][:, :], ACT.Abs).then_inc(abs_done, 1)

                def step(t, b, first, last):
                    if not last:
                        scale_shift(t + 1)
                    silu(t)
                    magnitude(t, b)
                    if not first:
                        turned_hi(t - 1)

                scale_shift(0)
                tiles(act, step)
                turned_hi(NT - 1)

            @block.vector
            def _(dve):
                dve.sem_inc(turn_lo, OPEN)
                dve.sem_inc(added, OPEN)
                chain = Chain(dve, chain_sem)
                row_stats(dve, m, chain, sqrt_in, sqrt_out)

                def norm(t, b):
                    if not (isinstance(t, int) and t < 2):
                        dve.wait_ge(x_mm, t - 1)
                    dve.tensor_scalar(xn[b][:, :], m.x[:, bass.ds(t, 1), :], m.meanvar[:, bass.ds(t, 1), 0], m.rstd[:, bass.ds(t, 1)],
                                      ALU.subtract, ALU.mult).then_inc(normed, 1)

                def multiply(t, b):
                    dve.wait_ge(silu_done, t + 1)
                    dve.wait_ge(up_mm, t + 1)
                    if not (isinstance(t, int) and t < 2):
                        dve.wait_ge(turn_mm, OPEN + t * 2 - 2)
                    dve.tensor_tensor(h[b][:, :], sg[:, :], p_up[:, :], ALU.mult).then_inc(mul_done, 1)

                def sparsify(t, b):
                    four = absh[:, :].rearrange("p (g e) -> p g e", e=4)

                    def by_group(plane):
                        return plane[:, :, :].rearrange("p e g -> p g e")

                    dve.wait_ge(abs_done, t + 1)
                    dve.tensor_tensor(by_group(cx), four[:, :, 0:2], four[:, :, 2:4], ALU.is_ge).then_inc(compared, 1)
                    dve.tensor_tensor(by_group(cy), four[:, :, 0:2], four[:, :, 3:1:-1], ALU.is_ge).then_inc(compared, 1)
                    dve.tensor_tensor(by_group(cz), four[:, :, 0:4:2], four[:, :, 1:4:2], ALU.is_ge).then_inc(compared, 1)
                    dve.wait_ge(compared, t * 3 + 3)
                    dve.tensor_tensor(cs[:, :, :], cx[:, :, :], cy[:, :, :], ALU.add).then_inc(summed, 1)
                    dve.tensor_tensor(ct[:, :, :], cx[:, :, :], cy[:, 1::-1, :], ALU.add).then_inc(summed, 1)
                    dve.wait_ge(summed, t * 2 + 2)
                    dve.tensor_tensor(wins[:, 0, :], cs[:, 0, :], cz[:, 0, :], ALU.add).then_inc(won, 1)
                    dve.tensor_tensor(wins[:, 1, :], cs[:, 1, :], cz[:, 0, :], ALU.subtract).then_inc(won, 1)
                    dve.tensor_tensor(wins[:, 2, :], cz[:, 1, :], ct[:, 0, :], ALU.subtract).then_inc(won, 1)
                    dve.tensor_tensor(wins[:, 3, :], ct[:, 1, :], cz[:, 1, :], ALU.add).then_inc(won, 1)
                    dve.wait_ge(won, t * 4 + 4)
                    kept = h[b][:, :].rearrange("p (g e) -> p g e", e=4)
                    for e, (test, bound) in enumerate(((ALU.is_ge, 2.0), (ALU.is_ge, 1.0), (ALU.is_ge, 0.0), (ALU.is_le, 1.0))):
                        dve.scalar_tensor_tensor(out=kept[:, :, e], in0=wins[:, e, :], scalar=bound, in1=kept[:, :, e],
                                                 op0=test, op1=ALU.mult).then_inc(sparse, 1)

                def turned_lo(t):
                    for n in range(2):
                        out = hsT[:, 4 * n:4 * n + 4, :]
                        dve.wait_ge(turn_hi, t * 2 + n + 1)
                        dve.tensor_tensor(out.lo, p_turn[n][:, :, :], as_f32(out.hi), ALU.subtract).then_inc(turn_lo, 1)

                def add(t):
                    dve.wait_ge(down_mm, OPEN + t + 1)
                    rows = m.x[:, bass.ds(t, 1), :].rearrange("p o d -> p (o d)")
                    dve.tensor_tensor(rows, p_y[:, 0:DM], rows, ALU.add).then_inc(added, 1)

                def step(t, b, first, last):
                    if not last:
                        norm(t + 1, 1 - b)
                    multiply(t, b)
                    if not first:
                        turned_lo(t - 1)
                    sparsify(t, b)
                    if not first:
                        add(t - 1)

                norm(0, 0)
                for n, (w, w_in) in enumerate(((wg, wg_in), (wu, wu_in))):
                    for k in range(KD):
                        dve.wait_ge(w_hi, 2 * n + k + 1)
                        dve.tensor_tensor(w.lo[:, k, :], w_in[:, k * I0:(k + 1) * I0], as_f32(w.hi[:, k, :]), ALU.subtract)\
                           .then_inc(wgu_ready, 1)
                tiles(dve, step)
                turned_lo(NT - 1)
                add(NT - 1)

            @block.gpsimd
            def _(pool):
                def split_x(t, b):
                    pool.wait_ge(h32_done, t + 1)
                    if not (isinstance(t, int) and t < 2):
                        pool.wait_ge(up_mm, t - 1)
                    pool.nop(nofuse=True)
                    pool.tensor_scalar(hx[b].hi[:, :, :], h32[:, :, :], 1.0, 1.0, ALU.mult, ALU.mult).then_inc(hx_hi, 1)
                    pool.wait_ge(hx_hi, t + 1)
                    pool.tensor_tensor(hx[b].lo[:, :, :], h32[:, :, :], as_f32(hx[b].hi[:, :, :]), ALU.subtract).then_inc(hx_ready, 1)

                def step(t, b, first, last):
                    if not last:
                        split_x(t + 1, 1 - b)

                split_x(0, 0)
                split_x(1, 1)
                pool.wait_ge(m.staged, 48)
                for c in range(I0 // P):
                    rows = wd_in[:, c * DM:(c + 1) * DM]
                    pool.tensor_tensor(rows, rows, m.gate[:, 0, 1, :], ALU.mult).then_inc(wd_gated, 1)
                pool.wait_ge(wd_gated, I0 // P)
                flat = wd("p c d -> p (c d)")
                pool.tensor_scalar(flat.hi, wd_in, 1.0, 1.0, ALU.mult, ALU.mult).then_inc(wd_hi, 1)
                pool.wait_ge(wd_hi, 1)
                pool.tensor_tensor(flat.lo, wd_in, as_f32(flat.hi), ALU.subtract).then_inc(wd_ready, 1)

                with pool.Fori(0, NT // 2 - 1) as r:
                    split_x(r * 2 + 2, 0)
                    split_x(r * 2 + 3, 1)


def attention1(nc, a, m, sems, sb, split):
    HS = H1 * NT
    ctx = ExitStack()
    with ctx:
        def buf(name, shape, dt=F32, c=ctx):
            return sb("at1_" + name, shape, dt, c)

        def sem(name):
            return sems("at1_" + name)

        h32 = buf("h32", [P, KD, S])
        transposed_rows(nc, m, sems, sb, 1, 0, "ln2", keep=h32)
        gT = m.hT
        wq, wk, wv = (split(f"at1_{n}", [P, KD, w], ctx) for n, w in (("wq", H1 * D1), ("wk", G1 * D1), ("wv", G1 * D1)))
        wo = split("at1_wo", [P, H1, DM], ctx)
        gated_ident = buf("gated_ident", [P, KD, P])
        norm_col = buf("norm_col", [P, 3, KD])
        wo_in = m.staging1[:, 1024:2048].rearrange("p (h n) -> p h n", h=H1)
        q = [buf(f"q{n}", [P, S], F32R) for n in range(2)]
        khi, klo = ([buf(f"{n}{g}", [P, S], F32R) for g in range(G1)] for n in ("khi", "klo"))
        v = [buf(f"v{g}", [P, NT, 2, D1], F32R) for g in range(G1)]
        staging = m.staging1
        wq_in = staging[:, 0:512].rearrange("p (k n) -> p k n", k=KD)
        wk_in = staging[:, 512:768].rearrange("p (k n) -> p k n", k=KD)
        wv_in = staging[:, 768:1024].rearrange("p (k n) -> p k n", k=KD)

        with ExitStack() as c1:
            square = buf("square", [P, KD, S], F32, c1)
            inv = buf("inv", [P, S], F32, c1)
            p_sum = c1.enter_context(nc.psum_tensor("at1_sum", [P, S], F32))
            small_in, squared, sum_mm, rooted, chain_sem, w_hi, ready = (
                sem(n) for n in ("small_in", "squared", "sum_mm", "rooted", "chain", "w_hi", "w_ready"))
            with nc.Block() as block:
                @block.sync
                def _(sp):
                    for n in range(2):
                        sp.dma_start(norm_col[:, n, :], a[("L1_attn_norm_scale", "L1_attn_split_scale")[n]]).then_inc(small_in, 16)
                    w1 = m.staging[:, 0:4096].rearrange("p (e k n) -> p e k n", e=8, k=KD)
                    w2 = m.staging[:, 4096:6144].rearrange("p (e n) -> p e n", e=8)
                    for e in range(8):
                        src1 = a["L1_ffn_shared_w1"][0] if e == 0 else a["L1_ffn_routed_w1"][e - 1]
                        sp.dma_start(w1[:, e, :, :], src1.rearrange("(k p) n -> p k n", p=P)).then_inc(m.staged, 16)
                    sp.dma_start(w2[:, 0, :], a["L1_ffn_shared_w2"][0]).then_inc(m.staged, 16)
                    sp.dma_start(w2[:, 1:8, :], a["L1_ffn_routed_w2"].rearrange("e p n -> p e n")).then_inc(m.staged, 16)

                @block.scalar
                def _(act):
                    for k in range(KD):
                        act.activation(square[:, k, :], h32[:, k, :], ACT.Square).then_inc(squared, 1)
                    act.wait_ge(m.staged1, 80)
                    for w, w_in in ((wq, wq_in), (wk, wk_in), (wv, wv_in)):
                        act.activation(w.hi, w_in, ACT.Copy).then_inc(w_hi, 1)
                    for half in range(2):
                        act.wait_ge(sum_mm, half + 1)
                        act.activation(inv[:, half * BANK:(half + 1) * BANK], p_sum[:, half * BANK:(half + 1) * BANK],
                                       ACT.Sqrt, scale=1.0 / DM).then_inc(rooted, 1)

                @block.tensor
                def _(pe):
                    pe.wait_ge(squared, KD)
                    for half in range(2):
                        cols = slice(half * BANK, (half + 1) * BANK)
                        for k in range(KD):
                            mm = pe.matmul(p_sum[:, cols], m.ones[:, :], square[:, k, cols], start=(k == 0), stop=(k == KD - 1))
                        mm.then_inc(sum_mm, 1)

                @block.vector
                def _(dve):
                    chain = Chain(dve, chain_sem)
                    dve.wait_ge(small_in, 32)
                    chain.run(dve.tensor_tensor(norm_col[:, 2, :], norm_col[:, 0, :], norm_col[:, 1, :], ALU.mult))
                    for k in range(KD):
                        chain.step(dve.tensor_tensor(gated_ident[:, k, :], m.ident[:, :], m.gate[:, 1, 0, k * P:(k + 1) * P], ALU.mult))
                    for half in range(2):
                        cols = slice(half * BANK, (half + 1) * BANK)
                        part = inv[:, cols]
                        dve.wait_ge(rooted, half + 1)
                        chain.run(dve.tensor_scalar(part, part, RMS_EPS, None, ALU.add))
                        chain.run(dve.reciprocal(part, part))
                        for k in range(KD):
                            chain.run(dve.scalar_tensor_tensor(out=square[:, k, cols], in0=h32[:, k, cols], scalar=norm_col[:, 2, k:k + 1],
                                                               in1=part, op0=ALU.mult, op1=ALU.mult))
                            chain.run(dve.tensor_copy(gT.hi[:, k, cols], square[:, k, cols]))
                            chain.run(dve.tensor_tensor(gT.lo[:, k, cols], square[:, k, cols], as_f32(gT.hi[:, k, cols]), ALU.subtract))
                    for n, (w, w_in) in enumerate(((wq, wq_in), (wk, wk_in), (wv, wv_in))):
                        dve.wait_ge(w_hi, n + 1)
                        dve.tensor_tensor(w.lo, w_in, as_f32(w.hi), ALU.subtract).then_inc(ready, 1)

                @block.gpsimd
                def _(pool):
                    chain = Chain(pool, sem("pool_chain"))
                    pool.wait_ge(m.staged1, 80)
                    for h in range(H1):
                        chain.step(pool.tensor_tensor(wo_in[:, h, :], wo_in[:, h, :], m.gate[:, 1, 0, :], ALU.mult))
                    chain.settle()
                    chain.run(pool.tensor_scalar(wo.hi, wo_in[:, :, :], 1.0, 1.0, ALU.mult, ALU.mult))
                    chain.run(pool.tensor_tensor(wo.lo, wo_in[:, :, :], as_f32(wo.hi), ALU.subtract))

        more_probs = buf("probs", [P, 2, S])
        probs = [staging[:, n * S:(n + 1) * S] for n in range(2)] + [more_probs[:, n, :] for n in range(2)]
        negmax, rowsum, rinv = buf("negmax", [P, 4]), buf("rowsum", [P, 4]), buf("rinv", [P, 4])
        pT = [split(f"at1_pT{n}", [P, NT, BANK], ctx) for n in range(2)]
        att = split("at1_att", [P, 2, S], ctx)
        p_scores = [ctx.enter_context(nc.psum_tensor(f"at1_scores{n}", [P, S], F32)) for n in range(2)]
        p_turn = [ctx.enter_context(nc.psum_tensor(f"at1_turn{n}", [P, 4, P], F32)) for n in range(2)]
        p_att = ctx.enter_context(nc.psum_tensor("at1_att_sum", [P, BANK], F32))
        p_proj = ctx.enter_context(nc.psum_tensor("at1_proj", [P, BANK], F32))
        job_mm, job_hi, proj_free = sem("job_mm"), sem("job_hi"), sem("proj_free")
        scores_mm, max_done, exp_done, rinv_done, normed = (sem(n) for n in ("scores_mm", "max_done", "exp_done", "rinv_done", "normed"))
        turn_mm, turn_hi, turn_lo = sem("turn_mm"), sem("turn_hi"), sem("turn_lo")
        att_mm, att_hi, att_lo = sem("att_mm"), sem("att_hi"), sem("att_lo")
        out_mm, out_added, bias_done = sem("out_mm"), sem("out_added"), sem("bias_done")
        SCALE = float(D1) ** -0.5

        jobs = [("k", 0, 0), ("k", 0, 1), ("q", 0, 0), ("q", 0, 1), ("v", 0, 0)]
        jobs += [("q", 1, 0), ("q", 1, 1), ("k", 1, 0), ("k", 1, 1), ("v", 1, 0), ("q", 2, 0), ("q", 2, 1), ("q", 3, 0), ("q", 3, 1)]
        first_slot = dict(zip(jobs[5:], (1, 3, 9, 11, 12, 13, 14, 17, 19)))

        def jobs_of(slot):
            return [(n, job) for n, job in enumerate(jobs) if first_slot.get(job, -1) == slot]

        out_slots = {22: (0,), 23: (1,), 24: (2, 3)}

        def out_bank(pair_index, j):
            return (p_proj, p_att)[j % 2 if pair_index else 0]

        with nc.Block() as block:
            @block.tensor
            def _(pe):
                def project(n, kind, index, c):
                    if n:
                        pe.wait_ge(proj_free, n)
                    cols = slice(index * D1, (index + 1) * D1)
                    if kind == "v":
                        for t in range(NT):
                            rows = slice(t * P, (t + 1) * P)
                            for k in range(KD):
                                mm = product(pe, p_proj[:, t * D1:(t + 1) * D1], gT[:, k, rows], wv[:, k, cols], k == 0, k == KD - 1)
                    else:
                        w = wq if kind == "q" else wk
                        for k in range(KD):
                            mm = product(pe, p_proj[0:D1, :], w[:, k, cols], gT[:, k, c * BANK:(c + 1) * BANK], k == 0, k == KD - 1)
                    mm.then_inc(job_mm, 1)

                def scores(s):
                    h, i = divmod(s, NT)
                    g = h // (H1 // G1)
                    if i == 0:
                        pe.wait_ge(proj_free, jobs.index(("q", h, 1)) + 1)
                        pe.wait_ge(proj_free, jobs.index(("k", g, 1)) + 1)
                    if s >= 2:
                        pe.wait_ge(exp_done, s - 1)
                    for c in range(2):
                        cols = slice(c * BANK, (c + 1) * BANK)
                        rows = q[h % 2][:, i * P:(i + 1) * P]
                        pe.matmul(p_scores[s % 2][:, cols], rows, khi[g][:, cols], start=True, stop=False)
                        mm = pe.matmul(p_scores[s % 2][:, cols], rows, klo[g][:, cols], start=False, stop=True)
                    mm.then_inc(scores_mm, 1)

                def turn(s):
                    pe.wait_ge(normed, s + 1)
                    for n in range(2):
                        if s:
                            pe.wait_ge(turn_lo, 2 * s - 1 + n)
                        for b in range(4):
                            mm = pe.transpose(p_turn[n][:, b, :], probs[s % 4][:, (4 * n + b) * P:(4 * n + b + 1) * P], m.ident[:, :])
                        mm.then_inc(turn_mm, 1)

                def attend(chunk, part):
                    g = chunk // 2 // (H1 // G1)
                    if part == 0:
                        pe.wait_ge(turn_lo, 8 * chunk + 8)
                        pe.wait_ge(proj_free, jobs.index(("v", g, 0)) + 1)
                        if chunk:
                            pe.wait_ge(att_lo, chunk)
                    for t in range(2 * part, 2 * part + 2):
                        values = v[g][:, t, :, :].rearrange("p a d -> p (a d)")
                        pe.matmul(p_att[:, :], values, pT[chunk % 2].hi[:, t, :], start=(t == 0), stop=False)
                        mm = pe.matmul(p_att[:, :], values, pT[chunk % 2].lo[:, t, :], start=False, stop=(t == NT - 1))
                    if part == 3:
                        mm.then_inc(att_mm, 1)

                def out_job(pair_index, j):
                    bank = out_bank(pair_index, j)
                    pe.wait_ge(proj_free, len(jobs) + 4 * pair_index + j)
                    pe.wait_ge(att_lo, 4 * pair_index + 4)
                    for n in range(2):
                        rows = slice((2 * j + n) * P, (2 * j + n + 1) * P)
                        for h in range(2):
                            mm = product(pe, bank[:, n * DM:(n + 1) * DM], att[:, h, rows], wo[:, 2 * pair_index + h, :],
                                         h == 0, h == 1 and pair_index == 0)
                        for k in range(KD if pair_index else 0):
                            mm = pe.matmul(bank[:, n * DM + k * P:n * DM + (k + 1) * P], h32[:, k, rows], gated_ident[:, k, :],
                                           start=False, stop=(k == KD - 1))
                    mm.then_inc(out_mm, 1)

                for n, job in jobs_of(-1):
                    project(n, *job)
                for s in range(HS):
                    scores(s)
                    if s >= 2:
                        turn(s - 2)
                    if s >= 6:
                        attend((s - 6) // 4, (s - 6) % 4)
                    for n, job in jobs_of(s):
                        project(n, *job)
                    for j in out_slots.get(s, ()):
                        out_job(0, j)
                for s in range(HS, HS + 6):
                    if s < HS + 2:
                        turn(s - 2)
                    attend((s - 6) // 4, (s - 6) % 4)
                for j in range(4):
                    out_job(1, j)

            @block.scalar
            def _(act):
                def job_high(n, kind, index, c):
                    act.wait_ge(job_mm, n + 1)
                    cols = slice(c * BANK, (c + 1) * BANK)
                    if kind == "v":
                        act.activation(v[index][:, :, 0, :], p_proj[:, :].rearrange("p (t d) -> p t d", d=D1), ACT.Copy).then_inc(job_hi, 1)
                    elif kind == "q":
                        if index >= 2:
                            act.wait_ge(scores_mm, (index - 1) * NT)
                        act.activation(q[index % 2][0:D1, cols], p_proj[0:D1, :], ACT.Copy).then_inc(job_hi, 1)
                    else:
                        act.activation(khi[index][D1:P, cols], p_proj[0:D1, :], ACT.Copy)
                        act.activation(khi[index][0:D1, cols], p_proj[0:D1, :], ACT.Copy).then_inc(job_hi, 1)

                def probs_hi(s):
                    chunk = s // 4
                    if s % 4 == 0 and chunk >= 2:
                        act.wait_ge(att_mm, chunk - 1)
                    for n in range(2):
                        act.wait_ge(turn_mm, 2 * s + n + 1)
                        act.activation(pT[chunk % 2].hi[:, 4 * n:4 * n + 4, (s % 4) * P:(s % 4 + 1) * P], p_turn[n][:, :, :], ACT.Copy)\
                           .then_inc(turn_hi, 1)

                def exp(s):
                    act.wait_ge(max_done, s + 1)
                    act.activation(negmax[:, s % 4:s % 4 + 1], negmax[:, s % 4:s % 4 + 1], ACT.Copy, scale=SCALE).then_inc(bias_done, 1)
                    if s >= 4:
                        act.wait_ge(turn_mm, 2 * (s - 3))
                    act.wait_ge(bias_done, s + 1)
                    act.activation(probs[s % 4], p_scores[s % 2][:, :], ACT.Exp, scale=SCALE,
                                   bias=negmax[:, s % 4:s % 4 + 1], accum_out=rowsum[:, s % 4:s % 4 + 1]).then_inc(exp_done, 1)

                def attended_hi(chunk):
                    act.wait_ge(att_mm, chunk + 1)
                    if chunk == 4:
                        act.wait_ge(out_mm, 4)
                    act.activation(att.hi[:, chunk // 2 % 2, chunk % 2 * BANK:(chunk % 2 + 1) * BANK], p_att[:, :], ACT.Copy).then_inc(att_hi, 1)

                for n, job in jobs_of(-1):
                    job_high(n, *job)
                for s in range(HS + 2):
                    if s >= 2:
                        probs_hi(s - 2)
                    if s < HS:
                        exp(s)
                    if s >= 9 and (s - 9) % 4 == 0:
                        attended_hi((s - 9) // 4)
                    for n, job in jobs_of(s):
                        job_high(n, *job)
                for chunk in range((HS + 1 - 9) // 4 + 1, 2 * H1):
                    attended_hi(chunk)

            @block.vector
            def _(dve):
                def job_low(n, kind, index, c):
                    dve.wait_ge(job_hi, n + 1)
                    cols = slice(c * BANK, (c + 1) * BANK)
                    if kind == "v":
                        dve.tensor_tensor(v[index][:, :, 1, :], p_proj[:, :].rearrange("p (t d) -> p t d", d=D1),
                                          as_f32(v[index][:, :, 0, :]), ALU.subtract).then_inc(proj_free, 1)
                    elif kind == "q":
                        out = q[index % 2]
                        dve.tensor_tensor(out[D1:P, cols], p_proj[0:D1, :], as_f32(out[0:D1, cols]), ALU.subtract).then_inc(proj_free, 1)
                    else:
                        hi, lo = khi[index], klo[index]
                        dve.tensor_tensor(lo[0:D1, cols], p_proj[0:D1, :], as_f32(hi[0:D1, cols]), ALU.subtract)
                        dve.tensor_tensor(lo[D1:P, cols], p_proj[0:D1, :], as_f32(hi[0:D1, cols]), ALU.subtract).then_inc(proj_free, 1)

                def maximum(s):
                    dve.wait_ge(scores_mm, s + 1)
                    dve.tensor_reduce(negmax[:, s % 4:s % 4 + 1], p_scores[s % 2][:, :], AX.X, ALU.max, negate=True).then_inc(max_done, 1)

                def inverse_sum(s):
                    dve.wait_ge(exp_done, s + 1)
                    dve.reciprocal(rinv[:, s % 4:s % 4 + 1], rowsum[:, s % 4:s % 4 + 1]).then_inc(rinv_done, 1)

                def probs_lo(s):
                    for n in range(2):
                        out = pT[s // 4 % 2][:, 4 * n:4 * n + 4, (s % 4) * P:(s % 4 + 1) * P]
                        dve.wait_ge(turn_hi, 2 * s + n + 1)
                        dve.tensor_tensor(out.lo, p_turn[n][:, :, :], as_f32(out.hi), ALU.subtract).then_inc(turn_lo, 1)

                def attended_lo(chunk):
                    out = att[:, chunk // 2 % 2, chunk % 2 * BANK:(chunk % 2 + 1) * BANK]
                    dve.wait_ge(att_hi, chunk + 1)
                    dve.tensor_tensor(out.lo, p_att[:, :], as_f32(out.hi), ALU.subtract).then_inc(att_lo, 1)

                def add_out(pair_index, j):
                    dve.wait_ge(out_mm, 4 * pair_index + j + 1)
                    rows = m.x[:, 2 * j:2 * j + 2, :]
                    dve.tensor_tensor(rows, out_bank(pair_index, j)[:, :].rearrange("p (n d) -> p n d", n=2), rows, ALU.add)\
                       .then_inc(proj_free, 1)

                for n, job in jobs_of(-1):
                    job_low(n, *job)
                for s in range(HS + 2):
                    if s < HS:
                        maximum(s)
                    if 1 <= s <= HS:
                        inverse_sum(s - 1)
                    if s >= 2:
                        probs_lo(s - 2)
                    if s >= 9 and (s - 9) % 4 == 0:
                        attended_lo((s - 9) // 4)
                    for n, job in jobs_of(s):
                        job_low(n, *job)
                    for j in out_slots.get(s, ()):
                        add_out(0, j)
                for chunk in range((HS + 1 - 9) // 4 + 1, 2 * H1):
                    attended_lo(chunk)
                for j in range(4):
                    add_out(1, j)

            @block.gpsimd
            def _(pool):
                for s in range(HS):
                    pool.wait_ge(rinv_done, s + 1)
                    pool.tensor_scalar(probs[s % 4], probs[s % 4], rinv[:, s % 4:s % 4 + 1], 1.0, ALU.mult, ALU.mult)\
                        .then_inc(normed, 1)


def ffn1(nc, a, m, sems, sb, split):
    transposed_rows(nc, m, sems, sb, 1, 6, "ln3")
    E8 = NE + 1
    with ExitStack() as ctx:
        def buf(name, shape, dt=F32):
            return sb("ff1_" + name, shape, dt, ctx)

        def sem(name):
            return sems("ff1_" + name)

        w1_in = m.staging[:, 0:4096].rearrange("p (e kn) -> p e kn", e=E8)
        w2_in = m.staging[:, 4096:6144].rearrange("p (e n) -> p e n", e=E8)
        w1, w2 = split("ff1_w1", [P, E8, KD * 2 * FE], ctx), split("ff1_w2", [P, E8, DM], ctx)
        gw_in, gw = buf("gw_in", [P, KD, E8]), split("ff1_gw", [P, KD, E8], ctx)
        bias = buf("bias", [1, E8])
        aff, marked = buf("aff", [P, NT, 16]), buf("marked", [P, NT, 16])
        best, best2 = buf("best", [P, NT, 8]), buf("best2", [P, NT, 8])
        mask, score = buf("mask", [P, NT, E8]), buf("score", [P, NT, E8])
        PAD = 8
        ranks = [buf(f"ranks{n}", [E8, S + PAD]) for n in range(2)]
        positive, weight = buf("positive", [E8, S]), buf("weight", [E8, S])
        row_best, row_last = buf("row_best", [E8, 8]), buf("row_last", [E8, 8])
        chosen = [buf(f"chosen{n}", [E8, S]) for n in range(2)]
        x1, act2 = ([buf(f"{s}{n}", [P, BANK]) for n in range(2)] for s in ("x1", "act2"))
        mid = buf("mid", [P, E8, S])
        weighted = buf("weighted", [P, S])
        fed = [split(f"ff1_fed{n}", [P, S], ctx) for n in range(2)]
        p_y = [ctx.enter_context(nc.psum_tensor(f"ff1_y{n}", [P, 2, DM], F32)) for n in range(4)]
        p_x1, p_x2 = ([ctx.enter_context(nc.psum_tensor(f"ff1_{s}{n}", [P, BANK], F32)) for n in range(2)] for s in ("px1", "px2"))
        gate_in, gate_ready, logits_mm, aff_done, score_done, ranks_mm = (
            sem(n) for n in ("gate_in", "gate_ready", "logits_mm", "aff_done", "score_done", "ranks_mm"))
        rank_chain, w1_hi, w1_ready, w2_gated, w2_hi, w2_ready = (
            sem(n) for n in ("rank_chain", "w1_hi", "w1_ready", "w2_gated", "w2_hi", "w2_ready"))
        up_mm, x1_read, x2_read, mid_done = (sem(n) for n in ("up_mm", "x1_read", "x2_read", "mid_done"))
        chosen_done, spread_mm, weighted_done, fed_hi, fed_ready, down_mm, summed, stored = (
            sem(n) for n in ("chosen_done", "spread_mm", "weighted_done", "fed_hi", "fed_ready", "down_mm", "summed", "stored"))

        with nc.Block() as block:
            @block.sync
            def _(sp):
                sp.wait_ge(gate_in, 1)
                with nc.allow_non_contiguous_dma(reason="seven columns"):
                    sp.dma_start(gw_in[:, :, 0:NE], a["L1_ffn_gate_w"].rearrange("(k p) e -> p k e", p=P)).then_inc(gate_in, 16)
                sp.dma_start(bias[0:1, 0:NE], a["L1_ffn_expert_bias"]).then_inc(gate_in, 16)
                rows = a["out"].rearrange("o (n p) d -> p (o n) d", p=P)
                for j in range(4):
                    sp.wait_ge(summed, j + 1)
                    sp.dma_start(rows[:, 2 * j:2 * j + 2, :], m.x[:, 2 * j:2 * j + 2, :]).then_inc(stored, 16)
                sp.wait_ge(stored, 64)

            @block.tensor
            def _(pe):
                p_logits = p_y[0][:, 0, 0:NT * E8]
                p_ranks = [p_y[n + 1][0:E8, :, :].rearrange("e a b -> e (a b)") for n in range(2)]
                pe.wait_ge(gate_ready, 2)
                for t in range(NT):
                    rows, cols = slice(t * P, (t + 1) * P), slice(t * E8, (t + 1) * E8)
                    for k in range(KD):
                        product(pe, p_logits[:, cols], m.hT[:, k, rows], gw[:, k, :], k == 0, False)
                    mm = pe.matmul(p_logits[:, cols], m.ones[0:1, :], bias[0:1, :], start=False, stop=True)
                mm.then_inc(logits_mm, 1)

                def up(e):
                    pe.wait_ge(w1_ready, e + 1)
                    for c in range(2):
                        n = 2 * e + c
                        for half, (bank, read) in enumerate(((p_x1, x1_read), (p_x2, x2_read))):
                            if n >= 2:
                                pe.wait_ge(read, n - 1)
                            for k in range(KD):
                                at = k * 2 * FE + half * FE
                                mm = product(pe, bank[c][:, :], w1[:, e, at:at + FE], m.hT[:, k, c * BANK:(c + 1) * BANK], k == 0, k == KD - 1)
                            mm.then_inc(up_mm, 1)

                def spread(e):
                    pe.wait_ge(chosen_done, e)
                    for c in range(2):
                        if e == 1:
                            pe.wait_ge(x1_read, 2 * E8)
                        else:
                            pe.wait_ge(weighted_done, 2 * (e - 2) + c + 1)
                        pe.matmul(p_x1[c][:, :], m.ones[0:E8, :], chosen[e % 2][:, c * BANK:(c + 1) * BANK], start=True, stop=True)\
                          .then_inc(spread_mm, 1)

                def down(e):
                    if e == 0:
                        pe.wait_ge(w2_ready, 1)
                    pe.wait_ge(fed_ready, 2 * e + 2)
                    for j in range(4):
                        for n in range(2):
                            rows = slice((2 * j + n) * P, (2 * j + n + 1) * P)
                            left, out = fed[e % 2][:, rows], p_y[j][:, n, :]
                            for q, (lhs, rhs) in enumerate(((left.hi, w2.hi[:, e, :]), (left.hi, w2.lo[:, e, :]), (left.lo, w2.hi[:, e, :]))):
                                mm = pe.matmul(out, lhs, rhs, start=(e == 0 and n == 0 and q == 0), stop=(e == E8 - 1 and q == 2),
                                               skip_group_check=True)
                        if e == E8 - 1:
                            mm.then_inc(down_mm, 1)
                    if e < E8 - 1:
                        mm.then_inc(down_mm, 1)

                up(0)
                pe.wait_ge(score_done, 1)
                for t in range(NT):
                    mm = pe.transpose(p_ranks[t // 4][:, t % 4 * P:(t % 4 + 1) * P], score[:, t, :], m.ident[:, :])
                mm.then_inc(ranks_mm, 1)
                for e in range(1, E8):
                    up(e)
                spread(1)
                down(0)
                for e in range(1, E8):
                    if e + 1 < E8:
                        spread(e + 1)
                    down(e)

            @block.scalar
            def _(act):
                def split_hi(e):
                    act.activation(w1.hi[:, e, :], w1_in[:, e, :], ACT.Copy).then_inc(w1_hi, 1)

                act.wait_ge(m.staged, 48 + 160)
                split_hi(0)
                act.wait_ge(logits_mm, 1)
                logits = p_y[0][:, 0, 0:NT * E8].rearrange("p (t e) -> p t e", e=E8)
                act.activation(aff[:, :, 0:NE], logits[:, :, 0:NE], ACT.Sigmoid).then_inc(aff_done, 1)
                for e in range(E8):
                    if e + 1 < E8:
                        split_hi(e + 1)
                    for c in range(2):
                        n = 2 * e + c
                        act.wait_ge(up_mm, 2 * n + 1)
                        if n >= 2:
                            act.wait_ge(mid_done, n - 1)
                        act.activation(x1[c][:, :], p_x1[c][:, :], ACT.Copy).then_inc(x1_read, 1)
                        act.wait_ge(up_mm, 2 * n + 2)
                        act.activation(act2[c][:, :], p_x2[c][:, :], ACT.Silu).then_inc(x2_read, 1)
                for e in range(E8):
                    for c in range(2):
                        cols = slice(c * BANK, (c + 1) * BANK)
                        if e >= 2 and c == 0:
                            act.wait_ge(down_mm, e - 1)
                        if e == 0:
                            act.wait_ge(mid_done, c + 1)
                        else:
                            act.wait_ge(weighted_done, 2 * e - 1 + c)
                        src = mid[:, 0, cols] if e == 0 else weighted[:, cols]
                        act.activation(fed[e % 2].hi[:, cols], src, ACT.Copy).then_inc(fed_hi, 1)

            @block.vector
            def _(dve):
                chain = Chain(dve, rank_chain)
                dve.memset(bias[:, :], 0.0)
                dve.memset(gw_in[:, :, :], 0.0).then_inc(gate_in, 1)
                for tile, value in ((aff, -1.0), (best2, -1.0), (row_last, -1.0), (score, -1.0), (ranks[0], -1.0)):
                    chain.step(dve.memset(tile[:], value))
                dve.wait_ge(gate_in, 33)
                dve.tensor_copy(gw.hi, gw_in[:, :, :]).then_inc(gate_ready, 1)
                dve.wait_ge(gate_ready, 1)
                dve.tensor_tensor(gw.lo, gw_in[:, :, :], as_f32(gw.hi), ALU.subtract).then_inc(gate_ready, 1)
                dve.wait_ge(w1_hi, 1)
                dve.tensor_tensor(w1.lo[:, 0, :], w1_in[:, 0, :], as_f32(w1.hi[:, 0, :]), ALU.subtract).then_inc(w1_ready, 1)

                chain.settle()
                dve.wait_ge(aff_done, 1)
                for t in range(NT):
                    chain.step(dve.max(best[:, t, :], aff[:, t, :]))
                chain.settle()
                chain.run(dve.tensor_copy(best2[:, :, 0:TOPK], best[:, :, 0:TOPK]))
                for t in range(NT):
                    chain.step(dve.match_replace(marked[:, t, :], best2[:, t, :], aff[:, t, :], -5.0))
                chain.settle()
                chain.run(dve.tensor_scalar(mask[:, :, 0:NE], marked[:, :, 0:NE], -5.0, None, ALU.is_equal))
                chain.run(dve.tensor_tensor(marked[:, :, 0:NE], aff[:, :, 0:NE], mask[:, :, 0:NE], ALU.mult))
                dve.scalar_tensor_tensor(out=score[:, :, 0:NE], in0=mask[:, :, 0:NE], scalar=-1.0, in1=marked[:, :, 0:NE],
                                         op0=ALU.add, op1=ALU.add).then_inc(score_done, 1)
                dve.wait_ge(ranks_mm, 1)
                for n in range(2):
                    chain.step(dve.tensor_copy(ranks[0][:, n * BANK:(n + 1) * BANK],
                                               p_y[n + 1][0:E8, :, :].rearrange("e a b -> e (a b)")))
                chain.settle()
                chain.step(dve.tensor_scalar(positive[:, :], ranks[0][:, 0:S], 0.0, None, ALU.max))

                full, rest = divmod(CAPACITY, 8)
                for r in range(full):
                    src, dst = ranks[r % 2], ranks[1 - r % 2]
                    chain.run(dve.max(row_best[:, :], src[:, :]))
                    chain.run(dve.match_replace(dst[:, :], row_best[:, :], src[:, :], -3.0))
                src, dst = ranks[full % 2], ranks[1 - full % 2]
                chain.run(dve.max(row_best[:, :], src[:, :]))
                chain.run(dve.tensor_copy(row_last[:, 0:rest], row_best[:, 0:rest]))
                chain.run(dve.match_replace(dst[:, :], row_last[:, :], src[:, :], -3.0))
                chain.run(dve.scalar_tensor_tensor(out=weight[:, :], in0=dst[:, 0:S], scalar=-3.0, in1=positive[:, :],
                                                   op0=ALU.is_equal, op1=ALU.mult))

                def choose(e):
                    if e > 2:
                        dve.wait_ge(spread_mm, 2 * (e - 2))
                    dve.tensor_scalar(chosen[e % 2][:, :], weight[:, :], m.ident[0:E8, e - 1:e], None, ALU.mult).then_inc(chosen_done, 1)

                def low(e, c):
                    cols = slice(c * BANK, (c + 1) * BANK)
                    dve.wait_ge(fed_hi, 2 * e + c + 1)
                    src = mid[:, 0, cols] if e == 0 else weighted[:, cols]
                    dve.tensor_tensor(fed[e % 2].lo[:, cols], src, as_f32(fed[e % 2].hi[:, cols]), ALU.subtract).then_inc(fed_ready, 1)

                choose(1)
                for e in range(E8):
                    if e:
                        if e < NE:
                            choose(e + 1)
                        for c in range(2):
                            cols = slice(c * BANK, (c + 1) * BANK)
                            dve.wait_ge(mid_done, 2 * e + c + 1)
                            dve.wait_ge(spread_mm, 2 * (e - 1) + c + 1)
                            if e > 1:
                                dve.wait_ge(fed_ready, 2 * e)
                            dve.tensor_tensor(weighted[:, cols], mid[:, e, cols], p_x1[c][:, :], ALU.mult).then_inc(weighted_done, 1)
                    for c in range(2):
                        low(e, c)
                for j in range(4):
                    dve.wait_ge(down_mm, E8 - 1 + j + 1)
                    rows = m.x[:, 2 * j:2 * j + 2, :]
                    dve.tensor_tensor(rows, p_y[j][:, :, :], rows, ALU.add).then_inc(summed, 1)

            @block.gpsimd
            def _(pool):
                def w1_low(e):
                    pool.wait_ge(w1_hi, e + 1)
                    if e == 1:
                        pool.wait_ge(w1_ready, 1)
                    pool.tensor_tensor(w1.lo[:, e, :], w1_in[:, e, :], as_f32(w1.hi[:, e, :]), ALU.subtract).then_inc(w1_ready, 1)

                def middle(e, c):
                    n = 2 * e + c
                    pool.wait_ge(x2_read, n + 1)
                    pool.wait_ge(x1_read, n + 1)
                    pool.tensor_tensor(mid[:, e, c * BANK:(c + 1) * BANK], x1[c][:, :], act2[c][:, :], ALU.mult).then_inc(mid_done, 1)

                w1_low(1)
                for e in range(E8):
                    middle(e, 0)
                    middle(e, 1)
                    if e + 2 < E8:
                        w1_low(e + 2)
                    pool.wait_ge(m.staged, 48 + 160)
                    pool.tensor_tensor(w2_in[:, e, :], w2_in[:, e, :], m.gate[:, 1, 1, :], ALU.mult).then_inc(w2_gated, 1)
                pool.wait_ge(w2_gated, E8)
                pool.tensor_scalar(w2.hi, w2_in, 1.0, 1.0, ALU.mult, ALU.mult).then_inc(w2_hi, 1)
                pool.wait_ge(w2_hi, 1)
                pool.tensor_tensor(w2.lo, w2_in, as_f32(w2.hi), ALU.subtract).then_inc(w2_ready, 1)


def constants():
    freqs = (np.float32(1.0) / np.float32(10000.0) ** (np.arange(0, D0, 2, dtype=np.float32) / np.float32(D0))).astype(np.float32)
    ang = (np.arange(S, dtype=np.float32)[:, None] * freqs[None, :]).astype(np.float32)
    root = np.float64(D0) ** -0.25
    c, s = (np.cos(ang.astype(np.float64)) * root).T, (np.sin(ang.astype(np.float64)) * root).T
    causal = np.where(np.arange(P)[None, :] > np.arange(P)[:, None], MASK_NEG, 0.0)
    return {
        "cos": np.concatenate([c, c]).astype(np.float32),
        "sin": np.concatenate([-s, s]).astype(np.float32),
        "mask": causal.astype(np.float32),
        "ident": np.eye(P, dtype=np.float32),
    }


INPUTS = ["L0_attn_x", "L0_attn_Wqkv", "L0_attn_Wo", "L0_ffn_w_gate", "L0_ffn_w_up", "L0_ffn_w_down", "L0_c", "L0_wmod",
          "L1_attn_norm_scale", "L1_attn_split_scale", "L1_attn_Wq", "L1_attn_Wk", "L1_attn_Wv", "L1_attn_Wo",
          "L1_ffn_gate_w", "L1_ffn_expert_bias", "L1_ffn_shared_w1", "L1_ffn_shared_w2", "L1_ffn_routed_w1",
          "L1_ffn_routed_w2", "L1_c", "L1_wmod"]


def columns(v):
    return np.asarray(v).reshape(-1, P).T


LAYOUTS = {
    "L0_c": columns, "L1_c": columns,
    "L1_attn_norm_scale": columns, "L1_attn_split_scale": columns,
    "L1_attn_Wq": np.transpose, "L1_attn_Wk": np.transpose, "L1_attn_Wv": np.transpose, "L1_attn_Wo": np.transpose,
    "L1_ffn_expert_bias": lambda v: np.asarray(v).reshape(1, -1),
}


def kernel(**inputs):
    import concourse.bacc as bacc
    from concourse.bass_utils import run_bass_kernel_spmd

    nc = bacc.Bacc("TRN2", target_bir_lowering=False, num_devices=1)
    arrays, aps = {}, {}
    for name, value in [(n, inputs[n]) for n in INPUTS] + list(constants().items()):
        if name in LAYOUTS:
            value = LAYOUTS[name](value)
        value = np.ascontiguousarray(value)
        arrays[name] = value
        aps[name] = nc.dram_tensor(name, value.shape, mybir.dt.from_np(value.dtype), kind="ExternalInput").ap()
    aps["out"] = nc.dram_tensor("out", (1, S, DM), F32, kind="ExternalOutput").ap()
    build(nc, aps)
    result = run_bass_kernel_spmd(nc, [arrays], core_ids=[0])
    return result.results[0]["out"]
```

```python
from contextlib import ExitStack

import numpy as np

import concourse.bass as bass
from concourse import mybir

P = 128
S = 1024
DM = 256
NT = S // P
KD = DM // P
BANK = 512
EPS = 1e-5

H0, KV0, D0 = 16, 4, 128
PER_KV = H0 // KV0
I0 = 1024
H1, G1, D1 = 4, 2, 64
RMS_EPS = 1e-8
NE, FE, TOPK = 7, 128, 2
CAPACITY = S // NE
MASK_NEG = -2.3819763e+38

F32 = mybir.dt.float32
F32R = mybir.dt.float32r
BF16 = mybir.dt.bfloat16
ALU = mybir.AluOpType
ACT = mybir.ActivationFunctionType
AX = mybir.AxisListType


class Split:

    def __init__(self, hi, lo):
        self.hi, self.lo = hi, lo

    def __getitem__(self, index):
        return Split(self.hi[index], self.lo[index])

    def __call__(self, pattern, **sizes):
        return Split(self.hi.rearrange(pattern, **sizes), self.lo.rearrange(pattern, **sizes))


def product(pe, out, left, right, start, stop):
    pe.matmul(out, left.hi, right.hi, start=start, stop=False)
    pe.matmul(out, left.hi, right.lo, start=False, stop=False)
    return pe.matmul(out, left.lo, right.hi, start=False, stop=stop)


def as_f32(ap):
    return ap.bitcast(F32)


class Chain:

    def __init__(self, engine, sem, value=0):
        self.engine, self.sem, self.value = engine, sem, value

    def step(self, ins):
        ins.then_inc(self.sem, 1)
        self.value += 1
        return ins

    def settle(self):
        self.engine.wait_ge(self.sem, self.value)

    def run(self, ins):
        self.step(ins)
        self.settle()
        return ins


def build(nc, a):
    top = ExitStack()
    with top:
        def sb(name, shape, dt=F32, ctx=top):
            return ctx.enter_context(nc.sbuf_tensor(name, shape, dt))

        def split(name, shape, ctx=top):
            return Split(sb(name + "_hi", shape, F32R, ctx)[:], sb(name + "_lo", shape, F32R, ctx)[:])

        x = sb("x", [P, NT, DM])
        ident = sb("ident_sb", [P, P])
        identb = sb("identb_sb", [P, P], BF16)
        maskb = sb("maskb_sb", [P, P], BF16)
        ones = sb("ones", [P, P])
        modcol = sb("modcol", [P, 2, 12])
        gate = sb("gate", [P, 2, 2, DM])
        stats = sb("stats", [P, NT, 6])
        meanvar = sb("meanvar", [P, NT, 2])
        vareps = sb("vareps", [P, NT])
        rstd = sb("rstd", [P, NT])
        tiny = sb("tiny", [P, 2, NT])
        hT = split("hT", [P, KD, S])
        sems = Sems(nc, top)
        staging, staging1 = sb("staging", [P, 6144]), sb("staging1", [P, 2048])
        staged, staged1 = sems("staged"), sems("staged1")
        m = Shared(x, ident, identb, maskb, ones, modcol, gate, stats, meanvar, vareps, rstd, tiny, hT,
                   staging, staging1, staged, staged1)
        modulation(nc, a, m, sems, sb, split)
        attention0(nc, a, m, sems, sb, split)
        ffn0(nc, a, m, sems, sb, split)
        attention1(nc, a, m, sems, sb, split)
        ffn1(nc, a, m, sems, sb, split)


class Shared:
    def __init__(self, x, ident, identb, maskb, ones, modcol, gate, stats, meanvar, vareps, rstd, tiny, hT,
                 staging, staging1, staged, staged1):
        self.x, self.ident, self.identb, self.maskb, self.ones = x, ident, identb, maskb, ones
        self.modcol, self.gate, self.stats, self.meanvar = modcol, gate, stats, meanvar
        self.vareps, self.rstd, self.tiny, self.hT = vareps, rstd, tiny, hT
        self.staging, self.staging1, self.staged, self.staged1 = staging, staging1, staged, staged1


class Sems:

    def __init__(self, nc, ctx):
        self.nc, self.ctx = nc, ctx

    def __call__(self, name):
        return self.ctx.enter_context(self.nc.semaphore(name))


def row_stats(dve, m, chain, sqrt_in, sqrt_out, meanwhile=lambda: None):
    for n in range(NT):
        chain.step(dve.bn_stats(m.stats[:, n, :], m.x[:, n, :]))
    chain.settle()
    for n in range(NT):
        chain.step(dve.bn_aggr(m.meanvar[:, n, :], m.stats[:, n, :]))
    chain.settle()
    dve.tensor_scalar(m.vareps[:, :], m.meanvar[:, :, 1], EPS, None, ALU.add).then_inc(sqrt_in, 1)
    meanwhile()
    dve.wait_ge(sqrt_out, 1)
    chain.run(dve.reciprocal(m.rstd[:, :], m.tiny[:, 0, :]))
    chain.run(dve.tensor_tensor(m.tiny[:, 1, :], m.rstd[:, :], m.rstd[:, :], ALU.mult))
    chain.run(dve.tensor_tensor(m.tiny[:, 1, :], m.tiny[:, 1, :], m.vareps[:, :], ALU.mult))
    chain.run(dve.tensor_scalar(m.tiny[:, 1, :], m.tiny[:, 1, :], -0.5, 1.5, ALU.mult, ALU.add))
    chain.run(dve.tensor_tensor(m.rstd[:, :], m.rstd[:, :], m.tiny[:, 1, :], ALU.mult))


def row_stats_sqrt(act, m, sqrt_in, sqrt_out):
    act.wait_ge(sqrt_in, 1)
    act.activation(m.tiny[:, 0, :], m.vareps[:, :], ACT.Sqrt).then_inc(sqrt_out, 1)


def modulation(nc, a, m, sems, sb, split):
    with ExitStack() as ctx:
        wmod = sb("wmod", [P, 2, KD, 6 * DM], F32, ctx)
        craw = sb("craw", [P, 2, KD], F32, ctx)
        csil = sb("csil", [P, 2, KD], F32, ctx)
        cwide = sb("cwide", [P, 2, KD, P], F32, ctx)
        mask32 = sb("mask32", [P, P], F32, ctx)
        sgn = sb("sgn", [P, 2, 2, DM], F32, ctx)
        p_col = ctx.enter_context(nc.psum_tensor("p_col", [P, 2, 12], F32))
        p_gate = [ctx.enter_context(nc.psum_tensor(f"p_gate{n}", [P, 2, DM], F32)) for n in range(2)]
        c_in, const_in = sems("c_in"), sems("const_in")
        w_in = [sems(f"wmod_in{n}") for n in range(2)]
        c_silu, c_wide, mod_done, mod_read = sems("c_silu"), sems("c_wide"), sems("mod_done"), sems("mod_read")
        chain_sem = sems("mod_chain")
        with nc.Block() as block:
            @block.sync
            def _(sp):
                for n in range(2):
                    sp.dma_start(craw[:, n, :], a[f"L{n}_c"]).then_inc(c_in, 16)
                sp.dma_start(wmod[:, 0, :, :], a["L0_wmod"].rearrange("(k p) n -> p k n", p=P)).then_inc(w_in[0], 16)
                sp.dma_start(wmod[:, 1, :, :], a["L1_wmod"].rearrange("(k p) n -> p k n", p=P)).then_inc(w_in[1], 16)

            @block.scalar
            def _(act):
                act.dma_start(m.x[:, :, :], a["L0_attn_x"].rearrange("o (n p) d -> p (o n) d", p=P)).then_inc(const_in, 16)
                act.dma_start(m.ident[:, :], a["ident"]).then_inc(const_in, 16)
                act.dma_start(mask32[:, :], a["mask"]).then_inc(const_in, 16)
                act.wait_ge(c_in, 32)
                act.activation(csil[:, :, :], craw[:, :, :], ACT.Silu).then_inc(c_silu, 1)

            @block.tensor
            def _(pe):
                pe.wait_ge(c_wide, 1)
                for n in range(2):
                    pe.wait_ge(w_in[n], 16)
                    for j in range(12):
                        for k in range(KD):
                            pe.matmul(p_col[:, n, j:j + 1], wmod[:, n, k, j * P:(j + 1) * P], csil[:, n, k:k + 1],
                                      start=(k == 0), stop=(k == KD - 1))
                    for g, part in enumerate((2, 5)):
                        for k in range(KD):
                            mm = pe.matmul(p_gate[n][:, g, :], cwide[:, n, k, :],
                                           wmod[:, n, k, part * DM:(part + 1) * DM],
                                           start=(k == 0), stop=(k == KD - 1))
                mm.then_inc(mod_done, 1)

            @block.vector
            def _(dve):
                chain = Chain(dve, chain_sem)
                chain.run(dve.memset(m.ones[:, :], 1.0))
                dve.wait_ge(c_silu, 1)
                for n in range(2):
                    for k in range(KD):
                        w = dve.tensor_scalar(cwide[:, n, k, :], m.ones[:, :], csil[:, n, k:k + 1], None, ALU.mult)
                        if n == 1 and k == KD - 1:
                            w.then_inc(c_wide, 1)
                dve.wait_ge(const_in, 48)
                chain.run(dve.tensor_copy(m.identb[:, :], m.ident[:, :]))
                chain.run(dve.tensor_copy(m.maskb[:, :], mask32[:, :]))
                dve.wait_ge(mod_done, 1)
                chain.run(dve.tensor_copy(m.modcol[:, :, :], p_col[:, :, :]))
                for j in (2, 8):
                    chain.run(dve.tensor_scalar(m.modcol[:, :, j:j + 2], m.modcol[:, :, j:j + 2], 1.0, None, ALU.add))
                for n in range(2):
                    g, out = p_gate[n][:, :, :], m.gate[:, n, :, :]
                    chain.run(dve.tensor_scalar(sgn[:, n, :, :], g, 0.0, 2.0, ALU.is_ge, ALU.mult))
                    chain.run(dve.tensor_scalar(sgn[:, n, :, :], sgn[:, n, :, :], -1.0, None, ALU.add))
                    chain.run(dve.tensor_tensor(out, g, sgn[:, n, :, :], ALU.mult))
                    chain.run(dve.tensor_scalar(out, out, 0.25, None, ALU.max))
                    chain.run(dve.tensor_tensor(out, out, sgn[:, n, :, :], ALU.mult))


def transposed_rows(nc, m, sems, sb, layer, part, name, keep=None, more=None):
    with ExitStack() as ctx:
        xn = sb(name + "_xn", [P, NT, DM], F32, ctx)
        h32 = sb(name + "_h32", [P, KD, S], F32, ctx) if keep is None else keep
        banks = [ctx.enter_context(nc.psum_tensor(f"{name}_bank{n}", [P, BANK], F32)) for n in range(4)]
        sqrt_in, sqrt_out = sems(name + "_sqrt_in"), sems(name + "_sqrt_out")
        normed, turned, scaled, chain_sem = (sems(f"{name}_{s}") for s in ("normed", "turned", "scaled", "chain"))
        with nc.Block() as block:
            @block.vector
            def _(dve):
                chain = Chain(dve, chain_sem)
                row_stats(dve, m, chain, sqrt_in, sqrt_out)
                for n in range(NT):
                    dve.tensor_scalar(xn[:, n, :], m.x[:, n, :], m.meanvar[:, n, 0:1], m.rstd[:, n:n + 1],
                                      ALU.subtract, ALU.mult).then_inc(normed, 1)
                for q in range(4 if keep is None else 0):
                    k, cols = q % KD, slice(q // KD * BANK, (q // KD + 1) * BANK)
                    dve.wait_ge(scaled, q + 1)
                    chain.run(dve.tensor_copy(m.hT.hi[:, k, cols], h32[:, k, cols]))
                    chain.run(dve.tensor_tensor(m.hT.lo[:, k, cols], h32[:, k, cols], as_f32(m.hT.hi[:, k, cols]),
                                                ALU.subtract))

            @block.scalar
            def _(act):
                row_stats_sqrt(act, m, sqrt_in, sqrt_out)
                for q in range(4):
                    k, cols = q % KD, slice(q // KD * BANK, (q // KD + 1) * BANK)
                    act.wait_ge(turned, q + 1)
                    act.activation(h32[:, k, cols], banks[q][:, :], ACT.Identity,
                                   scale=m.modcol[:, layer, part + 2 + k:part + 3 + k],
                                   bias=m.modcol[:, layer, part + k:part + k + 1]).then_inc(scaled, 1)

            @block.tensor
            def _(pe):
                for q in range(4):
                    k, half = q % KD, q // KD
                    pe.wait_ge(normed, 4 * (half + 1))
                    for n in range(4):
                        mm = pe.transpose(banks[q][:, n * P:(n + 1) * P], xn[:, 4 * half + n, k * P:(k + 1) * P],
                                          m.ident[:, :])
                    mm.then_inc(turned, 1)


def attention0(nc, a, m, sems, sb, split):
    transposed_rows(nc, m, sems, sb, 0, 0, "ln0")
    UNITS = PER_KV * NT
    TGROUPS = 12
    CH = 2
    with ExitStack() as ctx:
        def buf(name, shape, dt=F32):
            return sb("at0_" + name, shape, dt, ctx)

        def pair(name, shape):
            return split("at0_" + name, shape, ctx)

        cos, sin = buf("cos", [P, S]), buf("sin", [P, S])
        wq_in, wkv_in, wo_in = buf("wq_in", [P, KD, P]), buf("wkv_in", [P, KD, 2, P]), buf("wo_in", [P, DM])
        wq, wkv, wo = pair("wq", [P, KD, P]), pair("wkv", [P, KD, 2, P]), pair("wo", [P, DM])
        kT, v = pair("kT", [P, S]), pair("v", [P, NT, D0])
        k_next = buf("k_next", [P, S])
        q = [pair(f"q{n}", [P, S]) for n in range(2)]
        swapped, plain = buf("swapped", [P, 2, BANK]), buf("plain", [P, 2, BANK])
        probs = buf("probs", [P, 4, S])
        negmax, rowsum, rinv = buf("negmax", [P, 4]), buf("rowsum", [P, 2, NT]), buf("rinv", [P, 2, NT])
        pT = [pair("pT0", [P, 4, BANK]), pair("pT1", [P, 8, BANK])]
        att = pair("att", [P, 2, S])
        p_scores = [ctx.enter_context(nc.psum_tensor(f"at0_scores{n}", [P, S], F32)) for n in range(2)]
        p_turn = [ctx.enter_context(nc.psum_tensor(f"at0_turn{n}", [P, 4, P], F32)) for n in range(2)]
        p_att = ctx.enter_context(nc.psum_tensor("at0_att", [P, BANK], F32))
        p_proj = ctx.enter_context(nc.psum_tensor("at0_proj", [P, BANK], F32))

        def sem(name):
            return sems("at0_" + name)

        tables_in, wq_loaded, wkv_loaded, wo_loaded = (sem(n) for n in ("tables_in", "wq_loaded", "wkv_loaded", "wo_loaded"))
        wq_ready, wkv_ready, wo_ready = sem("wq_ready"), sem("wkv_ready"), sem("wo_ready")
        rope_mm = sem("rope_mm")
        rope_copied = sem("rope_copied")
        rope_done = sem("rope_done")
        keys_ready = sem("keys_ready")
        v_mm, v_hi = sem("v_mm"), sem("v_hi")
        proj_free = sem("proj_free")
        scores_mm, max_done, exp_done = (sem(n) for n in ("scores_mm", "max_done", "exp_done"))
        turn_mm, turn_hi, turn_lo = sem("turn_mm"), sem("turn_hi"), sem("turn_lo")
        inverted = sem("inverted")
        att_mm, att_hi, att_lo = sem("att_mm"), sem("att_hi"), sem("att_lo")
        out_mm = sem("out_mm")
        key_hi, w_hi, wo_gated, rope_turned, rope_sum, query_hi = (sem(n) for n in ("key_hi", "w_hi", "wo_gated", "rope_turned", "rope_sum", "query_hi"))

        JOBS, ROPES = 28, 10

        def tgroups_before(unit):
            h, i = divmod(unit, NT)
            return TGROUPS * h + (i if i < 4 else 4 + 2 * (i - 4))

        def blocks(i):
            return [(0, min(i + 1, 4))] + ([(4, i + 1)] if i >= 4 else [])

        QUERY_UNITS = (0, 1)
        KEY_SLOTS, VALUE_SLOTS = [(1, 3), (2, 3)], [(0, 3), (0, 5)]
        USES = [(h, i, kind) for h in range(PER_KV) for i in range(NT) for kind, here in (
            ("query", i in QUERY_UNITS), ("value", (h, i) in VALUE_SLOTS), ("key", (h, i) in KEY_SLOTS), ("out", i >= 4)) if here]

        def before(h, i, kind, first, last, ropes=False):
            done = USES[:USES.index((h, i, kind))]
            if first:
                done = [u for u in done if not (u[2] == "out" and u[0] == 0)]
            if last:
                done = [u for u in done if u[2] != "key" and not (u[2] == "query" and u[0] == PER_KV - 1)]
            return len([u for u in done if not ropes or u[2] in ("query", "key")])

        def job(g, h, i, kind, first, last):
            return g * JOBS + 4 * first + before(h, i, kind, first, last)

        def rope(h, i, kind, last):
            return 4 + before(h, i, kind, False, last, True)

        def body(g, first, last, slot):
            for s in range(UNITS):
                slot(g, s, first, last)

        def groups(engine, slot):
            body(0, True, False, slot)
            with engine.Fori(1, KV0 - 1) as g:
                body(g, False, False, slot)
            body(KV0 - 1, False, True, slot)

        wqkv = a["L0_attn_Wqkv"].rearrange("(k p) n -> p k n", p=P)
        wo_rows = a["L0_attn_Wo"].rearrange("(h p) n -> p h n", p=P)
        with nc.Block() as block:
            @block.sync
            def _(sp):
                def load_q(head, n):
                    if not (isinstance(n, int) and n == 0):
                        sp.wait_ge(wq_ready, n)
                    sp.dma_start(wq_in[:, :, :], wqkv[:, :, bass.ds(head * P, P)]).then_inc(wq_loaded, 16)

                def load_kv(g):
                    if not (isinstance(g, int) and g == 0):
                        sp.wait_ge(wkv_ready, g)
                    for j in range(2):
                        sp.dma_start(wkv_in[:, :, j, :], wqkv[:, :, bass.ds(g * P + (H0 + j * KV0) * P, P)])\
                          .then_inc(wkv_loaded, 16)

                def load_o(n):
                    if not (isinstance(n, int) and n == 0):
                        sp.wait_ge(wo_ready, n)
                    sp.dma_start(wo_in[:, :].rearrange("p (o d) -> p o d", o=1), wo_rows[:, bass.ds(n, 1), :]).then_inc(wo_loaded, 16)

                load_kv(0)
                load_q(0, 0)
                sp.dma_start(cos[:, :], a["cos"]).then_inc(tables_in, 16)
                sp.dma_start(sin[:, :], a["sin"]).then_inc(tables_in, 16)
                load_q(1, 1)
                for n, name in enumerate(("L0_ffn_w_gate", "L0_ffn_w_up")):
                    sp.dma_start(m.staging[:, n * 2048:(n + 1) * 2048].rearrange("p (k n) -> p k n", k=KD),
                                 a[name].rearrange("(k p) n -> p k n", p=P)).then_inc(m.staged, 16)
                sp.dma_start(m.staging[:, 4096:6144].rearrange("p (c d) -> p c d", d=DM),
                             a["L0_ffn_w_down"].rearrange("(c p) d -> p c d", p=P)).then_inc(m.staged, 16)

                at = 0
                for name in ("L1_attn_Wq", "L1_attn_Wk", "L1_attn_Wv"):
                    w = a[name]
                    n = KD * w.shape[1]
                    sp.dma_start(m.staging1[:, at:at + n].rearrange("p (k n) -> p k n", k=KD), w.rearrange("(k p) n -> p k n", p=P))\
                      .then_inc(m.staged1, 16)
                    at += n
                for half in range(2):
                    sp.dma_start(m.staging1[half * D1:(half + 1) * D1, at:].rearrange("p (h n) -> p h n", h=H1),
                                 a["L1_attn_Wo"].rearrange("(h p) n -> p h n", p=D1)).then_inc(m.staged1, 16)

                def group(g, last, first=False):
                    if not last:
                        load_kv(g + 1)
                    for h in range(PER_KV):
                        n = g * PER_KV + h
                        if not (first and h == 0):
                            load_o(n - 1)
                        if not (last and h >= 2):
                            load_q(n + 2, n + 2)

                group(0, False, True)
                with sp.Fori(1, KV0 - 1) as g:
                    group(g, False)
                group(KV0 - 1, True)
                load_o(H0 - 1)

            @block.tensor
            def _(pe):
                def proj_bank(n):
                    if not (isinstance(n, int) and n == 0):
                        pe.wait_ge(proj_free, n)

                def rope_job(n, w, c):
                    proj_bank(n)
                    for k in range(KD):
                        mm = product(pe, p_proj[:, :], w[:, k, :], m.hT[:, k, c * BANK:(c + 1) * BANK], k == 0, k == KD - 1)
                    mm.then_inc(rope_mm, 1)

                def key_job(n, g, c):
                    pe.wait_ge(wkv_ready, g + 1)
                    rope_job(n, wkv[:, :, 0, :], c)

                def query_job(n, head, c):
                    pe.wait_ge(wq_ready, head + 1)
                    rope_job(n, wq, c)

                def value_job(n, g, c):
                    proj_bank(n)
                    for t in range(4):
                        rows = slice((4 * c + t) * P, (4 * c + t + 1) * P)
                        for k in range(KD):
                            mm = product(pe, p_proj[:, t * P:(t + 1) * P], m.hT[:, k, rows], wkv[:, k, 1, :], k == 0, k == KD - 1)
                    mm.then_inc(v_mm, 1)

                def out_job(n, head, h, j):
                    proj_bank(n)
                    if j == 0:
                        pe.wait_ge(wo_ready, head + 1)
                        pe.wait_ge(att_lo, head * 2 + 2)
                    for t in range(2):
                        rows = slice((2 * j + t) * P, (2 * j + t + 1) * P)
                        mm = product(pe, p_proj[:, t * DM:(t + 1) * DM], att[:, h % 2, rows], wo, True, True)
                    mm.then_inc(out_mm, 1)

                def scores(g, s, first, last):
                    h, i = divmod(s, NT)
                    out, rows, width = p_scores[s % 2], slice(i * P, (i + 1) * P), (i + 1) * P
                    if s in (0, 4):
                        pe.wait_ge(keys_ready, 2 * g + 1 + s // 4)
                    if i == 0:
                        if h == 0:
                            pe.wait_ge(rope_done, g * ROPES + 4)
                        else:
                            pe.wait_ge(rope_done, g * ROPES + rope(h - 1, QUERY_UNITS[1], "query", last) + 1)
                    if not (first and s < 2):
                        pe.wait_ge(exp_done, g * UNITS + s - 1)
                    for c0 in range(0, width, BANK):
                        c1 = min(c0 + BANK, width)
                        qs, ks = q[h % 2][:, rows], kT[:, c0:c1]
                        pe.matmul(out[:, c0:c1], qs.hi, ks.hi, start=True, stop=False)
                        if c1 == width:
                            pe.matmul(out[:, width - P:width], m.identb[:, :], m.maskb[:, :], start=False, stop=False)
                        pe.matmul(out[:, c0:c1], qs.hi, ks.lo, start=False, stop=False)
                        mm = pe.matmul(out[:, c0:c1], qs.lo, ks.hi, start=False, stop=True)
                    mm.then_inc(scores_mm, 1)

                def turn(g, s):
                    h, i = divmod(s, NT)
                    pe.wait_ge(exp_done, g * UNITS + s + 1)
                    for n, (b0, b1) in enumerate(blocks(i)):
                        t = tgroups_before(s) + n
                        if not (isinstance(g, int) and g == 0 and t < 2):
                            pe.wait_ge(turn_lo, g * PER_KV * TGROUPS + t - 1)
                        for b in range(b0, b1):
                            mm = pe.transpose(p_turn[t % 2][:, b - b0, :], probs[:, s % 4, b * P:(b + 1) * P], m.ident[:, :])
                        mm.then_inc(turn_mm, 1)

                def attend(g, h, c, t0, t1):
                    last_tile = 4 * c + 3
                    if t0 == 0:
                        pe.wait_ge(turn_lo, g * PER_KV * TGROUPS + h * TGROUPS + (4 if c == 0 else TGROUPS))
                        pe.wait_ge(proj_free, job(g, *VALUE_SLOTS[c], "value", isinstance(g, int) and g == 0, False) + 1)
                        if not (isinstance(g, int) and g == 0 and h == 0 and c == 0):
                            pe.wait_ge(att_lo, (g * PER_KV + h) * 2 + c)
                    for t in range(t0, t1):
                        c0 = max(0, t - 4 * c) * P
                        mm = product(pe, p_att[:, c0:BANK], v[:, t, :], pT[c][:, t, c0:BANK], t == 0, t == last_tile)
                    if t1 == last_tile + 1:
                        mm.then_inc(att_mm, 1)

                def slot(g, s, first, last):
                    h, i = divmod(s, NT)
                    if (h, i) == VALUE_SLOTS[1]:
                        value_job(job(g, h, i, "value", first, last), g, 1)
                    if s == 0:
                        query_job(job(g, h, i, "query", first, last), g * PER_KV + h + 1, 0)
                    scores(g, s, first, last)
                    if s >= 2:
                        turn(g, s - 2)
                    elif not first:
                        turn(g - 1, UNITS + s - 2)
                    prev = (g, h - 1) if h else (g - 1, PER_KV - 1)
                    if i in (2, 3) and not (first and h == 0):
                        attend(*prev, 1, 4 * (i - 2), 4 * (i - 1))
                    if i == 6:
                        attend(g, h, 0, 0, 4)
                    if i in QUERY_UNITS and s and not (last and h == PER_KV - 1):
                        query_job(job(g, h, i, "query", first, last), g * PER_KV + h + 1, QUERY_UNITS.index(i))
                    if (h, i) in KEY_SLOTS and not last:
                        key_job(job(g, h, i, "key", first, last), g + 1, h - 1)
                    if (h, i) == VALUE_SLOTS[0]:
                        value_job(job(g, h, i, "value", first, last), g, 0)
                    if i >= 4 and not (first and h == 0):
                        out_job(job(g, h, i, "out", first, last), g * PER_KV + h - 1, (h - 1) % 2, i - 4)

                for c in range(CH):
                    key_job(c, 0, c)
                for c in range(CH):
                    query_job(2 + c, 0, c)
                groups(pe, slot)
                g = KV0 - 1
                turn(g, UNITS - 2)
                turn(g, UNITS - 1)
                attend(g, PER_KV - 1, 1, 0, 8)
                for j in range(4):
                    out_job(JOBS * KV0 - 4 + j, H0 - 1, 1, j)

            @block.scalar
            def _(act):
                def copy_rope(g, k):
                    r, n = g * ROPES + k, k % 2
                    act.wait_ge(rope_mm, r + 1)
                    if not (isinstance(r, int) and r < 2):
                        act.wait_ge(rope_done, r - 1)
                    half = P // 2
                    act.activation(swapped[0:half, n, :], p_proj[half:P, :], ACT.Copy)
                    act.activation(swapped[half:P, n, :], p_proj[0:half, :], ACT.Copy).then_inc(rope_copied, 1)

                def keys_hi(g):
                    act.wait_ge(rope_done, g * ROPES + 2)
                    if not (isinstance(g, int) and g == 0):
                        act.wait_ge(scores_mm, g * UNITS)
                    for c in range(CH):
                        act.activation(kT.hi[:, c * BANK:(c + 1) * BANK], k_next[:, c * BANK:(c + 1) * BANK], ACT.Copy).then_inc(key_hi, 1)

                def value_hi(g, c):
                    act.wait_ge(v_mm, g * 2 + c + 1)
                    if not (isinstance(g, int) and g == 0):
                        act.wait_ge(att_mm, g * 2 * PER_KV)
                    act.activation(v.hi[:, 4 * c:4 * c + 4, :], p_proj[:, :].rearrange("p (n d) -> p n d", n=4), ACT.Copy)\
                       .then_inc(v_hi, 1)

                def probs_hi(g, s):
                    h, i = divmod(s, NT)
                    c = i // 4
                    if i % 4 == 0 and not (isinstance(g, int) and g == 0 and h == 0):
                        act.wait_ge(att_mm, (g * PER_KV + h) * 2 - 1 + c)
                    for n, (b0, b1) in enumerate(blocks(i)):
                        t = tgroups_before(s) + n
                        act.wait_ge(turn_mm, g * PER_KV * TGROUPS + t + 1)
                        act.activation(pT[c].hi[:, b0:b1, (i % 4) * P:(i % 4 + 1) * P], p_turn[t % 2][:, 0:b1 - b0, :], ACT.Copy)\
                           .then_inc(turn_hi, 1)

                def exp(g, s, first):
                    i = s % NT
                    width = (i + 1) * P
                    act.wait_ge(max_done, g * UNITS + s + 1)
                    if not (first and s < 4):
                        before = tgroups_before(s - 3) if s >= 3 else tgroups_before(UNITS + s - 3) - PER_KV * TGROUPS
                        act.wait_ge(turn_mm, g * PER_KV * TGROUPS + before)
                    act.activation(probs[:, s % 4, 0:width], p_scores[s % 2][:, 0:width], ACT.Exp,
                                   bias=negmax[:, s % 4:s % 4 + 1], accum_out=rowsum[:, s // NT % 2, i:i + 1])\
                       .then_inc(exp_done, 1)

                def attended_hi(g, h, c):
                    n = (g * PER_KV + h) * 2 + c
                    act.wait_ge(att_mm, n + 1)
                    if c == 0 and not (isinstance(g, int) and g == 0 and h < 2):
                        act.wait_ge(out_mm, (g * PER_KV + h - 1) * 4)
                    act.activation(att.hi[:, h % 2, c * BANK:(c + 1) * BANK], p_att[:, :], ACT.Copy).then_inc(att_hi, 1)

                def slot(g, s, first, last):
                    h, i = divmod(s, NT)
                    if (h, i) == VALUE_SLOTS[1]:
                        value_hi(g, 1)
                    if s == 0:
                        copy_rope(g, rope(h, i, "query", last))
                    if s >= 2:
                        probs_hi(g, s - 2)
                    elif not first:
                        probs_hi(g - 1, UNITS + s - 2)
                    if s == UNITS - 1 and not last:
                        keys_hi(g + 1)
                    exp(g, s, first)
                    if i == 3 and not (first and h == 0):
                        attended_hi(*((g, h - 1) if h else (g - 1, PER_KV - 1)), 1)
                    if i == 6:
                        attended_hi(g, h, 0)
                    if i in QUERY_UNITS and s and not (last and h == PER_KV - 1):
                        copy_rope(g, rope(h, i, "query", last))
                    if (h, i) in KEY_SLOTS and not last:
                        copy_rope(g, rope(h, i, "key", last))
                    if (h, i) == VALUE_SLOTS[0]:
                        value_hi(g, 0)

                for r in range(4):
                    copy_rope(0, r)
                keys_hi(0)
                groups(act, slot)
                g = KV0 - 1
                probs_hi(g, UNITS - 2)
                probs_hi(g, UNITS - 1)
                attended_hi(g, PER_KV - 1, 1)

            @block.vector
            def _(dve):
                def keys_lo(g, c):
                    cols = slice(c * BANK, (c + 1) * BANK)
                    dve.wait_ge(key_hi, 2 * g + c + 1)
                    dve.tensor_tensor(kT.lo[:, cols], k_next[:, cols], as_f32(kT.hi[:, cols]), ALU.subtract).then_inc(keys_ready, 1)

                def value_lo(g, c):
                    dve.wait_ge(v_hi, g * 2 + c + 1)
                    out = v[:, 4 * c:4 * c + 4, :]
                    dve.tensor_tensor(out.lo, p_proj[:, :].rearrange("p (n d) -> p n d", n=4), as_f32(out.hi), ALU.subtract)\
                       .then_inc(proj_free, 1)

                def cos_rope(g, k, c):
                    r = g * ROPES + k
                    dve.wait_ge(rope_copied, r + 1)
                    if not (isinstance(r, int) and r < 2):
                        dve.wait_ge(rope_done, r - 1)
                    dve.tensor_tensor(plain[:, k % 2, :], p_proj[:, :], cos[:, c * BANK:(c + 1) * BANK], ALU.mult).then_inc(proj_free, 1)

                def maximum(g, s):
                    i = s % NT
                    dve.wait_ge(scores_mm, g * UNITS + s + 1)
                    dve.tensor_reduce(negmax[:, s % 4:s % 4 + 1], p_scores[s % 2][:, 0:(i + 1) * P], AX.X, ALU.max, negate=True)\
                       .then_inc(max_done, 1)

                def inverse_sums(g, h):
                    dve.wait_ge(exp_done, g * UNITS + h * NT + NT)
                    dve.reciprocal(rinv[:, h % 2, :], rowsum[:, h % 2, :]).then_inc(inverted, 1)

                def probs_lo(g, s):
                    h, i = divmod(s, NT)
                    for n, (b0, b1) in enumerate(blocks(i)):
                        t = tgroups_before(s) + n
                        out = pT[i // 4][:, b0:b1, (i % 4) * P:(i % 4 + 1) * P]
                        dve.wait_ge(turn_hi, g * PER_KV * TGROUPS + t + 1)
                        dve.tensor_tensor(out.lo, p_turn[t % 2][:, 0:b1 - b0, :], as_f32(out.hi), ALU.subtract).then_inc(turn_lo, 1)

                def attended_lo(g, h, c):
                    out = att[:, h % 2, c * BANK:(c + 1) * BANK]
                    dve.wait_ge(att_hi, (g * PER_KV + h) * 2 + c + 1)
                    dve.tensor_tensor(out.lo, p_att[:, :], as_f32(out.hi), ALU.subtract).then_inc(att_lo, 1)

                def add_out(head, h, j):
                    dve.wait_ge(out_mm, head * 4 + j + 1)
                    if j == 0:
                        dve.wait_ge(inverted, head + 1)
                    for t in range(2):
                        rows = m.x[:, 2 * j + t, :]
                        ins = dve.scalar_tensor_tensor(out=rows, in0=p_proj[:, t * DM:(t + 1) * DM], scalar=rinv[:, h % 2, 2 * j + t:2 * j + t + 1],
                                                       in1=rows, op0=ALU.mult, op1=ALU.add)
                    ins.then_inc(proj_free, 1)

                def slot(g, s, first, last):
                    h, i = divmod(s, NT)
                    if (h, i) == VALUE_SLOTS[1]:
                        value_lo(g, 1)
                    if s == 0:
                        cos_rope(g, rope(h, i, "query", last), 0)
                    maximum(g, s)
                    prev = (g, h - 1) if h else (g - 1, PER_KV - 1)
                    if i == 2 and not (first and h == 0):
                        inverse_sums(*prev)
                    if s >= 2:
                        probs_lo(g, s - 2)
                    elif not first:
                        probs_lo(g - 1, UNITS + s - 2)
                    if i == 3 and not (first and h == 0):
                        attended_lo(*prev, 1)
                    if i == 6:
                        attended_lo(g, h, 0)
                    if i in QUERY_UNITS and s and not (last and h == PER_KV - 1):
                        cos_rope(g, rope(h, i, "query", last), QUERY_UNITS.index(i))
                    if (h, i) in KEY_SLOTS and not last:
                        cos_rope(g, rope(h, i, "key", last), h - 1)
                    if (h, i) == VALUE_SLOTS[0]:
                        value_lo(g, 0)
                    if i >= 4 and not (first and h == 0):
                        add_out(g * PER_KV + h - 1, h - 1, i - 4)
                    if s == UNITS - 1 and not last:
                        for c in range(CH):
                            keys_lo(g + 1, c)

                dve.wait_ge(tables_in, 32)
                for r in range(4):
                    cos_rope(0, r, r % 2)
                for c in range(CH):
                    keys_lo(0, c)
                groups(dve, slot)
                g = KV0 - 1
                inverse_sums(g, PER_KV - 1)
                probs_lo(g, UNITS - 2)
                probs_lo(g, UNITS - 1)
                attended_lo(g, PER_KV - 1, 1)
                for j in range(4):
                    add_out(H0 - 1, PER_KV - 1, j)

            @block.gpsimd
            def _(pool):
                def alone():
                    pool.nop(nofuse=True)

                def turn_sum(rk, n, c, dst):
                    r, b = rk[0] * ROPES + rk[1], rk[1] % 2
                    cols = slice(c * BANK, (c + 1) * BANK)
                    pool.wait_ge(rope_copied, r + 1)
                    pool.tensor_tensor(swapped[:, b, :], swapped[:, b, :], sin[:, cols], ALU.mult).then_inc(rope_turned, 1)
                    pool.wait_ge(proj_free, n + 1)
                    pool.wait_ge(rope_turned, r + 1)
                    return pool.tensor_tensor(dst, plain[:, b, :], swapped[:, b, :], ALU.add)

                def key_turn(r, n, g, c):
                    if not (isinstance(g, int) and g == 0):
                        pool.wait_ge(keys_ready, 2 * g)
                    turn_sum(r, n, c, k_next[:, c * BANK:(c + 1) * BANK]).then_inc(rope_done, 1)

                def query_turn(r, n, queries, g, h, c, free=False):
                    turned = plain[:, r[1] % 2, :]
                    turn_sum(r, n, c, turned).then_inc(rope_sum, 1)
                    out = q[h % 2][:, c * BANK:(c + 1) * BANK]
                    if not free:
                        pool.wait_ge(scores_mm, g * UNITS + (h - 1) * NT)
                    pool.wait_ge(rope_sum, queries + 1)
                    alone()
                    pool.tensor_scalar(out.hi, turned, 1.0, 1.0, ALU.mult, ALU.mult).then_inc(query_hi, 1)
                    pool.wait_ge(query_hi, queries + 1)
                    pool.tensor_tensor(out.lo, turned, as_f32(out.hi), ALU.subtract).then_inc(rope_done, 1)

                def split_weights(n, staged, out, ready):
                    alone()
                    pool.tensor_scalar(out.hi, staged, 1.0, 1.0, ALU.mult, ALU.mult).then_inc(w_hi, 1)
                    pool.wait_ge(w_hi, n + 1)
                    pool.tensor_tensor(out.lo, staged, as_f32(out.hi), ALU.subtract).then_inc(ready, 1)

                def split_q(n, head, projected):
                    pool.wait_ge(wq_loaded, head * 16 + 16)
                    if projected is not None:
                        pool.wait_ge(rope_mm, projected)
                    split_weights(n, wq_in[:, :, :], wq, wq_ready)

                def split_kv(n, g):
                    pool.wait_ge(wkv_loaded, g * 32 + 32)
                    if not (isinstance(g, int) and g == 0):
                        pool.wait_ge(v_mm, g * 2)
                    split_weights(n, wkv_in[:, :, :, :], wkv, wkv_ready)

                def split_o(n, head):
                    pool.wait_ge(wo_loaded, head * 16 + 16)
                    pool.tensor_tensor(wo_in[:, :], wo_in[:, :], m.gate[:, 0, 0, :], ALU.mult).then_inc(wo_gated, 1)
                    if not (isinstance(head, int) and head == 0):
                        pool.wait_ge(out_mm, head * 4)
                    pool.wait_ge(wo_gated, head + 1)
                    split_weights(n, wo_in[:, :], wo, wo_ready)

                def slot(g, s, first, last):
                    h, i = divmod(s, NT)
                    head = g * PER_KV + h
                    if i in QUERY_UNITS and not (last and h == PER_KV - 1):
                        query_turn((g, rope(h, i, "query", last)), job(g, h, i, "query", first, last), g * 8 + 2 + 2 * h + QUERY_UNITS.index(i),
                                   g + (h + 1) // PER_KV, (h + 1) % PER_KV, QUERY_UNITS.index(i), first and h == 0)
                    if (h, i) in KEY_SLOTS and not last:
                        key_turn((g, rope(h, i, "key", last)), job(g, h, i, "key", first, last), g + 1, h - 1)
                    if i == 0 and not (first and h == 0):
                        split_o(splits(g, h, 0, first, last), head - 1)
                    if i == 2 and not (last and h >= 2):
                        split_q(splits(g, h, 1, first, last), head + 2, g * ROPES + rope(h, QUERY_UNITS[1], "query", last) + 1)
                    if (h, i) == VALUE_SLOTS[1] and not last:
                        split_kv(splits(g, h, 2, first, last), g + 1)

                def splits(g, h, kind, first, last):
                    order = [(hh, kk) for hh in range(PER_KV) for kk in range(3)
                             if not (kk == 0 and first and hh == 0) and not (kk == 1 and last and hh >= 2)
                             and not (kk == 2 and (hh != 0 or last))]
                    return (3 if first else g * 9 + 2) + order.index((h, kind))

                split_kv(0, 0)
                split_q(1, 0, None)
                pool.wait_ge(tables_in, 32)
                for c in range(CH):
                    key_turn((0, c), c, 0, c)
                for c in range(CH):
                    query_turn((0, 2 + c), 2 + c, c, 0, 0, c, True)
                split_q(2, 1, 4)
                groups(pool, slot)
                split_o(KV0 * 9 - 1, H0 - 1)


def ffn0(nc, a, m, sems, sb, split):
    with ExitStack() as ctx:
        def buf(name, shape, dt=F32):
            return sb("ff0_" + name, shape, dt, ctx)

        def pair(name, shape):
            return split("ff0_" + name, shape, ctx)

        def sem(name):
            return sems("ff0_" + name)

        wg_in, wu_in, wd_in = (m.staging[:, n * 2048:(n + 1) * 2048] for n in range(3))
        wg, wu, wd = pair("wg", [P, KD, I0]), pair("wu", [P, KD, I0]), pair("wd", [P, I0 // P, DM])
        xn = [buf(f"xn{n}", [P, DM]) for n in range(2)]
        h32 = buf("h32", [P, KD, P])
        hx = [pair(f"hx{n}", [P, KD, P]) for n in range(2)]
        sg, absh = buf("sg", [P, I0]), buf("absh", [P, I0])
        h = [buf(f"h{n}", [P, I0]) for n in range(2)]
        cx, cy, cz, cs, ct = (buf(n, [P, 2, I0 // 4], BF16) for n in ("cx", "cy", "cz", "cs", "ct"))
        wins = buf("wins", [P, 4, I0 // 4], BF16)
        hsT = pair("hsT", [P, I0 // P, P])
        p_gate, p_up = (ctx.enter_context(nc.psum_tensor(f"ff0_{n}", [P, I0], F32)) for n in ("gate", "up"))
        p_turn = [ctx.enter_context(nc.psum_tensor(f"ff0_turn{n}", [P, 4, P], F32)) for n in range(2)]
        p_x = ctx.enter_context(nc.psum_tensor("ff0_x", [P, BANK], F32))
        p_y = ctx.enter_context(nc.psum_tensor("ff0_y", [P, BANK], F32))
        sqrt_in, sqrt_out, chain_sem = sem("sqrt_in"), sem("sqrt_out"), sem("chain")
        w_hi, wg_ready, wu_ready, wu_ready_pool, wd_gated, wd_hi, wd_ready = (sem(n) for n in ("w_hi", "wg_ready", "wu_ready", "wu_ready_pool", "wd_gated", "wd_hi", "wd_ready"))
        normed, x_mm, h32_done, hx_hi, hx_ready = (sem(n) for n in ("normed", "x_mm", "h32_done", "hx_hi", "hx_ready"))
        gate_mm, up_mm, silu_done, mul_done, abs_done = (sem(n) for n in ("gate_mm", "up_mm", "silu_done", "mul_done", "abs_done"))
        compared, summed, won, sparse = (sem(n) for n in ("compared", "summed", "won", "sparse"))
        turn_mm, turn_hi, turn_lo, down_mm, added = (sem(n) for n in ("turn_mm", "turn_hi", "turn_lo", "down_mm", "added"))

        OPEN = 1

        def zero(t):
            return isinstance(t, int) and t == 0

        def tiles(engine, step):
            step(0, 0)
            step(1, 1)
            with engine.Fori(0, (NT - 4) // 2) as r:
                step(r * 2 + 2, 0)
                step(r * 2 + 3, 1)
            step(NT - 2, 0)
            step(NT - 1, 1)

        def ahead(t):
            return not isinstance(t, int) or t + 2 < NT

        def behind(t, n):
            return not isinstance(t, int) or t >= n

        with nc.Block() as block:
            @block.tensor
            def _(pe):
                def turn_x(t, b):
                    pe.wait_ge(normed, t + 1)
                    if not zero(t):
                        pe.wait_ge(h32_done, t)
                    for k in range(KD):
                        mm = pe.transpose(p_x[:, k * P:(k + 1) * P], xn[b][:, k * P:(k + 1) * P], m.ident[:, :])
                    mm.then_inc(x_mm, 1)

                def wide(t, b, w, out, free, done):
                    if not zero(t):
                        pe.wait_ge(free, t)
                    for c in range(I0 // BANK):
                        cols = slice(c * BANK, (c + 1) * BANK)
                        for k in range(KD):
                            mm = product(pe, out[:, cols], hx[b][:, k, :], w[:, k, cols], k == 0, k == KD - 1)
                    mm.then_inc(done, 1)

                def turn_h(t, b):
                    pe.wait_ge(sparse, t * 4 + 4)
                    pe.wait_ge(turn_lo, OPEN + t * 2)
                    for n in range(2):
                        for j in range(4):
                            c = 4 * n + j
                            mm = pe.transpose(p_turn[n][:, j, :], h[b][:, c * P:(c + 1) * P], m.ident[:, :])
                        mm.then_inc(turn_mm, 1)

                def down(t):
                    if zero(t):
                        pe.wait_ge(wd_ready, 1)
                    pe.wait_ge(added, OPEN + t)
                    for c in range(I0 // P):
                        if c % 4 == 0:
                            pe.wait_ge(turn_lo, OPEN + t * 2 + 1 + c // 4)
                        mm = product(pe, p_y[:, 0:DM], hsT[:, c, :], wd[:, c, :], c == 0, c == I0 // P - 1)
                    mm.then_inc(down_mm, 1)

                def step(t, b):
                    pe.wait_ge(hx_ready, t + 1)
                    if zero(t):
                        pe.wait_ge(wg_ready, KD)
                    wide(t, b, wg, p_gate, silu_done, gate_mm)
                    if behind(t, 2):
                        down(t - 2)
                    if zero(t):
                        pe.wait_ge(wu_ready, 1)
                        pe.wait_ge(wu_ready_pool, 1)
                    wide(t, b, wu, p_up, mul_done, up_mm)
                    if behind(t, 1):
                        turn_h(t - 1, 1 - b)
                    if ahead(t):
                        turn_x(t + 2, b)

                pe.sem_inc(turn_mm, OPEN)
                pe.sem_inc(down_mm, OPEN)
                turn_x(0, 0)
                turn_x(1, 1)
                tiles(pe, step)
                down(NT - 2)
                turn_h(NT - 1, 1)
                down(NT - 1)

            @block.scalar
            def _(act):
                for n, (w, w_in) in enumerate(((wg, wg_in), (wu, wu_in))):
                    act.wait_ge(m.staged, 16 * (n + 1))
                    for k in range(KD):
                        act.activation(w.hi[:, k, :], w_in[:, k * I0:(k + 1) * I0], ACT.Copy).then_inc(w_hi, 1)
                    if n == 0:
                        row_stats_sqrt(act, m, sqrt_in, sqrt_out)

                def scale_shift(t):
                    act.wait_ge(x_mm, t + 1)
                    if not zero(t):
                        act.wait_ge(hx_ready, t)
                    for k in range(KD):
                        ins = act.activation(h32[:, k, :], p_x[:, k * P:(k + 1) * P], ACT.Identity,
                                             scale=m.modcol[:, 0, 8 + k:9 + k], bias=m.modcol[:, 0, 6 + k:7 + k])
                    ins.then_inc(h32_done, 1)

                def silu(t):
                    act.wait_ge(gate_mm, t + 1)
                    if not zero(t):
                        act.wait_ge(mul_done, t)
                    act.activation(sg[:, :], p_gate[:, :], ACT.Silu).then_inc(silu_done, 1)

                def turned_hi(t):
                    for n in range(2):
                        act.wait_ge(turn_mm, OPEN + t * 2 + n + 1)
                        if n == 0:
                            act.wait_ge(down_mm, OPEN + t)
                        act.activation(hsT.hi[:, 4 * n:4 * n + 4, :], p_turn[n][:, :, :], ACT.Copy).then_inc(turn_hi, 1)

                def magnitude(t, b):
                    act.wait_ge(mul_done, t + 1)
                    if not zero(t):
                        act.wait_ge(compared, t * 3)
                    act.activation(absh[:, :], h[b][:, :], ACT.Abs).then_inc(abs_done, 1)

                def step(t, b):
                    silu(t)
                    if behind(t, 1):
                        turned_hi(t - 1)
                    magnitude(t, b)
                    if ahead(t):
                        scale_shift(t + 2)

                scale_shift(0)
                scale_shift(1)
                tiles(act, step)
                turned_hi(NT - 1)

            @block.vector
            def _(dve):
                dve.sem_inc(turn_lo, OPEN)
                dve.sem_inc(added, OPEN)
                chain = Chain(dve, chain_sem)

                def split_low(n, w, w_in, k, ready):
                    dve.wait_ge(w_hi, KD * n + k + 1)
                    dve.tensor_tensor(w.lo[:, k, :], w_in[:, k * I0:(k + 1) * I0], as_f32(w.hi[:, k, :]), ALU.subtract).then_inc(ready, 1)

                def gate_low():
                    for k in range(KD):
                        split_low(0, wg, wg_in, k, wg_ready)

                row_stats(dve, m, chain, sqrt_in, sqrt_out, gate_low)

                def norm(t, b):
                    if not (isinstance(t, int) and t < 2):
                        dve.wait_ge(x_mm, t - 1)
                    dve.tensor_scalar(xn[b][:, :], m.x[:, bass.ds(t, 1), :], m.meanvar[:, bass.ds(t, 1), 0], m.rstd[:, bass.ds(t, 1)],
                                      ALU.subtract, ALU.mult).then_inc(normed, 1)

                def multiply(t, b):
                    dve.wait_ge(silu_done, t + 1)
                    dve.wait_ge(up_mm, t + 1)
                    if not (isinstance(t, int) and t < 2):
                        dve.wait_ge(turn_mm, OPEN + t * 2 - 2)
                    dve.tensor_tensor(h[b][:, :], sg[:, :], p_up[:, :], ALU.mult).then_inc(mul_done, 1)

                def sparsify(t, b):
                    four = absh[:, :].rearrange("p (g e) -> p g e", e=4)

                    def by_group(plane):
                        return plane[:, :, :].rearrange("p e g -> p g e")

                    dve.wait_ge(abs_done, t + 1)
                    dve.tensor_tensor(by_group(cx), four[:, :, 0:2], four[:, :, 2:4], ALU.is_ge).then_inc(compared, 1)
                    dve.tensor_tensor(by_group(cy), four[:, :, 0:2], four[:, :, 3:1:-1], ALU.is_ge).then_inc(compared, 1)
                    dve.tensor_tensor(by_group(cz), four[:, :, 0:4:2], four[:, :, 1:4:2], ALU.is_ge).then_inc(compared, 1)
                    dve.wait_ge(compared, t * 3 + 3)
                    dve.tensor_tensor(cs[:, :, :], cx[:, :, :], cy[:, :, :], ALU.add).then_inc(summed, 1)
                    dve.tensor_tensor(ct[:, :, :], cx[:, :, :], cy[:, 1::-1, :], ALU.add).then_inc(summed, 1)
                    dve.wait_ge(summed, t * 2 + 2)
                    dve.tensor_tensor(wins[:, 0, :], cs[:, 0, :], cz[:, 0, :], ALU.add).then_inc(won, 1)
                    dve.tensor_tensor(wins[:, 1, :], cs[:, 1, :], cz[:, 0, :], ALU.subtract).then_inc(won, 1)
                    dve.tensor_tensor(wins[:, 2, :], cz[:, 1, :], ct[:, 0, :], ALU.subtract).then_inc(won, 1)
                    dve.tensor_tensor(wins[:, 3, :], ct[:, 1, :], cz[:, 1, :], ALU.add).then_inc(won, 1)
                    dve.wait_ge(won, t * 4 + 4)
                    kept = h[b][:, :].rearrange("p (g e) -> p g e", e=4)
                    for e, (test, bound) in enumerate(((ALU.is_ge, 2.0), (ALU.is_ge, 1.0), (ALU.is_ge, 0.0), (ALU.is_le, 1.0))):
                        dve.scalar_tensor_tensor(out=kept[:, :, e], in0=wins[:, e, :], scalar=bound, in1=kept[:, :, e],
                                                 op0=test, op1=ALU.mult).then_inc(sparse, 1)

                def turned_lo(t):
                    for n in range(2):
                        out = hsT[:, 4 * n:4 * n + 4, :]
                        dve.wait_ge(turn_hi, t * 2 + n + 1)
                        dve.tensor_tensor(out.lo, p_turn[n][:, :, :], as_f32(out.hi), ALU.subtract).then_inc(turn_lo, 1)

                def add(t):
                    dve.wait_ge(down_mm, OPEN + t + 1)
                    rows = m.x[:, bass.ds(t, 1), :].rearrange("p o d -> p (o d)")
                    dve.tensor_tensor(rows, p_y[:, 0:DM], rows, ALU.add).then_inc(added, 1)

                def step(t, b):
                    if ahead(t):
                        norm(t + 2, b)
                    if behind(t, 2):
                        add(t - 2)
                    multiply(t, b)
                    if behind(t, 1):
                        turned_lo(t - 1)
                    sparsify(t, b)

                norm(0, 0)
                norm(1, 1)
                split_low(1, wu, wu_in, 0, wu_ready)
                tiles(dve, step)
                add(NT - 2)
                turned_lo(NT - 1)
                add(NT - 1)

            @block.gpsimd
            def _(pool):
                def split_x(t, b):
                    pool.wait_ge(h32_done, t + 1)
                    if not (isinstance(t, int) and t < 2):
                        pool.wait_ge(up_mm, t - 1)
                    pool.nop(nofuse=True)
                    pool.tensor_scalar(hx[b].hi[:, :, :], h32[:, :, :], 1.0, 1.0, ALU.mult, ALU.mult).then_inc(hx_hi, 1)
                    pool.wait_ge(hx_hi, t + 1)
                    pool.tensor_tensor(hx[b].lo[:, :, :], h32[:, :, :], as_f32(hx[b].hi[:, :, :]), ALU.subtract).then_inc(hx_ready, 1)

                pool.wait_ge(w_hi, 2 * KD)
                pool.tensor_tensor(wu.lo[:, 1, :], wu_in[:, I0:], as_f32(wu.hi[:, 1, :]), ALU.subtract).then_inc(wu_ready_pool, 1)
                split_x(0, 0)
                split_x(1, 1)
                pool.wait_ge(m.staged, 48)
                for c in range(I0 // P):
                    rows = wd_in[:, c * DM:(c + 1) * DM]
                    pool.tensor_tensor(rows, rows, m.gate[:, 0, 1, :], ALU.mult).then_inc(wd_gated, 1)
                pool.wait_ge(wd_gated, I0 // P)
                flat = wd("p c d -> p (c d)")
                pool.tensor_scalar(flat.hi, wd_in, 1.0, 1.0, ALU.mult, ALU.mult).then_inc(wd_hi, 1)
                pool.wait_ge(wd_hi, 1)
                pool.tensor_tensor(flat.lo, wd_in, as_f32(flat.hi), ALU.subtract).then_inc(wd_ready, 1)

                with pool.Fori(0, NT // 2 - 1) as r:
                    split_x(r * 2 + 2, 0)
                    split_x(r * 2 + 3, 1)


def attention1(nc, a, m, sems, sb, split):
    HS = H1 * NT
    ctx = ExitStack()
    with ctx:
        def buf(name, shape, dt=F32, c=ctx):
            return sb("at1_" + name, shape, dt, c)

        def sem(name):
            return sems("at1_" + name)

        h32 = buf("h32", [P, KD, S])
        transposed_rows(nc, m, sems, sb, 1, 0, "ln2", keep=h32)
        gT = m.hT
        wq, wk, wv = (split(f"at1_{n}", [P, KD, w], ctx) for n, w in (("wq", H1 * D1), ("wk", G1 * D1), ("wv", G1 * D1)))
        wo = split("at1_wo", [P, H1, DM], ctx)
        gated_ident = buf("gated_ident", [P, KD, P])
        norm_col = buf("norm_col", [P, 3, KD])
        wo_in = m.staging1[:, 1024:2048].rearrange("p (h n) -> p h n", h=H1)
        q = [buf(f"q{n}", [P, S], F32R) for n in range(2)]
        khi, klo = ([buf(f"{n}{g}", [P, S], F32R) for g in range(G1)] for n in ("khi", "klo"))
        v = [buf(f"v{g}", [P, NT, 2, D1], F32R) for g in range(G1)]
        staging = m.staging1
        wq_in = staging[:, 0:512].rearrange("p (k n) -> p k n", k=KD)
        wk_in = staging[:, 512:768].rearrange("p (k n) -> p k n", k=KD)
        wv_in = staging[:, 768:1024].rearrange("p (k n) -> p k n", k=KD)

        with ExitStack() as c1:
            square = buf("square", [P, KD, S], F32, c1)
            inv = buf("inv", [P, S], F32, c1)
            p_sum = c1.enter_context(nc.psum_tensor("at1_sum", [P, S], F32))
            small_in, squared, sum_mm, rooted, chain_sem, w_hi, ready = (
                sem(n) for n in ("small_in", "squared", "sum_mm", "rooted", "chain", "w_hi", "w_ready"))
            with nc.Block() as block:
                @block.sync
                def _(sp):
                    for n in range(2):
                        sp.dma_start(norm_col[:, n, :], a[("L1_attn_norm_scale", "L1_attn_split_scale")[n]]).then_inc(small_in, 16)
                    w1 = m.staging[:, 0:4096].rearrange("p (e k n) -> p e k n", e=8, k=KD)
                    w2 = m.staging[:, 4096:6144].rearrange("p (e n) -> p e n", e=8)
                    for e in range(8):
                        src1 = a["L1_ffn_shared_w1"][0] if e == 0 else a["L1_ffn_routed_w1"][e - 1]
                        sp.dma_start(w1[:, e, :, :], src1.rearrange("(k p) n -> p k n", p=P)).then_inc(m.staged, 16)
                    sp.dma_start(w2[:, 0, :], a["L1_ffn_shared_w2"][0]).then_inc(m.staged, 16)
                    sp.dma_start(w2[:, 1:8, :], a["L1_ffn_routed_w2"].rearrange("e p n -> p e n")).then_inc(m.staged, 16)

                @block.scalar
                def _(act):
                    for k in range(KD):
                        act.activation(square[:, k, :], h32[:, k, :], ACT.Square).then_inc(squared, 1)
                    act.wait_ge(m.staged1, 80)
                    for w, w_in in ((wq, wq_in), (wk, wk_in), (wv, wv_in)):
                        act.activation(w.hi, w_in, ACT.Copy).then_inc(w_hi, 1)
                    for half in range(2):
                        act.wait_ge(sum_mm, half + 1)
                        act.activation(inv[:, half * BANK:(half + 1) * BANK], p_sum[:, half * BANK:(half + 1) * BANK],
                                       ACT.Sqrt, scale=1.0 / DM).then_inc(rooted, 1)

                @block.tensor
                def _(pe):
                    pe.wait_ge(squared, KD)
                    for half in range(2):
                        cols = slice(half * BANK, (half + 1) * BANK)
                        for k in range(KD):
                            mm = pe.matmul(p_sum[:, cols], m.ones[:, :], square[:, k, cols], start=(k == 0), stop=(k == KD - 1))
                        mm.then_inc(sum_mm, 1)

                @block.vector
                def _(dve):
                    chain = Chain(dve, chain_sem)
                    dve.wait_ge(small_in, 32)
                    chain.run(dve.tensor_tensor(norm_col[:, 2, :], norm_col[:, 0, :], norm_col[:, 1, :], ALU.mult))
                    for k in range(KD):
                        chain.step(dve.tensor_tensor(gated_ident[:, k, :], m.ident[:, :], m.gate[:, 1, 0, k * P:(k + 1) * P], ALU.mult))
                    for half in range(2):
                        cols = slice(half * BANK, (half + 1) * BANK)
                        part = inv[:, cols]
                        dve.wait_ge(rooted, half + 1)
                        chain.run(dve.tensor_scalar(part, part, RMS_EPS, None, ALU.add))
                        chain.run(dve.reciprocal(part, part))
                        for k in range(KD):
                            chain.run(dve.scalar_tensor_tensor(out=square[:, k, cols], in0=h32[:, k, cols], scalar=norm_col[:, 2, k:k + 1],
                                                               in1=part, op0=ALU.mult, op1=ALU.mult))
                            chain.run(dve.tensor_copy(gT.hi[:, k, cols], square[:, k, cols]))
                            chain.run(dve.tensor_tensor(gT.lo[:, k, cols], square[:, k, cols], as_f32(gT.hi[:, k, cols]), ALU.subtract))
                    for n, (w, w_in) in enumerate(((wq, wq_in), (wk, wk_in), (wv, wv_in))):
                        dve.wait_ge(w_hi, n + 1)
                        dve.tensor_tensor(w.lo, w_in, as_f32(w.hi), ALU.subtract).then_inc(ready, 1)

                @block.gpsimd
                def _(pool):
                    chain = Chain(pool, sem("pool_chain"))
                    pool.wait_ge(m.staged1, 80)
                    for h in range(H1):
                        chain.step(pool.tensor_tensor(wo_in[:, h, :], wo_in[:, h, :], m.gate[:, 1, 0, :], ALU.mult))
                    chain.settle()
                    chain.run(pool.tensor_scalar(wo.hi, wo_in[:, :, :], 1.0, 1.0, ALU.mult, ALU.mult))
                    chain.run(pool.tensor_tensor(wo.lo, wo_in[:, :, :], as_f32(wo.hi), ALU.subtract))

        more_probs = buf("probs", [P, 2, S])
        probs = [staging[:, n * S:(n + 1) * S] for n in range(2)] + [more_probs[:, n, :] for n in range(2)]
        negmax, rowsum, rinv = buf("negmax", [P, 4]), buf("rowsum", [P, 4]), buf("rinv", [P, 4])
        pT = [split(f"at1_pT{n}", [P, NT, BANK], ctx) for n in range(2)]
        att = split("at1_att", [P, 2, S], ctx)
        p_scores = [ctx.enter_context(nc.psum_tensor(f"at1_scores{n}", [P, S], F32)) for n in range(2)]
        p_turn = [ctx.enter_context(nc.psum_tensor(f"at1_turn{n}", [P, 4, P], F32)) for n in range(2)]
        p_att = ctx.enter_context(nc.psum_tensor("at1_att_sum", [P, BANK], F32))
        p_proj = ctx.enter_context(nc.psum_tensor("at1_proj", [P, BANK], F32))
        job_mm, job_hi, proj_free = sem("job_mm"), sem("job_hi"), sem("proj_free")
        scores_mm, max_done, exp_done, rinv_done, normed = (sem(n) for n in ("scores_mm", "max_done", "exp_done", "rinv_done", "normed"))
        turn_mm, turn_hi, turn_lo = sem("turn_mm"), sem("turn_hi"), sem("turn_lo")
        att_mm, att_hi, att_lo = sem("att_mm"), sem("att_hi"), sem("att_lo")
        out_mm, out_added, bias_done = sem("out_mm"), sem("out_added"), sem("bias_done")
        SCALE = float(D1) ** -0.5

        jobs = [("k", 0, 0), ("k", 0, 1), ("q", 0, 0), ("q", 0, 1), ("v", 0, 0)]
        jobs += [("q", 1, 0), ("q", 1, 1), ("k", 1, 0), ("k", 1, 1), ("v", 1, 0), ("q", 2, 0), ("q", 2, 1), ("q", 3, 0), ("q", 3, 1)]
        first_slot = dict(zip(jobs[5:], (1, 3, 9, 11, 12, 13, 14, 17, 19)))

        def jobs_of(slot):
            return [(n, job) for n, job in enumerate(jobs) if first_slot.get(job, -1) == slot]

        out_slots = {22: (0,), 23: (1,), 24: (2, 3)}

        def out_bank(pair_index, j):
            return (p_proj, p_att)[j % 2 if pair_index else 0]

        with nc.Block() as block:
            @block.tensor
            def _(pe):
                def project(n, kind, index, c):
                    if n:
                        pe.wait_ge(proj_free, n)
                    cols = slice(index * D1, (index + 1) * D1)
                    if kind == "v":
                        for t in range(NT):
                            rows = slice(t * P, (t + 1) * P)
                            for k in range(KD):
                                mm = product(pe, p_proj[:, t * D1:(t + 1) * D1], gT[:, k, rows], wv[:, k, cols], k == 0, k == KD - 1)
                    else:
                        w = wq if kind == "q" else wk
                        for k in range(KD):
                            mm = product(pe, p_proj[0:D1, :], w[:, k, cols], gT[:, k, c * BANK:(c + 1) * BANK], k == 0, k == KD - 1)
                    mm.then_inc(job_mm, 1)

                def scores(s):
                    h, i = divmod(s, NT)
                    g = h // (H1 // G1)
                    if i == 0:
                        pe.wait_ge(proj_free, jobs.index(("q", h, 1)) + 1)
                        pe.wait_ge(proj_free, jobs.index(("k", g, 1)) + 1)
                    if s >= 2:
                        pe.wait_ge(exp_done, s - 1)
                    for c in range(2):
                        cols = slice(c * BANK, (c + 1) * BANK)
                        rows = q[h % 2][:, i * P:(i + 1) * P]
                        pe.matmul(p_scores[s % 2][:, cols], rows, khi[g][:, cols], start=True, stop=False)
                        mm = pe.matmul(p_scores[s % 2][:, cols], rows, klo[g][:, cols], start=False, stop=True)
                    mm.then_inc(scores_mm, 1)

                def turn(s):
                    pe.wait_ge(normed, s + 1)
                    for n in range(2):
                        if s:
                            pe.wait_ge(turn_lo, 2 * s - 1 + n)
                        for b in range(4):
                            mm = pe.transpose(p_turn[n][:, b, :], probs[s % 4][:, (4 * n + b) * P:(4 * n + b + 1) * P], m.ident[:, :])
                        mm.then_inc(turn_mm, 1)

                def attend(chunk, part):
                    g = chunk // 2 // (H1 // G1)
                    if part == 0:
                        pe.wait_ge(turn_lo, 8 * chunk + 8)
                        pe.wait_ge(proj_free, jobs.index(("v", g, 0)) + 1)
                        if chunk:
                            pe.wait_ge(att_lo, chunk)
                    for t in range(2 * part, 2 * part + 2):
                        values = v[g][:, t, :, :].rearrange("p a d -> p (a d)")
                        pe.matmul(p_att[:, :], values, pT[chunk % 2].hi[:, t, :], start=(t == 0), stop=False)
                        mm = pe.matmul(p_att[:, :], values, pT[chunk % 2].lo[:, t, :], start=False, stop=(t == NT - 1))
                    if part == 3:
                        mm.then_inc(att_mm, 1)

                def out_job(pair_index, j):
                    bank = out_bank(pair_index, j)
                    pe.wait_ge(proj_free, len(jobs) + 4 * pair_index + j)
                    pe.wait_ge(att_lo, 4 * pair_index + 4)
                    for n in range(2):
                        rows = slice((2 * j + n) * P, (2 * j + n + 1) * P)
                        for h in range(2):
                            mm = product(pe, bank[:, n * DM:(n + 1) * DM], att[:, h, rows], wo[:, 2 * pair_index + h, :],
                                         h == 0, h == 1 and pair_index == 0)
                        for k in range(KD if pair_index else 0):
                            mm = pe.matmul(bank[:, n * DM + k * P:n * DM + (k + 1) * P], h32[:, k, rows], gated_ident[:, k, :],
                                           start=False, stop=(k == KD - 1))
                    mm.then_inc(out_mm, 1)

                for n, job in jobs_of(-1):
                    project(n, *job)
                for s in range(HS):
                    scores(s)
                    if s >= 2:
                        turn(s - 2)
                    if s >= 6:
                        attend((s - 6) // 4, (s - 6) % 4)
                    for n, job in jobs_of(s):
                        project(n, *job)
                    for j in out_slots.get(s, ()):
                        out_job(0, j)
                for s in range(HS, HS + 6):
                    if s < HS + 2:
                        turn(s - 2)
                    attend((s - 6) // 4, (s - 6) % 4)
                for j in range(4):
                    out_job(1, j)

            @block.scalar
            def _(act):
                def job_high(n, kind, index, c):
                    act.wait_ge(job_mm, n + 1)
                    cols = slice(c * BANK, (c + 1) * BANK)
                    if kind == "v":
                        act.activation(v[index][:, :, 0, :], p_proj[:, :].rearrange("p (t d) -> p t d", d=D1), ACT.Copy).then_inc(job_hi, 1)
                    elif kind == "q":
                        if index >= 2:
                            act.wait_ge(scores_mm, (index - 1) * NT)
                        act.activation(q[index % 2][0:D1, cols], p_proj[0:D1, :], ACT.Copy).then_inc(job_hi, 1)
                    else:
                        act.activation(khi[index][D1:P, cols], p_proj[0:D1, :], ACT.Copy)
                        act.activation(khi[index][0:D1, cols], p_proj[0:D1, :], ACT.Copy).then_inc(job_hi, 1)

                def probs_hi(s):
                    chunk = s // 4
                    if s % 4 == 0 and chunk >= 2:
                        act.wait_ge(att_mm, chunk - 1)
                    for n in range(2):
                        act.wait_ge(turn_mm, 2 * s + n + 1)
                        act.activation(pT[chunk % 2].hi[:, 4 * n:4 * n + 4, (s % 4) * P:(s % 4 + 1) * P], p_turn[n][:, :, :], ACT.Copy)\
                           .then_inc(turn_hi, 1)

                def exp(s):
                    act.wait_ge(max_done, s + 1)
                    act.activation(negmax[:, s % 4:s % 4 + 1], negmax[:, s % 4:s % 4 + 1], ACT.Copy, scale=SCALE).then_inc(bias_done, 1)
                    if s >= 4:
                        act.wait_ge(turn_mm, 2 * (s - 3))
                    act.wait_ge(bias_done, s + 1)
                    act.activation(probs[s % 4], p_scores[s % 2][:, :], ACT.Exp, scale=SCALE,
                                   bias=negmax[:, s % 4:s % 4 + 1], accum_out=rowsum[:, s % 4:s % 4 + 1]).then_inc(exp_done, 1)

                def attended_hi(chunk):
                    act.wait_ge(att_mm, chunk + 1)
                    if chunk == 4:
                        act.wait_ge(out_mm, 4)
                    act.activation(att.hi[:, chunk // 2 % 2, chunk % 2 * BANK:(chunk % 2 + 1) * BANK], p_att[:, :], ACT.Copy).then_inc(att_hi, 1)

                for n, job in jobs_of(-1):
                    job_high(n, *job)
                for s in range(HS + 2):
                    if s >= 2:
                        probs_hi(s - 2)
                    if s < HS:
                        exp(s)
                    if s >= 9 and (s - 9) % 4 == 0:
                        attended_hi((s - 9) // 4)
                    for n, job in jobs_of(s):
                        job_high(n, *job)
                for chunk in range((HS + 1 - 9) // 4 + 1, 2 * H1):
                    attended_hi(chunk)

            @block.vector
            def _(dve):
                def job_low(n, kind, index, c):
                    dve.wait_ge(job_hi, n + 1)
                    cols = slice(c * BANK, (c + 1) * BANK)
                    if kind == "v":
                        dve.tensor_tensor(v[index][:, :, 1, :], p_proj[:, :].rearrange("p (t d) -> p t d", d=D1),
                                          as_f32(v[index][:, :, 0, :]), ALU.subtract).then_inc(proj_free, 1)
                    elif kind == "q":
                        out = q[index % 2]
                        dve.tensor_tensor(out[D1:P, cols], p_proj[0:D1, :], as_f32(out[0:D1, cols]), ALU.subtract).then_inc(proj_free, 1)
                    else:
                        hi, lo = khi[index], klo[index]
                        dve.tensor_tensor(lo[0:D1, cols], p_proj[0:D1, :], as_f32(hi[0:D1, cols]), ALU.subtract)
                        dve.tensor_tensor(lo[D1:P, cols], p_proj[0:D1, :], as_f32(hi[0:D1, cols]), ALU.subtract).then_inc(proj_free, 1)

                def maximum(s):
                    dve.wait_ge(scores_mm, s + 1)
                    dve.tensor_reduce(negmax[:, s % 4:s % 4 + 1], p_scores[s % 2][:, :], AX.X, ALU.max, negate=True).then_inc(max_done, 1)

                def inverse_sum(s):
                    dve.wait_ge(exp_done, s + 1)
                    dve.reciprocal(rinv[:, s % 4:s % 4 + 1], rowsum[:, s % 4:s % 4 + 1]).then_inc(rinv_done, 1)

                def probs_lo(s):
                    for n in range(2):
                        out = pT[s // 4 % 2][:, 4 * n:4 * n + 4, (s % 4) * P:(s % 4 + 1) * P]
                        dve.wait_ge(turn_hi, 2 * s + n + 1)
                        dve.tensor_tensor(out.lo, p_turn[n][:, :, :], as_f32(out.hi), ALU.subtract).then_inc(turn_lo, 1)

                def attended_lo(chunk):
                    out = att[:, chunk // 2 % 2, chunk % 2 * BANK:(chunk % 2 + 1) * BANK]
                    dve.wait_ge(att_hi, chunk + 1)
                    dve.tensor_tensor(out.lo, p_att[:, :], as_f32(out.hi), ALU.subtract).then_inc(att_lo, 1)

                def add_out(pair_index, j):
                    dve.wait_ge(out_mm, 4 * pair_index + j + 1)
                    rows = m.x[:, 2 * j:2 * j + 2, :]
                    dve.tensor_tensor(rows, out_bank(pair_index, j)[:, :].rearrange("p (n d) -> p n d", n=2), rows, ALU.add)\
                       .then_inc(proj_free, 1)

                for n, job in jobs_of(-1):
                    job_low(n, *job)
                for s in range(HS + 2):
                    if s < HS:
                        maximum(s)
                    if 1 <= s <= HS:
                        inverse_sum(s - 1)
                    if s >= 2:
                        probs_lo(s - 2)
                    if s >= 9 and (s - 9) % 4 == 0:
                        attended_lo((s - 9) // 4)
                    for n, job in jobs_of(s):
                        job_low(n, *job)
                    for j in out_slots.get(s, ()):
                        add_out(0, j)
                for chunk in range((HS + 1 - 9) // 4 + 1, 2 * H1):
                    attended_lo(chunk)
                for j in range(4):
                    add_out(1, j)

            @block.gpsimd
            def _(pool):
                for s in range(HS):
                    pool.wait_ge(rinv_done, s + 1)
                    pool.tensor_scalar(probs[s % 4], probs[s % 4], rinv[:, s % 4:s % 4 + 1], 1.0, ALU.mult, ALU.mult)\
                        .then_inc(normed, 1)


def ffn1(nc, a, m, sems, sb, split):
    transposed_rows(nc, m, sems, sb, 1, 6, "ln3")
    E8 = NE + 1
    with ExitStack() as ctx:
        def buf(name, shape, dt=F32):
            return sb("ff1_" + name, shape, dt, ctx)

        def sem(name):
            return sems("ff1_" + name)

        w1_in = m.staging[:, 0:4096].rearrange("p (e kn) -> p e kn", e=E8)
        w2_in = m.staging[:, 4096:6144].rearrange("p (e n) -> p e n", e=E8)
        w1, w2 = split("ff1_w1", [P, E8, KD * 2 * FE], ctx), split("ff1_w2", [P, E8, DM], ctx)
        gw_in, gw = buf("gw_in", [P, KD, E8]), split("ff1_gw", [P, KD, E8], ctx)
        bias = buf("bias", [1, E8])
        aff, marked = buf("aff", [P, NT, 16]), buf("marked", [P, NT, 16])
        best, best2 = buf("best", [P, NT, 8]), buf("best2", [P, NT, 8])
        mask, score = buf("mask", [P, NT, E8]), buf("score", [P, NT, E8])
        PAD = 8
        ranks = [buf(f"ranks{n}", [E8, S + PAD]) for n in range(2)]
        positive, weight = buf("positive", [E8, S]), buf("weight", [E8, S])
        row_best, row_last = buf("row_best", [E8, 8]), buf("row_last", [E8, 8])
        chosen = [buf(f"chosen{n}", [E8, S]) for n in range(2)]
        x1, act2 = ([buf(f"{s}{n}", [P, BANK]) for n in range(2)] for s in ("x1", "act2"))
        mid = buf("mid", [P, E8, S])
        weighted = buf("weighted", [P, S])
        fed = [split(f"ff1_fed{n}", [P, S], ctx) for n in range(2)]
        p_y = [ctx.enter_context(nc.psum_tensor(f"ff1_y{n}", [P, 2, DM], F32)) for n in range(4)]
        p_x1, p_x2 = ([ctx.enter_context(nc.psum_tensor(f"ff1_{s}{n}", [P, BANK], F32)) for n in range(2)] for s in ("px1", "px2"))
        gate_in, gate_ready, logits_mm, aff_done, score_done, ranks_mm = (
            sem(n) for n in ("gate_in", "gate_ready", "logits_mm", "aff_done", "score_done", "ranks_mm"))
        rank_chain, w1_hi, w1_ready, w2_gated, w2_hi, w2_ready = (
            sem(n) for n in ("rank_chain", "w1_hi", "w1_ready", "w2_gated", "w2_hi", "w2_ready"))
        up_mm, x1_read, x2_read, mid_done = (sem(n) for n in ("up_mm", "x1_read", "x2_read", "mid_done"))
        chosen_done, spread_mm, weighted_done, fed_hi, fed_ready, down_mm, summed, stored = (
            sem(n) for n in ("chosen_done", "spread_mm", "weighted_done", "fed_hi", "fed_ready", "down_mm", "summed", "stored"))

        with nc.Block() as block:
            @block.sync
            def _(sp):
                sp.wait_ge(gate_in, 1)
                with nc.allow_non_contiguous_dma(reason="seven columns"):
                    sp.dma_start(gw_in[:, :, 0:NE], a["L1_ffn_gate_w"].rearrange("(k p) e -> p k e", p=P)).then_inc(gate_in, 16)
                sp.dma_start(bias[0:1, 0:NE], a["L1_ffn_expert_bias"]).then_inc(gate_in, 16)
                rows = a["out"].rearrange("o (n p) d -> p (o n) d", p=P)
                for j in range(4):
                    sp.wait_ge(summed, j + 1)
                    sp.dma_start(rows[:, 2 * j:2 * j + 2, :], m.x[:, 2 * j:2 * j + 2, :]).then_inc(stored, 16)
                sp.wait_ge(stored, 64)

            @block.tensor
            def _(pe):
                p_logits = p_y[0][:, 0, 0:NT * E8]
                p_ranks = [p_y[n + 1][0:E8, :, :].rearrange("e a b -> e (a b)") for n in range(2)]
                pe.wait_ge(gate_ready, 2)
                for t in range(NT):
                    rows, cols = slice(t * P, (t + 1) * P), slice(t * E8, (t + 1) * E8)
                    for k in range(KD):
                        product(pe, p_logits[:, cols], m.hT[:, k, rows], gw[:, k, :], k == 0, False)
                    mm = pe.matmul(p_logits[:, cols], m.ones[0:1, :], bias[0:1, :], start=False, stop=True)
                mm.then_inc(logits_mm, 1)

                def up(e):
                    pe.wait_ge(w1_ready, e + 1)
                    for c in range(2):
                        n = 2 * e + c
                        for half, (bank, read) in enumerate(((p_x1, x1_read), (p_x2, x2_read))):
                            if n >= 2:
                                pe.wait_ge(read, n - 1)
                            for k in range(KD):
                                at = k * 2 * FE + half * FE
                                mm = product(pe, bank[c][:, :], w1[:, e, at:at + FE], m.hT[:, k, c * BANK:(c + 1) * BANK], k == 0, k == KD - 1)
                            mm.then_inc(up_mm, 1)

                def spread(e):
                    pe.wait_ge(chosen_done, e)
                    for c in range(2):
                        if e == 1:
                            pe.wait_ge(x1_read, 2 * E8)
                        else:
                            pe.wait_ge(weighted_done, 2 * (e - 2) + c + 1)
                        pe.matmul(p_x1[c][:, :], m.ones[0:E8, :], chosen[e % 2][:, c * BANK:(c + 1) * BANK], start=True, stop=True)\
                          .then_inc(spread_mm, 1)

                def down(e):
                    if e == 0:
                        pe.wait_ge(w2_ready, 1)
                    pe.wait_ge(fed_ready, 2 * e + 2)
                    for j in range(4):
                        for n in range(2):
                            rows = slice((2 * j + n) * P, (2 * j + n + 1) * P)
                            left, out = fed[e % 2][:, rows], p_y[j][:, n, :]
                            for q, (lhs, rhs) in enumerate(((left.hi, w2.hi[:, e, :]), (left.hi, w2.lo[:, e, :]), (left.lo, w2.hi[:, e, :]))):
                                mm = pe.matmul(out, lhs, rhs, start=(e == 0 and n == 0 and q == 0), stop=(e == E8 - 1 and q == 2),
                                               skip_group_check=True)
                        if e == E8 - 1:
                            mm.then_inc(down_mm, 1)
                    if e < E8 - 1:
                        mm.then_inc(down_mm, 1)

                up(0)
                pe.wait_ge(score_done, 1)
                for t in range(NT):
                    mm = pe.transpose(p_ranks[t // 4][:, t % 4 * P:(t % 4 + 1) * P], score[:, t, :], m.ident[:, :])
                mm.then_inc(ranks_mm, 1)
                for e in range(1, E8):
                    up(e)
                spread(1)
                down(0)
                for e in range(1, E8):
                    if e + 1 < E8:
                        spread(e + 1)
                    down(e)

            @block.scalar
            def _(act):
                def split_hi(e):
                    act.activation(w1.hi[:, e, :], w1_in[:, e, :], ACT.Copy).then_inc(w1_hi, 1)

                act.wait_ge(m.staged, 48 + 160)
                split_hi(0)
                act.wait_ge(logits_mm, 1)
                logits = p_y[0][:, 0, 0:NT * E8].rearrange("p (t e) -> p t e", e=E8)
                act.activation(aff[:, :, 0:NE], logits[:, :, 0:NE], ACT.Sigmoid).then_inc(aff_done, 1)
                for e in range(E8):
                    if e + 1 < E8:
                        split_hi(e + 1)
                    for c in range(2):
                        n = 2 * e + c
                        act.wait_ge(up_mm, 2 * n + 1)
                        if n >= 2:
                            act.wait_ge(mid_done, n - 1)
                        act.activation(x1[c][:, :], p_x1[c][:, :], ACT.Copy).then_inc(x1_read, 1)
                        act.wait_ge(up_mm, 2 * n + 2)
                        act.activation(act2[c][:, :], p_x2[c][:, :], ACT.Silu).then_inc(x2_read, 1)
                for e in range(E8):
                    for c in range(2):
                        cols = slice(c * BANK, (c + 1) * BANK)
                        if e >= 2 and c == 0:
                            act.wait_ge(down_mm, e - 1)
                        if e == 0:
                            act.wait_ge(mid_done, c + 1)
                        else:
                            act.wait_ge(weighted_done, 2 * e - 1 + c)
                        src = mid[:, 0, cols] if e == 0 else weighted[:, cols]
                        act.activation(fed[e % 2].hi[:, cols], src, ACT.Copy).then_inc(fed_hi, 1)

            @block.vector
            def _(dve):
                chain = Chain(dve, rank_chain)
                dve.memset(bias[:, :], 0.0)
                dve.memset(gw_in[:, :, :], 0.0).then_inc(gate_in, 1)
                for tile, value in ((aff, -1.0), (best2, -1.0), (row_last, -1.0), (score, -1.0), (ranks[0], -1.0)):
                    chain.step(dve.memset(tile[:], value))
                dve.wait_ge(gate_in, 33)
                dve.tensor_copy(gw.hi, gw_in[:, :, :]).then_inc(gate_ready, 1)
                dve.wait_ge(gate_ready, 1)
                dve.tensor_tensor(gw.lo, gw_in[:, :, :], as_f32(gw.hi), ALU.subtract).then_inc(gate_ready, 1)
                dve.wait_ge(w1_hi, 1)
                dve.tensor_tensor(w1.lo[:, 0, :], w1_in[:, 0, :], as_f32(w1.hi[:, 0, :]), ALU.subtract).then_inc(w1_ready, 1)

                chain.settle()
                dve.wait_ge(aff_done, 1)
                for t in range(NT):
                    chain.step(dve.max(best[:, t, :], aff[:, t, :]))
                chain.settle()
                chain.run(dve.tensor_copy(best2[:, :, 0:TOPK], best[:, :, 0:TOPK]))
                for t in range(NT):
                    chain.step(dve.match_replace(marked[:, t, :], best2[:, t, :], aff[:, t, :], -5.0))
                chain.settle()
                chain.run(dve.tensor_scalar(mask[:, :, 0:NE], marked[:, :, 0:NE], -5.0, None, ALU.is_equal))
                chain.run(dve.tensor_tensor(marked[:, :, 0:NE], aff[:, :, 0:NE], mask[:, :, 0:NE], ALU.mult))
                dve.scalar_tensor_tensor(out=score[:, :, 0:NE], in0=mask[:, :, 0:NE], scalar=-1.0, in1=marked[:, :, 0:NE],
                                         op0=ALU.add, op1=ALU.add).then_inc(score_done, 1)
                dve.wait_ge(ranks_mm, 1)
                for n in range(2):
                    chain.step(dve.tensor_copy(ranks[0][:, n * BANK:(n + 1) * BANK],
                                               p_y[n + 1][0:E8, :, :].rearrange("e a b -> e (a b)")))
                chain.settle()
                chain.step(dve.tensor_scalar(positive[:, :], ranks[0][:, 0:S], 0.0, None, ALU.max))

                full, rest = divmod(CAPACITY, 8)
                for r in range(full):
                    src, dst = ranks[r % 2], ranks[1 - r % 2]
                    chain.run(dve.max(row_best[:, :], src[:, :]))
                    chain.run(dve.match_replace(dst[:, :], row_best[:, :], src[:, :], -3.0))
                src, dst = ranks[full % 2], ranks[1 - full % 2]
                chain.run(dve.max(row_best[:, :], src[:, :]))
                chain.run(dve.tensor_copy(row_last[:, 0:rest], row_best[:, 0:rest]))
                chain.run(dve.match_replace(dst[:, :], row_last[:, :], src[:, :], -3.0))
                chain.run(dve.scalar_tensor_tensor(out=weight[:, :], in0=dst[:, 0:S], scalar=-3.0, in1=positive[:, :],
                                                   op0=ALU.is_equal, op1=ALU.mult))

                def choose(e):
                    if e > 2:
                        dve.wait_ge(spread_mm, 2 * (e - 2))
                    dve.tensor_scalar(chosen[e % 2][:, :], weight[:, :], m.ident[0:E8, e - 1:e], None, ALU.mult).then_inc(chosen_done, 1)

                def low(e, c):
                    cols = slice(c * BANK, (c + 1) * BANK)
                    dve.wait_ge(fed_hi, 2 * e + c + 1)
                    src = mid[:, 0, cols] if e == 0 else weighted[:, cols]
                    dve.tensor_tensor(fed[e % 2].lo[:, cols], src, as_f32(fed[e % 2].hi[:, cols]), ALU.subtract).then_inc(fed_ready, 1)

                choose(1)
                for e in range(E8):
                    if e:
                        if e < NE:
                            choose(e + 1)
                        for c in range(2):
                            cols = slice(c * BANK, (c + 1) * BANK)
                            dve.wait_ge(mid_done, 2 * e + c + 1)
                            dve.wait_ge(spread_mm, 2 * (e - 1) + c + 1)
                            if e > 1:
                                dve.wait_ge(fed_ready, 2 * e)
                            dve.tensor_tensor(weighted[:, cols], mid[:, e, cols], p_x1[c][:, :], ALU.mult).then_inc(weighted_done, 1)
                    for c in range(2):
                        low(e, c)
                for j in range(4):
                    dve.wait_ge(down_mm, E8 - 1 + j + 1)
                    rows = m.x[:, 2 * j:2 * j + 2, :]
                    dve.tensor_tensor(rows, p_y[j][:, :, :], rows, ALU.add).then_inc(summed, 1)

            @block.gpsimd
            def _(pool):
                def w1_low(e):
                    pool.wait_ge(w1_hi, e + 1)
                    if e == 1:
                        pool.wait_ge(w1_ready, 1)
                    pool.tensor_tensor(w1.lo[:, e, :], w1_in[:, e, :], as_f32(w1.hi[:, e, :]), ALU.subtract).then_inc(w1_ready, 1)

                def middle(e, c):
                    n = 2 * e + c
                    pool.wait_ge(x2_read, n + 1)
                    pool.wait_ge(x1_read, n + 1)
                    pool.tensor_tensor(mid[:, e, c * BANK:(c + 1) * BANK], x1[c][:, :], act2[c][:, :], ALU.mult).then_inc(mid_done, 1)

                w1_low(1)
                for e in range(E8):
                    middle(e, 0)
                    middle(e, 1)
                    if e + 2 < E8:
                        w1_low(e + 2)
                    pool.wait_ge(m.staged, 48 + 160)
                    pool.tensor_tensor(w2_in[:, e, :], w2_in[:, e, :], m.gate[:, 1, 1, :], ALU.mult).then_inc(w2_gated, 1)
                pool.wait_ge(w2_gated, E8)
                pool.tensor_scalar(w2.hi, w2_in, 1.0, 1.0, ALU.mult, ALU.mult).then_inc(w2_hi, 1)
                pool.wait_ge(w2_hi, 1)
                pool.tensor_tensor(w2.lo, w2_in, as_f32(w2.hi), ALU.subtract).then_inc(w2_ready, 1)


def constants():
    freqs = (np.float32(1.0) / np.float32(10000.0) ** (np.arange(0, D0, 2, dtype=np.float32) / np.float32(D0))).astype(np.float32)
    ang = (np.arange(S, dtype=np.float32)[:, None] * freqs[None, :]).astype(np.float32)
    root = np.float64(D0) ** -0.25
    c, s = (np.cos(ang.astype(np.float64)) * root).T, (np.sin(ang.astype(np.float64)) * root).T
    causal = np.where(np.arange(P)[None, :] > np.arange(P)[:, None], MASK_NEG, 0.0)
    return {
        "cos": np.concatenate([c, c]).astype(np.float32),
        "sin": np.concatenate([-s, s]).astype(np.float32),
        "mask": causal.astype(np.float32),
        "ident": np.eye(P, dtype=np.float32),
    }


INPUTS = ["L0_attn_x", "L0_attn_Wqkv", "L0_attn_Wo", "L0_ffn_w_gate", "L0_ffn_w_up", "L0_ffn_w_down", "L0_c", "L0_wmod",
          "L1_attn_norm_scale", "L1_attn_split_scale", "L1_attn_Wq", "L1_attn_Wk", "L1_attn_Wv", "L1_attn_Wo",
          "L1_ffn_gate_w", "L1_ffn_expert_bias", "L1_ffn_shared_w1", "L1_ffn_shared_w2", "L1_ffn_routed_w1",
          "L1_ffn_routed_w2", "L1_c", "L1_wmod"]


def columns(v):
    return np.asarray(v).reshape(-1, P).T


LAYOUTS = {
    "L0_c": columns, "L1_c": columns,
    "L1_attn_norm_scale": columns, "L1_attn_split_scale": columns,
    "L1_attn_Wq": np.transpose, "L1_attn_Wk": np.transpose, "L1_attn_Wv": np.transpose, "L1_attn_Wo": np.transpose,
    "L1_ffn_expert_bias": lambda v: np.asarray(v).reshape(1, -1),
}


def kernel(**inputs):
    import concourse.bacc as bacc
    from concourse.bass_utils import run_bass_kernel_spmd

    nc = bacc.Bacc("TRN2", target_bir_lowering=False, num_devices=1)
    arrays, aps = {}, {}
    for name, value in [(n, inputs[n]) for n in INPUTS] + list(constants().items()):
        if name in LAYOUTS:
            value = LAYOUTS[name](value)
        value = np.ascontiguousarray(value)
        arrays[name] = value
        aps[name] = nc.dram_tensor(name, value.shape, mybir.dt.from_np(value.dtype), kind="ExternalInput").ap()
    aps["out"] = nc.dram_tensor("out", (1, S, DM), F32, kind="ExternalOutput").ap()
    build(nc, aps)
    result = run_bass_kernel_spmd(nc, [arrays], core_ids=[0])
    return result.results[0]["out"]
```

```python
from contextlib import ExitStack

import numpy as np

import concourse.bass as bass
from concourse import mybir

P = 128
S = 1024
DM = 256
NT = S // P
KD = DM // P
BANK = 512
EPS = 1e-5

H0, KV0, D0 = 16, 4, 128
PER_KV = H0 // KV0
I0 = 1024
H1, G1, D1 = 4, 2, 64
RMS_EPS = 1e-8
NE, FE, TOPK = 7, 128, 2
CAPACITY = S // NE
MASK_NEG = -2.3819763e+38

F32 = mybir.dt.float32
F32R = mybir.dt.float32r
BF16 = mybir.dt.bfloat16
ALU = mybir.AluOpType
ACT = mybir.ActivationFunctionType
AX = mybir.AxisListType


class Split:

    def __init__(self, hi, lo):
        self.hi, self.lo = hi, lo

    def __getitem__(self, index):
        return Split(self.hi[index], self.lo[index])

    def __call__(self, pattern, **sizes):
        return Split(self.hi.rearrange(pattern, **sizes), self.lo.rearrange(pattern, **sizes))


def product(pe, out, left, right, start, stop):
    pe.matmul(out, left.hi, right.hi, start=start, stop=False)
    pe.matmul(out, left.hi, right.lo, start=False, stop=False)
    return pe.matmul(out, left.lo, right.hi, start=False, stop=stop)


def as_f32(ap):
    return ap.bitcast(F32)


class Chain:

    def __init__(self, engine, sem, value=0):
        self.engine, self.sem, self.value = engine, sem, value

    def step(self, ins):
        ins.then_inc(self.sem, 1)
        self.value += 1
        return ins

    def settle(self):
        self.engine.wait_ge(self.sem, self.value)

    def run(self, ins):
        self.step(ins)
        self.settle()
        return ins


def build(nc, a):
    top = ExitStack()
    with top:
        def sb(name, shape, dt=F32, ctx=top):
            return ctx.enter_context(nc.sbuf_tensor(name, shape, dt))

        def split(name, shape, ctx=top):
            return Split(sb(name + "_hi", shape, F32R, ctx)[:], sb(name + "_lo", shape, F32R, ctx)[:])

        x = sb("x", [P, NT, DM])
        ident = sb("ident_sb", [P, P])
        identb = sb("identb_sb", [P, P], BF16)
        maskb = sb("maskb_sb", [P, P], BF16)
        modcol = sb("modcol", [P, 2, 12])
        gate = sb("gate", [P, 2, 2, DM])
        mod_row = sb("mod_row", [P, 2, DM])
        stats = sb("stats", [P, NT, 6])
        meanvar = sb("meanvar", [P, NT, 2])
        vareps = sb("vareps", [P, NT])
        rstd = sb("rstd", [P, NT])
        tiny = sb("tiny", [P, 2, NT])
        tables = sb("tables", [P, 3])
        hT = split("hT", [P, KD, S])
        sems = Sems(nc, top)
        staging, staging1 = sb("staging", [P, 6144]), sb("staging1", [P, 2048])
        staged, staged1 = sems("staged"), sems("staged1")
        gate_w, expert_bias, gate_in = split("gate_w", [P, KD, NE]), sb("expert_bias", [NE, 1]), sems("gate_in")
        w2_gated = sems("w2_gated")
        m = Shared(x, ident, identb, maskb, modcol, gate, stats, meanvar, vareps, rstd, tiny, hT,
                   staging, staging1, staged, staged1, gate_w, expert_bias, gate_in, mod_row, tables, w2_gated)
        attention0(nc, a, m, sems, sb, split)
        ffn0(nc, a, m, sems, sb, split)
        attention1(nc, a, m, sems, sb, split)
        ffn1(nc, a, m, sems, sb, split)


class Shared:
    def __init__(self, x, ident, identb, maskb, modcol, gate, stats, meanvar, vareps, rstd, tiny, hT,
                 staging, staging1, staged, staged1, gate_w, expert_bias, gate_in, mod_row, tables, w2_gated):
        self.tables, self.w2_gated = tables, w2_gated
        self.x, self.ident, self.identb, self.maskb = x, ident, identb, maskb
        self.modcol, self.gate, self.stats, self.meanvar = modcol, gate, stats, meanvar
        self.vareps, self.rstd, self.tiny, self.hT = vareps, rstd, tiny, hT
        self.gate_w, self.expert_bias, self.gate_in, self.mod_row = gate_w, expert_bias, gate_in, mod_row
        self.staging, self.staging1, self.staged, self.staged1 = staging, staging1, staged, staged1


class Sems:

    def __init__(self, nc, ctx):
        self.nc, self.ctx = nc, ctx

    def __call__(self, name):
        return self.ctx.enter_context(self.nc.semaphore(name))


def load_table(act, m, func, n):
    act.activation(m.tables[:, n:n + 1], m.ident[:, 0:1], func)


def row_stats(dve, m, chain, sqrt_in, sqrt_out, meanwhile=lambda: None, begun=False):
    for n in range(0 if begun else NT):
        chain.step(dve.bn_stats(m.stats[:, n, :], m.x[:, n, :]))
    chain.settle()
    for n in range(NT):
        chain.step(dve.bn_aggr(m.meanvar[:, n, :], m.stats[:, n, :]))
    chain.settle()
    dve.tensor_scalar(m.vareps[:, :], m.meanvar[:, :, 1], EPS, None, ALU.add).then_inc(sqrt_in, 1)
    meanwhile()
    dve.wait_ge(sqrt_out, 1)
    chain.run(dve.reciprocal(m.rstd[:, :], m.tiny[:, 0, :]))
    chain.run(dve.tensor_tensor(m.tiny[:, 1, :], m.rstd[:, :], m.rstd[:, :], ALU.mult))
    chain.run(dve.tensor_tensor(m.tiny[:, 1, :], m.tiny[:, 1, :], m.vareps[:, :], ALU.mult))
    chain.run(dve.tensor_scalar(m.tiny[:, 1, :], m.tiny[:, 1, :], -0.5, 1.5, ALU.mult, ALU.add))
    chain.run(dve.tensor_tensor(m.rstd[:, :], m.rstd[:, :], m.tiny[:, 1, :], ALU.mult))


def row_stats_sqrt(act, m, sqrt_in, sqrt_out):
    act.wait_ge(sqrt_in, 1)
    act.activation(m.tiny[:, 0, :], m.vareps[:, :], ACT.Sqrt).then_inc(sqrt_out, 1)


def opening(nc, a, m, sems, sb, load_early, split_early):
    PARTS = 6 * DM // BANK
    with ExitStack() as ctx:
        wmod = sb("wmod", [P, 2, KD, 6 * DM], F32, ctx)
        craw = sb("craw", [P, 2, KD], F32, ctx)
        csil = sb("csil", [P, 2, KD], F32, ctx)
        ones = sb("ones", [P, P], F32, ctx)
        cwide = sb("cwide", [P, 2, KD, P], F32, ctx)
        rows = sb("mod_rows", [P, 2, 6 * DM], F32, ctx)
        mask32 = sb("mask32", [P, P], F32, ctx)
        sgn = sb("sgn", [P, 2, DM], F32, ctx)
        xn = sb("ln0_xn", [P, NT, DM], F32, ctx)
        h32 = sb("ln0_h32", [P, KD, S], F32, ctx)
        p_rows = [ctx.enter_context(nc.psum_tensor(f"p_rows{n}", [P, BANK], F32)) for n in range(PARTS)]
        p_col = ctx.enter_context(nc.psum_tensor("p_col", [P, 2, 12], F32))
        banks = [ctx.enter_context(nc.psum_tensor(f"ln0_bank{n}", [P, BANK], F32)) for n in range(4)]
        c_in, x_in, const_in = sems("c_in"), sems("x_in"), sems("const_in")
        w_in = [sems(f"wmod_in{n}") for n in range(PARTS + 1)]
        ones_done, c_silu, c_wide, rows_mm, rows_read = (sems(n) for n in ("ones_done", "c_silu", "c_wide", "rows_mm", "rows_read"))
        col_mm, col_read, col_done, chain_sem = (sems(n) for n in ("col_mm", "col_read", "col_done", "mod_chain"))
        sqrt_in, sqrt_out, normed, turned, scaled = (sems("ln0_" + n) for n in ("sqrt_in", "sqrt_out", "normed", "turned", "scaled"))

        def quarter(q):
            return q % KD, slice(q // KD * BANK, (q // KD + 1) * BANK)

        with nc.Block() as block:
            @block.sync
            def _(sp):
                for n in range(2):
                    sp.dma_start(craw[:, n, :], a[f"L{n}_c"]).then_inc(c_in, 16)
                w = a["L0_wmod"].rearrange("(k p) n -> p k n", p=P)
                for b in range(PARTS):
                    cols = slice(b * BANK, (b + 1) * BANK)
                    sp.dma_start(wmod[:, 0, :, cols], w[:, :, cols]).then_inc(w_in[b], 16)
                load_early(sp)
                sp.dma_start(wmod[:, 1, :, :], a["L1_wmod"].rearrange("(k p) n -> p k n", p=P)).then_inc(w_in[PARTS], 16)

            @block.scalar
            def _(act):
                act.dma_start(m.x[:, :, :], a["L0_attn_x"].rearrange("o (n p) d -> p (o n) d", p=P)).then_inc(x_in, 16)
                act.dma_start(m.ident[:, :], a["ident"]).then_inc(const_in, 16)
                act.dma_start(mask32[:, :], a["mask"]).then_inc(const_in, 16)
                act.wait_ge(c_in, 32)
                act.activation(csil[:, :, :], craw[:, :, :], ACT.Silu).then_inc(c_silu, 1)

                def read_rows(layer, b):
                    act.wait_ge(rows_mm, layer * PARTS + b + 1)
                    act.activation(rows[:, layer, b * BANK:(b + 1) * BANK], p_rows[b][:, :], ACT.Copy).then_inc(rows_read, 1)

                read_rows(0, 0)
                row_stats_sqrt(act, m, sqrt_in, sqrt_out)
                read_rows(0, 1)
                read_rows(0, 2)
                act.wait_ge(col_done, 1)
                for q in range(4):
                    k, cols = quarter(q)
                    act.wait_ge(turned, q + 1)
                    act.activation(h32[:, k, cols], banks[q][:, :], ACT.Identity,
                                   scale=m.modcol[:, 0, 2 + k:3 + k], bias=m.modcol[:, 0, k:k + 1]).then_inc(scaled, 1)
                for b in range(PARTS):
                    read_rows(1, b)

            @block.tensor
            def _(pe):
                def mod_rows(layer, b):
                    pe.wait_ge(w_in[PARTS if layer else b], 16)
                    if layer:
                        pe.wait_ge(rows_read, b + 1)
                    for k in range(KD):
                        mm = pe.matmul(p_rows[b][:, :], cwide[:, layer, k, :], wmod[:, layer, k, b * BANK:(b + 1) * BANK],
                                       start=(k == 0), stop=(k == KD - 1))
                    mm.then_inc(rows_mm, 1)

                def mod_columns(layer, j0, j1):
                    for j in range(j0, j1):
                        mm = pe.transpose(p_col[:, layer, j:j + 1], rows[0:1, layer, j * P:(j + 1) * P], m.ident[0:1, 0:1])
                    mm.then_inc(col_mm, 1)

                pe.wait_ge(c_wide, 2 * KD)
                for b in range(PARTS):
                    mod_rows(0, b)
                pe.wait_ge(const_in, 32)
                pe.wait_ge(rows_read, 1)
                mod_columns(0, 0, 4)
                for q in range(4):
                    k, half = q % KD, q // KD
                    pe.wait_ge(normed, 4 * (half + 1))
                    for n in range(4):
                        mm = pe.transpose(banks[q][:, n * P:(n + 1) * P], xn[:, 4 * half + n, k * P:(k + 1) * P], m.ident[:, :])
                    mm.then_inc(turned, 1)
                for b in range(PARTS):
                    mod_rows(1, b)
                pe.wait_ge(col_read, 1)
                mod_columns(0, 4, 12)
                pe.wait_ge(rows_read, 2 * PARTS)
                mod_columns(1, 0, 12)

            @block.vector
            def _(dve):
                chain = Chain(dve, chain_sem)
                chain.run(dve.memset(ones[:, :], 1.0))
                dve.wait_ge(c_silu, 1)
                for n in range(2):
                    for k in range(KD):
                        dve.tensor_scalar(cwide[:, n, k, :], ones[:, :], csil[:, n, k:k + 1], None, ALU.mult).then_inc(c_wide, 1)

                def gates(n):
                    dve.wait_ge(rows_read, PARTS * (n + 1))
                    for g, part in enumerate((2, 5)):
                        raw, out, s = rows[:, n, part * DM:(part + 1) * DM], m.gate[:, n, g, :], sgn[:, g, :]
                        chain.run(dve.tensor_scalar(s, raw, 0.0, 2.0, ALU.is_ge, ALU.mult))
                        chain.run(dve.tensor_scalar(s, s, -1.0, None, ALU.add))
                        chain.run(dve.tensor_tensor(out, raw, s, ALU.mult))
                        chain.run(dve.tensor_scalar(out, out, 0.25, None, ALU.max))
                        chain.run(dve.tensor_tensor(out, out, s, ALU.mult))

                def first_columns():
                    dve.wait_ge(col_mm, 1)
                    dve.tensor_copy(m.modcol[:, 0, 0:4], p_col[:, 0, 0:4]).then_inc(col_read, 1)
                    dve.wait_ge(col_read, 1)
                    dve.tensor_scalar(m.modcol[:, 0, 2:4], m.modcol[:, 0, 2:4], 1.0, None, ALU.add).then_inc(col_done, 1)

                dve.wait_ge(x_in, 16)
                row_stats(dve, m, chain, sqrt_in, sqrt_out, first_columns)
                for n in range(NT):
                    dve.tensor_scalar(xn[:, n, :], m.x[:, n, :], m.meanvar[:, n, 0:1], m.rstd[:, n:n + 1],
                                      ALU.subtract, ALU.mult).then_inc(normed, 1)
                dve.wait_ge(const_in, 32)
                dve.tensor_copy(m.identb[:, :], m.ident[:, :])
                dve.tensor_copy(m.maskb[:, :], mask32[:, :])
                gates(0)
                for q in range(4):
                    k, cols = quarter(q)
                    dve.wait_ge(scaled, q + 1)
                    chain.run(dve.tensor_copy(m.hT.hi[:, k, cols], h32[:, k, cols]))
                    dve.tensor_tensor(m.hT.lo[:, k, cols], h32[:, k, cols], as_f32(m.hT.hi[:, k, cols]), ALU.subtract)
                gates(1)
                dve.tensor_copy(m.mod_row[:, 0, :], rows[:, 1, 0:DM])
                dve.tensor_scalar(m.mod_row[:, 1, :], rows[:, 1, DM:2 * DM], 1.0, None, ALU.add)
                dve.wait_ge(col_mm, 3)
                chain.step(dve.tensor_copy(m.modcol[:, 0, 4:12], p_col[:, 0, 4:12]))
                chain.run(dve.tensor_copy(m.modcol[:, 1, :], p_col[:, 1, :]))
                chain.step(dve.tensor_scalar(m.modcol[:, 0, 8:10], m.modcol[:, 0, 8:10], 1.0, None, ALU.add))
                for j in (2, 8):
                    chain.step(dve.tensor_scalar(m.modcol[:, 1, j:j + 2], m.modcol[:, 1, j:j + 2], 1.0, None, ALU.add))

            @block.gpsimd
            def _(pool):
                split_early(pool)


def transposed_rows(nc, m, sems, sb, layer, part, name):
    with ExitStack() as ctx:
        xn = sb(name + "_xn", [P, NT, DM], F32, ctx)
        h32 = sb(name + "_h32", [P, KD, S], F32, ctx)
        banks = [ctx.enter_context(nc.psum_tensor(f"{name}_bank{n}", [P, BANK], F32)) for n in range(4)]
        sqrt_in, sqrt_out = sems(name + "_sqrt_in"), sems(name + "_sqrt_out")
        normed, turned, scaled, chain_sem = (sems(f"{name}_{s}") for s in ("normed", "turned", "scaled", "chain"))
        with nc.Block() as block:
            @block.vector
            def _(dve):
                chain = Chain(dve, chain_sem)
                row_stats(dve, m, chain, sqrt_in, sqrt_out)
                for n in range(NT):
                    dve.tensor_scalar(xn[:, n, :], m.x[:, n, :], m.meanvar[:, n, 0:1], m.rstd[:, n:n + 1],
                                      ALU.subtract, ALU.mult).then_inc(normed, 1)
                for q in range(4):
                    k, cols = q % KD, slice(q // KD * BANK, (q // KD + 1) * BANK)
                    dve.wait_ge(scaled, q + 1)
                    chain.run(dve.tensor_copy(m.hT.hi[:, k, cols], h32[:, k, cols]))
                    chain.run(dve.tensor_tensor(m.hT.lo[:, k, cols], h32[:, k, cols], as_f32(m.hT.hi[:, k, cols]),
                                                ALU.subtract))

            @block.scalar
            def _(act):
                row_stats_sqrt(act, m, sqrt_in, sqrt_out)
                for q in range(4):
                    k, cols = q % KD, slice(q // KD * BANK, (q // KD + 1) * BANK)
                    act.wait_ge(turned, q + 1)
                    act.activation(h32[:, k, cols], banks[q][:, :], ACT.Identity,
                                   scale=m.modcol[:, layer, part + 2 + k:part + 3 + k],
                                   bias=m.modcol[:, layer, part + k:part + k + 1]).then_inc(scaled, 1)

            @block.tensor
            def _(pe):
                for q in range(4):
                    k, half = q % KD, q // KD
                    pe.wait_ge(normed, 4 * (half + 1))
                    for n in range(4):
                        mm = pe.transpose(banks[q][:, n * P:(n + 1) * P], xn[:, 4 * half + n, k * P:(k + 1) * P],
                                          m.ident[:, :])
                    mm.then_inc(turned, 1)


def attention0(nc, a, m, sems, sb, split):
    UNITS = PER_KV * NT
    TGROUPS = 12
    CH = 2
    with ExitStack() as ctx:
        def buf(name, shape, dt=F32):
            return sb("at0_" + name, shape, dt, ctx)

        def pair(name, shape):
            return split("at0_" + name, shape, ctx)

        cos, sin = buf("cos", [P, S]), buf("sin", [P, S])
        wq_in, wkv_in, wo_in = buf("wq_in", [P, KD, P]), buf("wkv_in", [P, KD, 2, P]), buf("wo_in", [P, DM])
        wq, wkv, wo = pair("wq", [P, KD, P]), pair("wkv", [P, KD, 2, P]), pair("wo", [P, DM])
        def sem(name):
            return sems("at0_" + name)

        tables_in, wq_loaded, wkv_loaded, wo_loaded = (sem(n) for n in ("tables_in", "wq_loaded", "wkv_loaded", "wo_loaded"))
        wq_ready, wkv_ready, wo_ready = sem("wq_ready"), sem("wkv_ready"), sem("wo_ready")
        rope_mm = sem("rope_mm")
        rope_copied = sem("rope_copied")
        rope_done = sem("rope_done")
        keys_ready = sem("keys_ready")
        v_mm, v_hi = sem("v_mm"), sem("v_hi")
        proj_free = sem("proj_free")
        query_free = sem("query_free")
        scores_mm, max_done, exp_done = (sem(n) for n in ("scores_mm", "max_done", "exp_done"))
        turn_mm, turn_hi, turn_lo = sem("turn_mm"), sem("turn_hi"), sem("turn_lo")
        inverted = sem("inverted")
        att_mm, att_hi, att_lo = sem("att_mm"), sem("att_hi"), sem("att_lo")
        out_mm = sem("out_mm")
        key_hi, w_hi, wo_gated, rope_turned, rope_sum, query_hi = (sem(n) for n in ("key_hi", "w_hi", "wo_gated", "rope_turned", "rope_sum", "query_hi"))

        wqkv = a["L0_attn_Wqkv"].rearrange("(k p) n -> p k n", p=P)
        wo_rows = a["L0_attn_Wo"].rearrange("(h p) n -> p h n", p=P)

        def load_q(sp, head, n):
            if not (isinstance(n, int) and n == 0):
                sp.wait_ge(wq_ready, n)
            sp.dma_start(wq_in[:, :, :], wqkv[:, :, bass.ds(head * P, P)]).then_inc(wq_loaded, 16)

        def load_kv(sp, g):
            if not (isinstance(g, int) and g == 0):
                sp.wait_ge(wkv_ready, g)
            for j in range(2):
                sp.dma_start(wkv_in[:, :, j, :], wqkv[:, :, bass.ds(g * P + (H0 + j * KV0) * P, P)]).then_inc(wkv_loaded, 16)

        def load_early(sp):
            load_kv(sp, 0)
            load_q(sp, 0, 0)
            sp.dma_start(cos[:, :], a["cos"]).then_inc(tables_in, 16)
            sp.dma_start(sin[:, :], a["sin"]).then_inc(tables_in, 16)

        def alone(pool):
            pool.nop(nofuse=True)

        def split_weights(pool, n, staged, out, ready):
            alone(pool)
            pool.tensor_scalar(out.hi, staged, 1.0, 1.0, ALU.mult, ALU.mult).then_inc(w_hi, 1)
            pool.wait_ge(w_hi, n + 1)
            pool.tensor_tensor(out.lo, staged, as_f32(out.hi), ALU.subtract).then_inc(ready, 1)

        def split_q(pool, n, head, projected):
            pool.wait_ge(wq_loaded, head * 16 + 16)
            if projected is not None:
                pool.wait_ge(rope_mm, projected)
            split_weights(pool, n, wq_in[:, :, :], wq, wq_ready)

        def split_kv(pool, n, g):
            pool.wait_ge(wkv_loaded, g * 32 + 32)
            if not (isinstance(g, int) and g == 0):
                pool.wait_ge(v_mm, g * 2)
            split_weights(pool, n, wkv_in[:, :, :, :], wkv, wkv_ready)

        def split_early(pool):
            split_kv(pool, 0, 0)
            split_q(pool, 1, 0, None)

        opening(nc, a, m, sems, sb, load_early, split_early)
        kT, v = pair("kT", [P, S]), pair("v", [P, NT, D0])
        k_next = buf("k_next", [P, S])
        q = [pair(f"q{n}", [P, S]) for n in range(2)]
        swapped, plain = buf("swapped", [P, 2, BANK]), buf("plain", [P, 2, BANK])
        probs = buf("probs", [P, 4, S])
        negmax, rowsum, rinv = buf("negmax", [P, 4]), buf("rowsum", [P, 2, NT]), buf("rinv", [P, 2, NT])
        pT = [pair("pT0", [P, 4, BANK]), pair("pT1", [P, 8, BANK])]
        att = pair("att", [P, 2, S])
        p_scores = [ctx.enter_context(nc.psum_tensor(f"at0_scores{n}", [P, S], F32)) for n in range(2)]
        p_turn = [ctx.enter_context(nc.psum_tensor(f"at0_turn{n}", [P, 4, P], F32)) for n in range(2)]
        p_att = ctx.enter_context(nc.psum_tensor("at0_att", [P, BANK], F32))
        p_proj = ctx.enter_context(nc.psum_tensor("at0_proj", [P, BANK], F32))


        early_banks = [p_proj[:, :], p_att[:, :]] + [p_turn[n][:, :, :].rearrange("p a b -> p (a b)") for n in range(2)]

        last_banks = [p_proj[:, :], p_scores[0][:, 0:BANK], p_scores[0][:, BANK:S], p_scores[1][:, 0:BANK]]

        def query_bank(c):
            return p_scores[c][:, BANK:S]

        JOBS, ROPES, QUERIES = 20, 10, 8

        def tgroups_before(unit):
            h, i = divmod(unit, NT)
            return TGROUPS * h + (i if i < 4 else 4 + 2 * (i - 4))

        def blocks(i):
            return [(0, min(i + 1, 4))] + ([(4, i + 1)] if i >= 4 else [])

        QUERY_UNITS = (0, 1)
        KEY_SLOTS, VALUE_SLOTS = [(1, 1), (2, 1)], [(0, 3), (0, 5)]
        USES = [(h, i, kind) for h in range(PER_KV) for i in range(NT) for kind, here in (
            ("query", i in QUERY_UNITS), ("value", (h, i) in VALUE_SLOTS), ("key", (h, i) in KEY_SLOTS), ("out", i >= 4)) if here]

        def before(h, i, kind, first, last, kinds):
            done = USES[:USES.index((h, i, kind))]
            if first:
                done = [u for u in done if not (u[2] == "out" and u[0] == 0)]
            if last:
                done = [u for u in done if u[2] != "key" and not (u[2] == "query" and u[0] == PER_KV - 1)]
            return len([u for u in done if u[2] in kinds])

        def job(g, h, i, kind, first, last):
            return g * JOBS + (2 if first else -2) + before(h, i, kind, first, last, ("value", "key", "out"))

        def query(g, h, c):
            return g * QUERIES + 2 + 2 * h + c

        def rope(h, i, kind, last):
            return 4 + before(h, i, kind, False, last, ("query", "key"))

        def body(g, first, last, slot):
            for s in range(UNITS):
                slot(g, s, first, last)

        def groups(engine, slot):
            body(0, True, False, slot)
            with engine.Fori(1, KV0 - 1) as g:
                body(g, False, False, slot)
            body(KV0 - 1, False, True, slot)

        with nc.Block() as block:
            @block.sync
            def _(sp):
                def load_o(n):
                    if not (isinstance(n, int) and n == 0):
                        sp.wait_ge(wo_ready, n)
                    sp.dma_start(wo_in[:, :].rearrange("p (o d) -> p o d", o=1), wo_rows[:, bass.ds(n, 1), :]).then_inc(wo_loaded, 16)

                load_q(sp, 1, 1)
                for n, name in enumerate(("L0_ffn_w_gate", "L0_ffn_w_up")):
                    sp.dma_start(m.staging[:, n * 2048:(n + 1) * 2048].rearrange("p (k n) -> p k n", k=KD),
                                 a[name].rearrange("(k p) n -> p k n", p=P)).then_inc(m.staged, 16)
                sp.dma_start(m.staging[:, 4096:6144].rearrange("p (c d) -> p c d", d=DM),
                             a["L0_ffn_w_down"].rearrange("(c p) d -> p c d", p=P)).then_inc(m.staged, 16)

                at = 0
                for name in ("L1_attn_Wq", "L1_attn_Wk", "L1_attn_Wv"):
                    w = a[name]
                    n = KD * w.shape[1]
                    sp.dma_start(m.staging1[:, at:at + n].rearrange("p (k n) -> p k n", k=KD), w.rearrange("(k p) n -> p k n", p=P))\
                      .then_inc(m.staged1, 16)
                    at += n
                for half in range(2):
                    sp.dma_start(m.staging1[half * D1:(half + 1) * D1, at:].rearrange("p (h n) -> p h n", h=H1),
                                 a["L1_attn_Wo"].rearrange("(h p) n -> p h n", p=D1)).then_inc(m.staged1, 16)

                def group(g, last, first=False):
                    if not last:
                        load_kv(sp, g + 1)
                    for h in range(PER_KV):
                        n = g * PER_KV + h
                        if not (first and h == 0):
                            load_o(n - 1)
                        if not (last and h >= 2):
                            load_q(sp, n + 2, n + 2)

                group(0, False, True)
                with sp.Fori(1, KV0 - 1) as g:
                    group(g, False)
                group(KV0 - 1, True)
                load_o(H0 - 1)

            @block.tensor
            def _(pe):
                def proj_bank(n):
                    if not (isinstance(n, int) and n == 0):
                        pe.wait_ge(proj_free, n)

                def rope_job(w, c, bank):
                    for k in range(KD):
                        mm = product(pe, bank, w[:, k, :], m.hT[:, k, c * BANK:(c + 1) * BANK], k == 0, k == KD - 1)
                    mm.then_inc(rope_mm, 1)

                def key_job(g, c, bank):
                    pe.wait_ge(wkv_ready, g + 1)
                    rope_job(wkv[:, :, 0, :], c, bank)

                def query_job(head, c, bank):
                    pe.wait_ge(wq_ready, head + 1)
                    rope_job(wq, c, bank)

                def value_job(n, g, c):
                    proj_bank(n)
                    for t in range(4):
                        rows = slice((4 * c + t) * P, (4 * c + t + 1) * P)
                        for k in range(KD):
                            mm = product(pe, p_proj[:, t * P:(t + 1) * P], m.hT[:, k, rows], wkv[:, k, 1, :], k == 0, k == KD - 1)
                    mm.then_inc(v_mm, 1)

                def out_job(n, head, h, j, bank=p_proj[:, :]):
                    if n is not None:
                        proj_bank(n)
                    if j == 0:
                        pe.wait_ge(wo_ready, head + 1)
                    if j % 2 == 0:
                        pe.wait_ge(att_lo, head * 2 + 1 + j // 2)
                    for t in range(2):
                        rows = slice((2 * j + t) * P, (2 * j + t + 1) * P)
                        mm = product(pe, bank[:, t * DM:(t + 1) * DM], att[:, h % 2, rows], wo, True, True)
                    mm.then_inc(out_mm, 1)

                def scores(g, s, first, last):
                    h, i = divmod(s, NT)
                    out, rows, width = p_scores[s % 2], slice(i * P, (i + 1) * P), (i + 1) * P
                    if s in (0, 4):
                        pe.wait_ge(keys_ready, 2 * g + 1 + s // 4)
                    if first and s == 4:
                        pe.wait_ge(rope_done, 4)
                    if i in (4, 5) and not (last and h == PER_KV - 1):
                        pe.wait_ge(query_free, query(g, h, i - 4) + 1)
                    if i == 0:
                        if h == 0:
                            pe.wait_ge(rope_done, 2 if first else g * ROPES + 4)
                        else:
                            pe.wait_ge(rope_done, g * ROPES + rope(h - 1, QUERY_UNITS[1], "query", last) + 1)
                    if not (first and s < 2):
                        pe.wait_ge(exp_done, g * UNITS + s - 1)
                    for c0 in range(0, width, BANK):
                        c1 = min(c0 + BANK, width)
                        qs, ks = q[h % 2][:, rows], kT[:, c0:c1]
                        pe.matmul(out[:, c0:c1], qs.hi, ks.hi, start=True, stop=False)
                        if c1 == width:
                            pe.matmul(out[:, width - P:width], m.identb[:, :], m.maskb[:, :], start=False, stop=False)
                        pe.matmul(out[:, c0:c1], qs.hi, ks.lo, start=False, stop=False)
                        mm = pe.matmul(out[:, c0:c1], qs.lo, ks.hi, start=False, stop=True)
                    mm.then_inc(scores_mm, 1)

                def turn(g, s):
                    h, i = divmod(s, NT)
                    pe.wait_ge(exp_done, g * UNITS + s + 1)
                    for n, (b0, b1) in enumerate(blocks(i)):
                        t = tgroups_before(s) + n
                        if not (isinstance(g, int) and g == 0 and t < 2):
                            pe.wait_ge(turn_lo, g * PER_KV * TGROUPS + t - 1)
                        for b in range(b0, b1):
                            mm = pe.transpose(p_turn[t % 2][:, b - b0, :], probs[:, s % 4, b * P:(b + 1) * P], m.ident[:, :])
                        mm.then_inc(turn_mm, 1)

                def attend(g, h, c, t0, t1):
                    last_tile = 4 * c + 3
                    if t0 == 0:
                        pe.wait_ge(turn_lo, g * PER_KV * TGROUPS + h * TGROUPS + (4 if c == 0 else TGROUPS))
                        pe.wait_ge(proj_free, job(g, *VALUE_SLOTS[c], "value", isinstance(g, int) and g == 0, False) + 1)
                        if not (isinstance(g, int) and g == 0 and h == 0 and c == 0):
                            pe.wait_ge(att_lo, (g * PER_KV + h) * 2 + c)
                    for t in range(t0, t1):
                        c0 = max(0, t - 4 * c) * P
                        mm = product(pe, p_att[:, c0:BANK], v[:, t, :], pT[c][:, t, c0:BANK], t == 0, t == last_tile)
                    if t1 == last_tile + 1:
                        mm.then_inc(att_mm, 1)

                def slot(g, s, first, last):
                    h, i = divmod(s, NT)
                    if (h, i) == VALUE_SLOTS[1]:
                        value_job(job(g, h, i, "value", first, last), g, 1)
                    if s == 0 and not first:
                        pe.wait_ge(exp_done, g * UNITS - 1)
                        query_job(g * PER_KV + h + 1, 0, query_bank(0))
                    if first and s == 2:
                        pe.wait_ge(proj_free, 2)
                        pe.wait_ge(query_free, 2)
                    scores(g, s, first, last)
                    if s >= 2:
                        turn(g, s - 2)
                    elif not first:
                        turn(g - 1, UNITS + s - 2)
                    prev = (g, h - 1) if h else (g - 1, PER_KV - 1)
                    if i in (2, 3) and not (first and h == 0):
                        attend(*prev, 1, 4 * (i - 2), 4 * (i - 1))
                    if i == 6:
                        attend(g, h, 0, 0, 4)
                    if i in QUERY_UNITS and (s or first) and not (last and h == PER_KV - 1):
                        query_job(g * PER_KV + h + 1, i, query_bank(i))
                    if (h, i) in KEY_SLOTS and not last:
                        proj_bank(job(g, h, i, "key", first, last))
                        key_job(g + 1, h - 1, p_proj[:, :])
                    if (h, i) == VALUE_SLOTS[0]:
                        value_job(job(g, h, i, "value", first, last), g, 0)
                    if i >= 4 and not (first and h == 0):
                        out_job(job(g, h, i, "out", first, last), g * PER_KV + h - 1, (h - 1) % 2, i - 4)

                for c in range(CH):
                    key_job(0, c, early_banks[2 * c])
                    query_job(0, c, early_banks[2 * c + 1])
                groups(pe, slot)
                g = KV0 - 1
                turn(g, UNITS - 2)
                turn(g, UNITS - 1)
                attend(g, PER_KV - 1, 1, 0, 8)
                for j in range(4):
                    out_job(JOBS * KV0 - 4 if j == 0 else None, H0 - 1, 1, j, last_banks[j])

            @block.scalar
            def _(act):
                def copy_rope(g, k, bank):
                    r, n = g * ROPES + k, k % 2
                    act.wait_ge(rope_mm, r + 1)
                    if not (isinstance(r, int) and r < 2):
                        act.wait_ge(rope_done, r - 1)
                    half = P // 2
                    act.activation(swapped[0:half, n, :], bank[half:P, :], ACT.Copy)
                    act.activation(swapped[half:P, n, :], bank[0:half, :], ACT.Copy).then_inc(rope_copied, 1)

                def keys_hi(g, halves=range(CH)):
                    if isinstance(g, int) and g == 0:
                        act.wait_ge(rope_done, 2 * halves[-1] + 1)
                    else:
                        act.wait_ge(rope_done, g * ROPES + 2)
                        act.wait_ge(scores_mm, g * UNITS)
                    for c in halves:
                        act.activation(kT.hi[:, c * BANK:(c + 1) * BANK], k_next[:, c * BANK:(c + 1) * BANK], ACT.Copy).then_inc(key_hi, 1)

                def value_hi(g, c):
                    act.wait_ge(v_mm, g * 2 + c + 1)
                    if not (isinstance(g, int) and g == 0):
                        act.wait_ge(att_mm, g * 2 * PER_KV)
                    act.activation(v.hi[:, 4 * c:4 * c + 4, :], p_proj[:, :].rearrange("p (n d) -> p n d", n=4), ACT.Copy)\
                       .then_inc(v_hi, 1)

                def probs_hi(g, s):
                    h, i = divmod(s, NT)
                    c = i // 4
                    if i % 4 == 0 and not (isinstance(g, int) and g == 0 and h == 0):
                        act.wait_ge(att_mm, (g * PER_KV + h) * 2 - 1 + c)
                    for n, (b0, b1) in enumerate(blocks(i)):
                        t = tgroups_before(s) + n
                        act.wait_ge(turn_mm, g * PER_KV * TGROUPS + t + 1)
                        act.activation(pT[c].hi[:, b0:b1, (i % 4) * P:(i % 4 + 1) * P], p_turn[t % 2][:, 0:b1 - b0, :], ACT.Copy)\
                           .then_inc(turn_hi, 1)

                def exp(g, s, first):
                    i = s % NT
                    width = (i + 1) * P
                    act.wait_ge(max_done, g * UNITS + s + 1)
                    if not (first and s < 4):
                        before = tgroups_before(s - 3) if s >= 3 else tgroups_before(UNITS + s - 3) - PER_KV * TGROUPS
                        act.wait_ge(turn_mm, g * PER_KV * TGROUPS + before)
                    act.activation(probs[:, s % 4, 0:width], p_scores[s % 2][:, 0:width], ACT.Exp,
                                   bias=negmax[:, s % 4:s % 4 + 1], accum_out=rowsum[:, s // NT % 2, i:i + 1])\
                       .then_inc(exp_done, 1)

                def attended_hi(g, h, c):
                    n = (g * PER_KV + h) * 2 + c
                    act.wait_ge(att_mm, n + 1)
                    if c == 0 and not (isinstance(g, int) and g == 0 and h < 2):
                        act.wait_ge(out_mm, (g * PER_KV + h - 1) * 4)
                    act.activation(att.hi[:, h % 2, c * BANK:(c + 1) * BANK], p_att[:, :], ACT.Copy).then_inc(att_hi, 1)

                def slot(g, s, first, last):
                    h, i = divmod(s, NT)
                    if (h, i) == VALUE_SLOTS[1]:
                        value_hi(g, 1)
                    if first and s == 2:
                        keys_hi(0, [1])
                    if s == 0 and not first:
                        copy_rope(g, rope(h, i, "query", last), query_bank(i))
                    if s >= 2:
                        probs_hi(g, s - 2)
                    elif not first:
                        probs_hi(g - 1, UNITS + s - 2)
                    if s == UNITS - 1 and not last:
                        keys_hi(g + 1)
                    exp(g, s, first)
                    if i == 3 and not (first and h == 0):
                        attended_hi(*((g, h - 1) if h else (g - 1, PER_KV - 1)), 1)
                    if i == 6:
                        attended_hi(g, h, 0)
                    if i in QUERY_UNITS and (s or first) and not (last and h == PER_KV - 1):
                        copy_rope(g, rope(h, i, "query", last), query_bank(i))
                    if (h, i) in KEY_SLOTS and not last:
                        copy_rope(g, rope(h, i, "key", last), p_proj[:, :])
                    if (h, i) == VALUE_SLOTS[0]:
                        value_hi(g, 0)

                load_table(act, m, ACT.Exp, 0)
                for r in range(4):
                    copy_rope(0, r, early_banks[r])
                    if r == 1:
                        keys_hi(0, [0])
                groups(act, slot)
                g = KV0 - 1
                probs_hi(g, UNITS - 2)
                probs_hi(g, UNITS - 1)
                attended_hi(g, PER_KV - 1, 1)

            @block.vector
            def _(dve):
                def keys_lo(g, c):
                    cols = slice(c * BANK, (c + 1) * BANK)
                    dve.wait_ge(key_hi, 2 * g + c + 1)
                    dve.tensor_tensor(kT.lo[:, cols], k_next[:, cols], as_f32(kT.hi[:, cols]), ALU.subtract).then_inc(keys_ready, 1)

                def value_lo(g, c):
                    dve.wait_ge(v_hi, g * 2 + c + 1)
                    out = v[:, 4 * c:4 * c + 4, :]
                    dve.tensor_tensor(out.lo, p_proj[:, :].rearrange("p (n d) -> p n d", n=4), as_f32(out.hi), ALU.subtract)\
                       .then_inc(proj_free, 1)

                def cos_rope(g, k, c, bank, free):
                    r = g * ROPES + k
                    dve.wait_ge(rope_copied, r + 1)
                    if not (isinstance(r, int) and r < 2):
                        dve.wait_ge(rope_done, r - 1)
                    dve.tensor_tensor(plain[:, k % 2, :], bank, cos[:, c * BANK:(c + 1) * BANK], ALU.mult).then_inc(free, 1)

                def maximum(g, s):
                    i = s % NT
                    dve.wait_ge(scores_mm, g * UNITS + s + 1)
                    dve.tensor_reduce(negmax[:, s % 4:s % 4 + 1], p_scores[s % 2][:, 0:(i + 1) * P], AX.X, ALU.max, negate=True)\
                       .then_inc(max_done, 1)

                def inverse_sums(g, h):
                    dve.wait_ge(exp_done, g * UNITS + h * NT + NT)
                    dve.reciprocal(rinv[:, h % 2, :], rowsum[:, h % 2, :]).then_inc(inverted, 1)

                def probs_lo(g, s):
                    h, i = divmod(s, NT)
                    for n, (b0, b1) in enumerate(blocks(i)):
                        t = tgroups_before(s) + n
                        out = pT[i // 4][:, b0:b1, (i % 4) * P:(i % 4 + 1) * P]
                        dve.wait_ge(turn_hi, g * PER_KV * TGROUPS + t + 1)
                        dve.tensor_tensor(out.lo, p_turn[t % 2][:, 0:b1 - b0, :], as_f32(out.hi), ALU.subtract).then_inc(turn_lo, 1)

                def attended_lo(g, h, c):
                    out = att[:, h % 2, c * BANK:(c + 1) * BANK]
                    dve.wait_ge(att_hi, (g * PER_KV + h) * 2 + c + 1)
                    dve.tensor_tensor(out.lo, p_att[:, :], as_f32(out.hi), ALU.subtract).then_inc(att_lo, 1)

                def add_out(head, h, j, bank=p_proj[:, :]):
                    dve.wait_ge(out_mm, head * 4 + j + 1)
                    if j == 0:
                        dve.wait_ge(inverted, head + 1)
                    for t in range(2):
                        rows = m.x[:, 2 * j + t, :]
                        ins = dve.scalar_tensor_tensor(out=rows, in0=bank[:, t * DM:(t + 1) * DM], scalar=rinv[:, h % 2, 2 * j + t:2 * j + t + 1],
                                                       in1=rows, op0=ALU.mult, op1=ALU.add)
                    ins.then_inc(proj_free, 1)

                def slot(g, s, first, last):
                    h, i = divmod(s, NT)
                    if (h, i) == VALUE_SLOTS[1]:
                        value_lo(g, 1)
                    if first and s == 2:
                        keys_lo(0, 1)
                    if s == 0 and not first:
                        cos_rope(g, rope(h, i, "query", last), 0, query_bank(0), query_free)
                    maximum(g, s)
                    prev = (g, h - 1) if h else (g - 1, PER_KV - 1)
                    if i == 2 and not (first and h == 0):
                        inverse_sums(*prev)
                    if s >= 2:
                        probs_lo(g, s - 2)
                    elif not first:
                        probs_lo(g - 1, UNITS + s - 2)
                    if i == 3 and not (first and h == 0):
                        attended_lo(*prev, 1)
                    if i == 6:
                        attended_lo(g, h, 0)
                    if i in QUERY_UNITS and (s or first) and not (last and h == PER_KV - 1):
                        cos_rope(g, rope(h, i, "query", last), i, query_bank(i), query_free)
                    if (h, i) in KEY_SLOTS and not last:
                        cos_rope(g, rope(h, i, "key", last), h - 1, p_proj[:, :], proj_free)
                    if (h, i) == VALUE_SLOTS[0]:
                        value_lo(g, 0)
                    if i >= 4 and not (first and h == 0):
                        add_out(g * PER_KV + h - 1, h - 1, i - 4)
                    if s == UNITS - 1 and not last:
                        for c in range(CH):
                            keys_lo(g + 1, c)

                dve.wait_ge(tables_in, 32)
                for r in range(4):
                    cos_rope(0, r, r // 2, early_banks[r], (proj_free, query_free)[r % 2])
                    if r == 1:
                        keys_lo(0, 0)
                groups(dve, slot)
                g = KV0 - 1
                inverse_sums(g, PER_KV - 1)
                probs_lo(g, UNITS - 2)
                probs_lo(g, UNITS - 1)
                attended_lo(g, PER_KV - 1, 1)
                for j in range(4):
                    add_out(H0 - 1, PER_KV - 1, j, last_banks[j])

            @block.gpsimd
            def _(pool):
                def turn_sum(rk, free, n, c, dst):
                    r, b = rk[0] * ROPES + rk[1], rk[1] % 2
                    cols = slice(c * BANK, (c + 1) * BANK)
                    pool.wait_ge(rope_copied, r + 1)
                    pool.tensor_tensor(swapped[:, b, :], swapped[:, b, :], sin[:, cols], ALU.mult).then_inc(rope_turned, 1)
                    pool.wait_ge(free, n + 1)
                    pool.wait_ge(rope_turned, r + 1)
                    return pool.tensor_tensor(dst, plain[:, b, :], swapped[:, b, :], ALU.add)

                def key_turn(r, n, g, c):
                    if not (isinstance(g, int) and g == 0):
                        pool.wait_ge(keys_ready, 2 * g)
                    turn_sum(r, proj_free, n, c, k_next[:, c * BANK:(c + 1) * BANK]).then_inc(rope_done, 1)

                def query_turn(r, queries, g, h, c, free=False):
                    turned = plain[:, r[1] % 2, :]
                    turn_sum(r, query_free, queries, c, turned).then_inc(rope_sum, 1)
                    out = q[h % 2][:, c * BANK:(c + 1) * BANK]
                    if not free:
                        pool.wait_ge(scores_mm, g * UNITS + (h - 1) * NT)
                    pool.wait_ge(rope_sum, queries + 1)
                    alone(pool)
                    pool.tensor_scalar(out.hi, turned, 1.0, 1.0, ALU.mult, ALU.mult).then_inc(query_hi, 1)
                    pool.wait_ge(query_hi, queries + 1)
                    pool.tensor_tensor(out.lo, turned, as_f32(out.hi), ALU.subtract).then_inc(rope_done, 1)

                def split_o(n, head):
                    pool.wait_ge(wo_loaded, head * 16 + 16)
                    pool.tensor_tensor(wo_in[:, :], wo_in[:, :], m.gate[:, 0, 0, :], ALU.mult).then_inc(wo_gated, 1)
                    if not (isinstance(head, int) and head == 0):
                        pool.wait_ge(out_mm, head * 4)
                    pool.wait_ge(wo_gated, head + 1)
                    split_weights(pool, n, wo_in[:, :], wo, wo_ready)

                def slot(g, s, first, last):
                    h, i = divmod(s, NT)
                    head = g * PER_KV + h
                    if i in QUERY_UNITS and not (last and h == PER_KV - 1):
                        query_turn((g, rope(h, i, "query", last)), query(g, h, i), g + (h + 1) // PER_KV, (h + 1) % PER_KV, i, first and h == 0)
                    if (h, i) in KEY_SLOTS and not last:
                        key_turn((g, rope(h, i, "key", last)), job(g, h, i, "key", first, last), g + 1, h - 1)
                    if i == 0 and not (first and h == 0):
                        split_o(splits(g, h, 0, first, last), head - 1)
                    if i == 2 and not (last and h >= 2):
                        split_q(pool, splits(g, h, 1, first, last), head + 2, g * ROPES + rope(h, QUERY_UNITS[1], "query", last) + 1)
                    if (h, i) == VALUE_SLOTS[1] and not last:
                        split_kv(pool, splits(g, h, 2, first, last), g + 1)

                def splits(g, h, kind, first, last):
                    order = [(hh, kk) for hh in range(PER_KV) for kk in range(3)
                             if not (kk == 0 and first and hh == 0) and not (kk == 1 and last and hh >= 2)
                             and not (kk == 2 and (hh != 0 or last))]
                    return (3 if first else g * 9 + 2) + order.index((h, kind))

                pool.wait_ge(tables_in, 32)
                for c in range(CH):
                    key_turn((0, 2 * c), c, 0, c)
                    query_turn((0, 2 * c + 1), c, 0, 0, c, True)
                    if c == 0:
                        split_q(pool, 2, 1, 4)
                groups(pool, slot)
                split_o(KV0 * 9 - 1, H0 - 1)


def ffn0(nc, a, m, sems, sb, split):
    with ExitStack() as ctx:
        def buf(name, shape, dt=F32):
            return sb("ff0_" + name, shape, dt, ctx)

        def pair(name, shape):
            return split("ff0_" + name, shape, ctx)

        def sem(name):
            return sems("ff0_" + name)

        wg_in, wu_in, wd_in = (m.staging[:, n * 2048:(n + 1) * 2048] for n in range(3))
        wg, wu, wd = pair("wg", [P, KD, I0]), pair("wu", [P, KD, I0]), pair("wd", [P, I0 // P, DM])
        xn = [buf(f"xn{n}", [P, DM]) for n in range(2)]
        h32 = buf("h32", [P, KD, P])
        hx = [pair(f"hx{n}", [P, KD, P]) for n in range(2)]
        sg, absh = buf("sg", [P, I0]), buf("absh", [P, I0])
        h = [buf(f"h{n}", [P, I0]) for n in range(2)]
        cx, cy, cz, cs, ct = (buf(n, [P, 2, I0 // 4], BF16) for n in ("cx", "cy", "cz", "cs", "ct"))
        wins = buf("wins", [P, 4, I0 // 4], BF16)
        hsT = pair("hsT", [P, I0 // P, P])
        p_gate, p_up = (ctx.enter_context(nc.psum_tensor(f"ff0_{n}", [P, I0], F32)) for n in ("gate", "up"))
        p_turn = [ctx.enter_context(nc.psum_tensor(f"ff0_turn{n}", [P, 4, P], F32)) for n in range(2)]
        p_x = ctx.enter_context(nc.psum_tensor("ff0_x", [P, BANK], F32))
        p_y = ctx.enter_context(nc.psum_tensor("ff0_y", [P, BANK], F32))
        sqrt_in, sqrt_out, chain_sem = sem("sqrt_in"), sem("sqrt_out"), sem("chain")
        w_hi, wg_ready, wu_ready, wu_ready_pool, wd_gated, wd_hi, wd_ready = (sem(n) for n in ("w_hi", "wg_ready", "wu_ready", "wu_ready_pool", "wd_gated", "wd_hi", "wd_ready"))
        normed, x_mm, h32_done, hx_hi, hx_ready = (sem(n) for n in ("normed", "x_mm", "h32_done", "hx_hi", "hx_ready"))
        gate_mm, up_mm, silu_done, mul_done, abs_done = (sem(n) for n in ("gate_mm", "up_mm", "silu_done", "mul_done", "abs_done"))
        compared, summed, won, sparse = (sem(n) for n in ("compared", "summed", "won", "sparse"))
        turn_mm, turn_hi, turn_lo, down_mm, added = (sem(n) for n in ("turn_mm", "turn_hi", "turn_lo", "down_mm", "added"))

        OPEN = 1

        def zero(t):
            return isinstance(t, int) and t == 0

        def tiles(engine, step):
            step(0, 0)
            step(1, 1)
            with engine.Fori(0, (NT - 4) // 2) as r:
                step(r * 2 + 2, 0)
                step(r * 2 + 3, 1)
            step(NT - 2, 0)
            step(NT - 1, 1)

        def ahead(t):
            return not isinstance(t, int) or t + 2 < NT

        def behind(t, n):
            return not isinstance(t, int) or t >= n

        with nc.Block() as block:
            @block.tensor
            def _(pe):
                def turn_x(t, b):
                    pe.wait_ge(normed, t + 1)
                    if not zero(t):
                        pe.wait_ge(h32_done, t)
                    for k in range(KD):
                        mm = pe.transpose(p_x[:, k * P:(k + 1) * P], xn[b][:, k * P:(k + 1) * P], m.ident[:, :])
                    mm.then_inc(x_mm, 1)

                def wide(t, b, w, out, free, done):
                    if not zero(t):
                        pe.wait_ge(free, t)
                    for c in range(I0 // BANK):
                        cols = slice(c * BANK, (c + 1) * BANK)
                        for k in range(KD):
                            mm = product(pe, out[:, cols], hx[b][:, k, :], w[:, k, cols], k == 0, k == KD - 1)
                    mm.then_inc(done, 1)

                def turn_h(t, b):
                    pe.wait_ge(sparse, t * 4 + 4)
                    pe.wait_ge(turn_lo, OPEN + t * 2)
                    for n in range(2):
                        for j in range(4):
                            c = 4 * n + j
                            mm = pe.transpose(p_turn[n][:, j, :], h[b][:, c * P:(c + 1) * P], m.ident[:, :])
                        mm.then_inc(turn_mm, 1)

                def down(t):
                    if zero(t):
                        pe.wait_ge(wd_ready, 1)
                    pe.wait_ge(added, OPEN + t)
                    for c in range(I0 // P):
                        if c % 4 == 0:
                            pe.wait_ge(turn_lo, OPEN + t * 2 + 1 + c // 4)
                        mm = product(pe, p_y[:, 0:DM], hsT[:, c, :], wd[:, c, :], c == 0, c == I0 // P - 1)
                    mm.then_inc(down_mm, 1)

                def step(t, b):
                    pe.wait_ge(hx_ready, t + 1)
                    if zero(t):
                        pe.wait_ge(wg_ready, KD)
                    wide(t, b, wg, p_gate, silu_done, gate_mm)
                    if behind(t, 2):
                        down(t - 2)
                    if zero(t):
                        pe.wait_ge(wu_ready, 1)
                        pe.wait_ge(wu_ready_pool, 1)
                    wide(t, b, wu, p_up, mul_done, up_mm)
                    if behind(t, 1):
                        turn_h(t - 1, 1 - b)
                    if ahead(t):
                        turn_x(t + 2, b)

                pe.sem_inc(turn_mm, OPEN)
                pe.sem_inc(down_mm, OPEN)
                turn_x(0, 0)
                turn_x(1, 1)
                tiles(pe, step)
                down(NT - 2)
                turn_h(NT - 1, 1)
                down(NT - 1)

            @block.scalar
            def _(act):
                for n, (w, w_in) in enumerate(((wg, wg_in), (wu, wu_in))):
                    act.wait_ge(m.staged, 16 * (n + 1))
                    for k in range(KD):
                        act.activation(w.hi[:, k, :], w_in[:, k * I0:(k + 1) * I0], ACT.Copy).then_inc(w_hi, 1)
                    if n == 0:
                        row_stats_sqrt(act, m, sqrt_in, sqrt_out)

                def scale_shift(t):
                    act.wait_ge(x_mm, t + 1)
                    if not zero(t):
                        act.wait_ge(hx_ready, t)
                    for k in range(KD):
                        ins = act.activation(h32[:, k, :], p_x[:, k * P:(k + 1) * P], ACT.Identity,
                                             scale=m.modcol[:, 0, 8 + k:9 + k], bias=m.modcol[:, 0, 6 + k:7 + k])
                    ins.then_inc(h32_done, 1)

                def silu(t):
                    act.wait_ge(gate_mm, t + 1)
                    if not zero(t):
                        act.wait_ge(mul_done, t)
                    act.activation(sg[:, :], p_gate[:, :], ACT.Silu).then_inc(silu_done, 1)

                def turned_hi(t):
                    for n in range(2):
                        act.wait_ge(turn_mm, OPEN + t * 2 + n + 1)
                        if n == 0:
                            act.wait_ge(down_mm, OPEN + t)
                        act.activation(hsT.hi[:, 4 * n:4 * n + 4, :], p_turn[n][:, :, :], ACT.Copy).then_inc(turn_hi, 1)

                def magnitude(t, b):
                    act.wait_ge(mul_done, t + 1)
                    if not zero(t):
                        act.wait_ge(compared, t * 3)
                    act.activation(absh[:, :], h[b][:, :], ACT.Abs).then_inc(abs_done, 1)

                def step(t, b):
                    silu(t)
                    if behind(t, 1):
                        turned_hi(t - 1)
                    magnitude(t, b)
                    if ahead(t):
                        scale_shift(t + 2)

                scale_shift(0)
                scale_shift(1)
                tiles(act, step)
                turned_hi(NT - 1)

            @block.vector
            def _(dve):
                dve.sem_inc(turn_lo, OPEN)
                dve.sem_inc(added, OPEN)
                chain = Chain(dve, chain_sem)

                def split_low(n, w, w_in, k, ready):
                    dve.wait_ge(w_hi, KD * n + k + 1)
                    dve.tensor_tensor(w.lo[:, k, :], w_in[:, k * I0:(k + 1) * I0], as_f32(w.hi[:, k, :]), ALU.subtract).then_inc(ready, 1)

                def gate_low():
                    for k in range(KD):
                        split_low(0, wg, wg_in, k, wg_ready)

                row_stats(dve, m, chain, sqrt_in, sqrt_out, gate_low)

                def norm(t, b):
                    if not (isinstance(t, int) and t < 2):
                        dve.wait_ge(x_mm, t - 1)
                    dve.tensor_scalar(xn[b][:, :], m.x[:, bass.ds(t, 1), :], m.meanvar[:, bass.ds(t, 1), 0], m.rstd[:, bass.ds(t, 1)],
                                      ALU.subtract, ALU.mult).then_inc(normed, 1)

                def multiply(t, b):
                    dve.wait_ge(silu_done, t + 1)
                    dve.wait_ge(up_mm, t + 1)
                    if not (isinstance(t, int) and t < 2):
                        dve.wait_ge(turn_mm, OPEN + t * 2 - 2)
                    dve.tensor_tensor(h[b][:, :], sg[:, :], p_up[:, :], ALU.mult).then_inc(mul_done, 1)

                def sparsify(t, b):
                    four = absh[:, :].rearrange("p (g e) -> p g e", e=4)

                    def by_group(plane):
                        return plane[:, :, :].rearrange("p e g -> p g e")

                    dve.wait_ge(abs_done, t + 1)
                    dve.tensor_tensor(by_group(cx), four[:, :, 0:2], four[:, :, 2:4], ALU.is_ge).then_inc(compared, 1)
                    dve.tensor_tensor(by_group(cy), four[:, :, 0:2], four[:, :, 3:1:-1], ALU.is_ge).then_inc(compared, 1)
                    dve.tensor_tensor(by_group(cz), four[:, :, 0:4:2], four[:, :, 1:4:2], ALU.is_ge).then_inc(compared, 1)
                    dve.wait_ge(compared, t * 3 + 3)
                    dve.tensor_tensor(cs[:, :, :], cx[:, :, :], cy[:, :, :], ALU.add).then_inc(summed, 1)
                    dve.tensor_tensor(ct[:, :, :], cx[:, :, :], cy[:, 1::-1, :], ALU.add).then_inc(summed, 1)
                    dve.wait_ge(summed, t * 2 + 2)
                    dve.tensor_tensor(wins[:, 0, :], cs[:, 0, :], cz[:, 0, :], ALU.add).then_inc(won, 1)
                    dve.tensor_tensor(wins[:, 1, :], cs[:, 1, :], cz[:, 0, :], ALU.subtract).then_inc(won, 1)
                    dve.tensor_tensor(wins[:, 2, :], cz[:, 1, :], ct[:, 0, :], ALU.subtract).then_inc(won, 1)
                    dve.tensor_tensor(wins[:, 3, :], ct[:, 1, :], cz[:, 1, :], ALU.add).then_inc(won, 1)
                    dve.wait_ge(won, t * 4 + 4)
                    kept = h[b][:, :].rearrange("p (g e) -> p g e", e=4)
                    for e, (test, bound) in enumerate(((ALU.is_ge, 2.0), (ALU.is_ge, 1.0), (ALU.is_ge, 0.0), (ALU.is_le, 1.0))):
                        dve.scalar_tensor_tensor(out=kept[:, :, e], in0=wins[:, e, :], scalar=bound, in1=kept[:, :, e],
                                                 op0=test, op1=ALU.mult).then_inc(sparse, 1)

                def turned_lo(t):
                    for n in range(2):
                        out = hsT[:, 4 * n:4 * n + 4, :]
                        dve.wait_ge(turn_hi, t * 2 + n + 1)
                        dve.tensor_tensor(out.lo, p_turn[n][:, :, :], as_f32(out.hi), ALU.subtract).then_inc(turn_lo, 1)

                def add(t):
                    dve.wait_ge(down_mm, OPEN + t + 1)
                    rows = m.x[:, bass.ds(t, 1), :].rearrange("p o d -> p (o d)")
                    dve.tensor_tensor(rows, p_y[:, 0:DM], rows, ALU.add).then_inc(added, 1)

                def step(t, b):
                    if ahead(t):
                        norm(t + 2, b)
                    if behind(t, 2):
                        add(t - 2)
                    multiply(t, b)
                    if behind(t, 1):
                        turned_lo(t - 1)
                    sparsify(t, b)

                norm(0, 0)
                norm(1, 1)
                split_low(1, wu, wu_in, 0, wu_ready)
                tiles(dve, step)
                add(NT - 2)
                turned_lo(NT - 1)
                dve.wait_ge(added, OPEN + NT - 1)
                for n in range(NT - 1):
                    dve.bn_stats(m.stats[:, n, :], m.x[:, n, :])
                add(NT - 1)
                dve.wait_ge(added, OPEN + NT)
                dve.bn_stats(m.stats[:, NT - 1, :], m.x[:, NT - 1, :])

            @block.gpsimd
            def _(pool):
                def split_x(t, b):
                    pool.wait_ge(h32_done, t + 1)
                    if not (isinstance(t, int) and t < 2):
                        pool.wait_ge(up_mm, t - 1)
                    pool.nop(nofuse=True)
                    pool.tensor_scalar(hx[b].hi[:, :, :], h32[:, :, :], 1.0, 1.0, ALU.mult, ALU.mult).then_inc(hx_hi, 1)
                    pool.wait_ge(hx_hi, t + 1)
                    pool.tensor_tensor(hx[b].lo[:, :, :], h32[:, :, :], as_f32(hx[b].hi[:, :, :]), ALU.subtract).then_inc(hx_ready, 1)

                pool.wait_ge(w_hi, 2 * KD)
                pool.tensor_tensor(wu.lo[:, 1, :], wu_in[:, I0:], as_f32(wu.hi[:, 1, :]), ALU.subtract).then_inc(wu_ready_pool, 1)
                split_x(0, 0)
                split_x(1, 1)
                pool.wait_ge(m.staged, 48)
                for c in range(I0 // P):
                    rows = wd_in[:, c * DM:(c + 1) * DM]
                    pool.tensor_tensor(rows, rows, m.gate[:, 0, 1, :], ALU.mult).then_inc(wd_gated, 1)
                pool.wait_ge(wd_gated, I0 // P)
                flat = wd("p c d -> p (c d)")
                pool.tensor_scalar(flat.hi, wd_in, 1.0, 1.0, ALU.mult, ALU.mult).then_inc(wd_hi, 1)
                pool.wait_ge(wd_hi, 1)
                pool.tensor_tensor(flat.lo, wd_in, as_f32(flat.hi), ALU.subtract).then_inc(wd_ready, 1)

                with pool.Fori(0, NT // 2 - 1) as r:
                    split_x(r * 2 + 2, 0)
                    split_x(r * 2 + 3, 1)


def attention1(nc, a, m, sems, sb, split):
    HS = H1 * NT
    ctx = ExitStack()
    with ctx:
        def buf(name, shape, dt=F32, c=ctx):
            return sb("at1_" + name, shape, dt, c)

        def sem(name):
            return sems("at1_" + name)

        h_row = buf("h_row", [P, NT, DM])
        gT = m.hT
        wq = split("at1_wq", [P, KD, H1 * D1], ctx)
        pT = [split(f"at1_pT{n}", [P, NT, BANK], ctx) for n in range(2)]
        room = pT[1].lo.rearrange("p t j -> p (t j)")
        wk = Split(room[:, 0:512], room[:, 512:1024])("p (k g a d) -> p k g a d", k=KD, g=G1, a=2)
        wv = Split(room[:, 1024:1280], room[:, 1280:1536])("p (k n) -> p k n", k=KD)
        wo = split("at1_wo", [P, H1, DM], ctx)
        norm_col = buf("norm_col", [P, 3, KD])
        wo_in = m.staging1[:, 1024:2048].rearrange("p (h n) -> p h n", h=H1)
        q = [buf(f"q{n}", [P, S], F32R) for n in range(2)]
        khi, klo = ([buf(f"{n}{g}", [P, S], F32R) for g in range(G1)] for n in ("khi", "klo"))
        v = [buf(f"v{g}", [P, NT, 2, D1], F32R) for g in range(G1)]
        staging = m.staging1
        wq_in = staging[:, 0:512].rearrange("p (k n) -> p k n", k=KD)
        wk_in = staging[:, 512:768].rearrange("p (k n) -> p k n", k=KD)
        wv_in = staging[:, 768:1024].rearrange("p (k n) -> p k n", k=KD)

        with ExitStack() as c1:
            g_row = buf("g_row", [P, NT, DM], F32, c1)
            squares, root, inv = (buf(n, [P, NT], F32, c1) for n in ("squares", "root", "inv"))
            gate_w_in = buf("gate_w_in", [P, KD, NE], F32, c1)
            banks = [c1.enter_context(nc.psum_tensor(f"at1_bank{n}", [P, BANK], F32)) for n in range(4)]
            small_in, sqrt_in, sqrt_out, centered, h_done, squared, rooted, inverted, scaled, scaled_act, turned, turned_hi, chain_sem, w_hi = (
                sem(n) for n in ("small_in", "sqrt_in", "sqrt_out", "centered", "h_done", "squared", "rooted", "inverted", "scaled", "scaled_act",
                                 "row_turned", "row_hi", "chain", "w_hi"))
            pool_h = sem("pool_h")
            POOL_TILES = (5, 6, 7)
            quarters = [(k, slice(half * BANK, (half + 1) * BANK)) for half in range(2) for k in range(KD)]
            with nc.Block() as block:
                @block.sync
                def _(sp):
                    for n in range(2):
                        sp.dma_start(norm_col[:, n, :], a[("L1_attn_norm_scale", "L1_attn_split_scale")[n]]).then_inc(small_in, 16)
                    with nc.allow_non_contiguous_dma(reason="seven columns"):
                        sp.dma_start(gate_w_in[:, :, :], a["L1_ffn_gate_w"].rearrange("(k p) e -> p k e", p=P)).then_inc(m.gate_in, 16)
                        sp.dma_start(m.expert_bias[:, :], a["L1_ffn_expert_bias"]).then_inc(m.gate_in, 16)
                    w1 = m.staging[:, 0:4096].rearrange("p (e k n) -> p e k n", e=8, k=KD)
                    w2 = m.staging[:, 4096:6144].rearrange("p (e n) -> p e n", e=8)
                    for e in range(8):
                        src1 = a["L1_ffn_shared_w1"][0] if e == 0 else a["L1_ffn_routed_w1"][e - 1]
                        sp.dma_start(w1[:, e, :, :], src1.rearrange("(k p) n -> p k n", p=P)).then_inc(m.staged, 16)
                    sp.dma_start(w2[:, 0, :], a["L1_ffn_shared_w2"][0]).then_inc(m.staged, 16)
                    sp.dma_start(w2[:, 1:8, :], a["L1_ffn_routed_w2"].rearrange("e p n -> p e n")).then_inc(m.staged, 16)

                @block.scalar
                def _(act):
                    row_stats_sqrt(act, m, sqrt_in, sqrt_out)
                    for n in range(NT):
                        if n in POOL_TILES:
                            act.wait_ge(pool_h, 2 * (POOL_TILES.index(n) + 1))
                        else:
                            act.wait_ge(h_done, n + 1)
                        act.activation(g_row[:, n, :], h_row[:, n, :], ACT.Square, accum_out=squares[:, n:n + 1]).then_inc(squared, 1)
                    act.wait_ge(squared, NT)
                    act.activation(root[:, :], squares[:, :], ACT.Sqrt, scale=1.0 / DM).then_inc(rooted, 1)
                    act.wait_ge(m.staged1, 80)
                    act.activation(wq.hi, wq_in, ACT.Copy).then_inc(w_hi, 1)
                    act.wait_ge(inverted, 1)
                    for n in range(4, NT):
                        act.activation(g_row[:, n, :], h_row[:, n, :], ACT.Copy, scale=inv[:, n:n + 1]).then_inc(scaled_act, 1)
                    for n, (k, cols) in enumerate(quarters):
                        act.wait_ge(turned, n + 1)
                        act.activation(gT.hi[:, k, cols], banks[n][:, :], ACT.Copy, scale=norm_col[:, 2, k:k + 1]).then_inc(turned_hi, 1)
                    for n in range(2):
                        act.activation(wk.hi[:, :, :, n, :], wk_in.rearrange("p k (g d) -> p k g d", d=D1), ACT.Copy).then_inc(w_hi, 1)
                    act.activation(wv.hi, wv_in, ACT.Copy).then_inc(w_hi, 1)

                @block.tensor
                def _(pe):
                    for q, (k, cols) in enumerate(quarters):
                        half = q // KD
                        pe.wait_ge(scaled_act if half else scaled, 4)
                        for n in range(4):
                            mm = pe.transpose(banks[q][:, n * P:(n + 1) * P], g_row[:, 4 * half + n, k * P:(k + 1) * P], m.ident[:, :])
                        mm.then_inc(turned, 1)

                @block.vector
                def _(dve):
                    chain = Chain(dve, chain_sem)
                    def center(tiles):
                        for n in tiles:
                            dve.scalar_tensor_tensor(out=h_row[:, n, :], in0=m.x[:, n, :], scalar=m.meanvar[:, n, 0:1], in1=m.mod_row[:, 1, :],
                                                     op0=ALU.subtract, op1=ALU.mult).then_inc(centered, 1)

                    own = [n for n in range(NT) if n not in POOL_TILES]
                    row_stats(dve, m, chain, sqrt_in, sqrt_out, lambda: center(POOL_TILES), begun=True)
                    center(own)
                    dve.wait_ge(centered, NT)
                    for n in own:
                        dve.scalar_tensor_tensor(out=h_row[:, n, :], in0=h_row[:, n, :], scalar=m.rstd[:, n:n + 1], in1=m.mod_row[:, 0, :],
                                                 op0=ALU.mult, op1=ALU.add).then_inc(h_done, 1)
                    dve.wait_ge(small_in, 32)
                    chain.step(dve.tensor_tensor(norm_col[:, 2, :], norm_col[:, 0, :], norm_col[:, 1, :], ALU.mult))
                    dve.wait_ge(m.gate_in, 32)
                    chain.run(dve.tensor_copy(m.gate_w.hi, gate_w_in[:, :, :]))
                    dve.tensor_tensor(m.gate_w.lo, gate_w_in[:, :, :], as_f32(m.gate_w.hi), ALU.subtract)
                    dve.wait_ge(rooted, 1)
                    chain.run(dve.tensor_scalar(inv[:, :], root[:, :], RMS_EPS, None, ALU.add))
                    dve.reciprocal(inv[:, :], inv[:, :]).then_inc(inverted, 1)
                    dve.wait_ge(inverted, 1)
                    for n in range(4):
                        dve.tensor_scalar(g_row[:, n, :], h_row[:, n, :], inv[:, n:n + 1], None, ALU.mult).then_inc(scaled, 1)
                    for n, (k, cols) in enumerate(quarters):
                        dve.wait_ge(turned_hi, n + 1)
                        dve.scalar_tensor_tensor(out=gT.lo[:, k, cols], in0=banks[n][:, :], scalar=norm_col[:, 2, k:k + 1],
                                                 in1=as_f32(gT.hi[:, k, cols]), op0=ALU.mult, op1=ALU.subtract)

                @block.gpsimd
                def _(pool):
                    for t, n in enumerate(POOL_TILES):
                        pool.wait_ge(centered, len(POOL_TILES) + 1)
                        pool.tensor_scalar(h_row[:, n, :], h_row[:, n, :], m.rstd[:, n:n + 1], 1.0, ALU.mult, ALU.mult).then_inc(pool_h, 1)
                        pool.wait_ge(pool_h, 2 * t + 1)
                        pool.tensor_tensor(h_row[:, n, :], h_row[:, n, :], m.mod_row[:, 0, :], ALU.add).then_inc(pool_h, 1)
                    pool.wait_ge(w_hi, 1)
                    pool.tensor_tensor(wq.lo, wq_in, as_f32(wq.hi), ALU.subtract)
                    for n in range(2):
                        pool.wait_ge(w_hi, n + 2)
                        pool.tensor_tensor(wk.lo[:, :, :, n, :], wk_in.rearrange("p k (g d) -> p k g d", d=D1), as_f32(wk.hi[:, :, :, n, :]), ALU.subtract)
                    pool.wait_ge(w_hi, 4)
                    pool.tensor_tensor(wv.lo, wv_in, as_f32(wv.hi), ALU.subtract)

        more_probs = buf("probs", [P, 2, S])
        probs = [staging[:, 0:S]] + [more_probs[:, n, :] for n in range(2)] + [staging[:, S:2 * S]]
        negmax, rowsum, rinv = buf("negmax", [P, 4]), buf("rowsum", [P, 4]), buf("rinv", [P, 4])
        att = split("at1_att", [P, 2, S], ctx)
        p_scores = [ctx.enter_context(nc.psum_tensor(f"at1_scores{n}", [P, S], F32)) for n in range(2)]
        p_turn = [ctx.enter_context(nc.psum_tensor(f"at1_turn{n}", [P, 4, P], F32)) for n in range(2)]
        p_att = ctx.enter_context(nc.psum_tensor("at1_att_sum", [P, BANK], F32))
        p_proj = ctx.enter_context(nc.psum_tensor("at1_proj", [P, BANK], F32))
        job_mm, job_hi, proj_free = sem("job_mm"), sem("job_hi"), sem("proj_free")
        scores_mm, max_done, exp_done, rinv_done, normed = (sem(n) for n in ("scores_mm", "max_done", "exp_done", "rinv_done", "normed"))
        turn_mm, turn_hi, turn_lo = sem("turn_mm"), sem("turn_hi"), sem("turn_lo")
        att_mm, att_hi, att_lo = sem("att_mm"), sem("att_hi"), sem("att_lo")
        out_mm, wo_ready, bias_done, residual = sem("out_mm"), sem("wo_ready"), sem("bias_done"), sem("residual")
        SCALE = float(D1) ** -0.5

        jobs = [("k", 0, 0), ("k", 0, 1), ("qq", 0, 0), ("qq", 0, 1), ("v", 0, 0), ("v", 0, 1)]
        first = [p_proj[:, :], p_att[:, :], p_scores[1][:, 0:BANK], p_scores[1][:, BANK:S]]
        first += [p_turn[n][:, :, :].rearrange("p a b -> p (a b)") for n in range(2)]
        jobs += [("k", 1, 0), ("k", 1, 1), ("q", 2, 0), ("q", 2, 1), ("q", 3, 0), ("q", 3, 1)]
        first_slot = dict(zip(jobs[4:], (-1, 1, 3, 5, 10, 13, 17, 19)))

        def bank_of(n):
            return first[n] if n < len(first) else p_proj[:, :]

        def jobs_of(slot):
            return [(n, job) for n, job in enumerate(jobs) if first_slot.get(job, -1) == slot]

        FIRST_RESIDUAL = 5
        FIRST_GATED = 21
        LAG = 3
        ATT = LAG + 4
        out_slots = {ATT + 16: (0,), ATT + 17: (1,), ATT + 18: (2,), ATT + 19: (3,)}

        def out_bank(pair_index, j):
            return (p_proj[:, :], p_scores[0][:, 0:BANK], p_scores[0][:, BANK:S], p_scores[1][:, 0:BANK])[j if pair_index else 0]

        with nc.Block() as block:
            @block.tensor
            def _(pe):
                def project(n, kind, index, c):
                    bank = bank_of(n)
                    if n >= len(first):
                        pe.wait_ge(proj_free, n)
                    if kind == "v":
                        for t in range(4):
                            rows = slice((4 * c + t) * P, (4 * c + t + 1) * P)
                            for k in range(KD):
                                mm = product(pe, bank[:, t * P:(t + 1) * P], gT[:, k, rows], wv[:, k, :], k == 0, k == KD - 1)
                    else:
                        width = D1 if kind == "q" else P
                        for k in range(KD):
                            w = wk[:, k, index, :, :]("p a d -> p (a d)") if kind == "k" else wq[:, k, index * D1:index * D1 + width]
                            mm = product(pe, bank[0:width, :], w, gT[:, k, c * BANK:(c + 1) * BANK], k == 0, k == KD - 1)
                    mm.then_inc(job_mm, 1)

                def scores(s):
                    h, i = divmod(s, NT)
                    g = h // (H1 // G1)
                    if i == 0:
                        pe.wait_ge(proj_free, jobs.index(("q", h, 1) if h >= 2 else ("qq", 0, 1)) + 1)
                        pe.wait_ge(proj_free, jobs.index(("k", g, 1)) + 1)
                    if s >= 2:
                        pe.wait_ge(exp_done, s - 1)
                    for c in range(2):
                        cols = slice(c * BANK, (c + 1) * BANK)
                        rows = q[h % 2][:, i * P:(i + 1) * P]
                        pe.matmul(p_scores[s % 2][:, cols], rows, khi[g][:, cols], start=True, stop=False)
                        mm = pe.matmul(p_scores[s % 2][:, cols], rows, klo[g][:, cols], start=False, stop=True)
                    mm.then_inc(scores_mm, 1)

                def turn(s):
                    pe.wait_ge(normed, s + 1)
                    if s == 0:
                        pe.wait_ge(proj_free, len(first))
                    for n in range(2):
                        if s:
                            pe.wait_ge(turn_lo, 2 * s - 1 + n)
                        for b in range(4):
                            mm = pe.transpose(p_turn[n][:, b, :], probs[s % 4][:, (4 * n + b) * P:(4 * n + b + 1) * P], m.ident[:, :])
                        mm.then_inc(turn_mm, 1)

                def attend(chunk, part):
                    g = chunk // 2 // (H1 // G1)
                    if part == 0:
                        pe.wait_ge(turn_lo, 8 * chunk + 8)
                        if chunk:
                            pe.wait_ge(att_lo, chunk)
                    for t in range(2 * part, 2 * part + 2):
                        values = v[g][:, t, :, :].rearrange("p a d -> p (a d)")
                        pe.matmul(p_att[:, :], values, pT[chunk % 2].hi[:, t, :], start=(t == 0), stop=False)
                        mm = pe.matmul(p_att[:, :], values, pT[chunk % 2].lo[:, t, :], start=False, stop=(t == NT - 1))
                    if part == 3:
                        mm.then_inc(att_mm, 1)

                def out_job(pair_index, j):
                    bank = out_bank(pair_index, j)
                    pe.wait_ge(proj_free, len(jobs) + (4 if pair_index else j))
                    pe.wait_ge(att_lo, 4 * pair_index + 4)
                    pe.wait_ge(wo_ready, 1)
                    for n in range(2):
                        rows = slice((2 * j + n) * P, (2 * j + n + 1) * P)
                        for h in range(2):
                            mm = product(pe, bank[:, n * DM:(n + 1) * DM], att[:, h, rows], wo[:, 2 * pair_index + h, :],
                                         h == 0, h == 1)
                    mm.then_inc(out_mm, 1)

                for n, job in jobs_of(-1):
                    project(n, *job)
                for s in range(HS + ATT):
                    if s < HS:
                        scores(s)
                    if LAG <= s < HS + LAG:
                        turn(s - LAG)
                    if s >= ATT:
                        attend((s - ATT) // 4, (s - ATT) % 4)
                    for n, job in jobs_of(s):
                        project(n, *job)
                    for j in out_slots.get(s, ()):
                        out_job(0, j)
                for j in range(4):
                    out_job(1, j)

            @block.scalar
            def _(act):
                def job_high(n, kind, index, c):
                    act.wait_ge(job_mm, n + 1)
                    cols, bank = slice(c * BANK, (c + 1) * BANK), bank_of(n)
                    if kind == "v":
                        for g in range(G1):
                            ins = act.activation(v[g][:, 4 * c:4 * c + 4, 0, :], bank.rearrange("p (t g d) -> p t g d", g=G1, d=D1)[:, :, g, :], ACT.Copy)
                        ins.then_inc(job_hi, 1)
                    elif kind == "qq":
                        for h in range(2):
                            ins = act.activation(q[h][0:D1, cols], bank[h * D1:(h + 1) * D1, :], ACT.Copy)
                        ins.then_inc(job_hi, 1)
                    elif kind == "q":
                        act.wait_ge(scores_mm, (index - 1) * NT)
                        act.activation(q[index % 2][0:D1, cols], bank[0:D1, :], ACT.Copy).then_inc(job_hi, 1)
                    else:
                        act.activation(khi[index][:, cols], bank, ACT.Copy).then_inc(job_hi, 1)

                def probs_hi(s):
                    chunk = s // 4
                    if s % 4 == 0 and chunk >= 2:
                        act.wait_ge(att_mm, chunk - 1)
                    for n in range(2):
                        act.wait_ge(turn_mm, 2 * s + n + 1)
                        if s == 4 and n == 0:
                            act.wait_ge(job_mm, jobs.index(("k", 1, 1)) + 1)
                        act.activation(pT[chunk % 2].hi[:, 4 * n:4 * n + 4, (s % 4) * P:(s % 4 + 1) * P], p_turn[n][:, :, :], ACT.Copy)\
                           .then_inc(turn_hi, 1)

                def exp(s):
                    act.wait_ge(max_done, s + 1)
                    act.activation(negmax[:, s % 4:s % 4 + 1], negmax[:, s % 4:s % 4 + 1], ACT.Copy, scale=SCALE).then_inc(bias_done, 1)
                    if s >= 4:
                        act.wait_ge(turn_mm, 2 * (s - 3))
                    if s == 3:
                        act.wait_ge(wo_ready, 1)
                    act.wait_ge(bias_done, s + 1)
                    act.activation(probs[s % 4], p_scores[s % 2][:, :], ACT.Exp, scale=SCALE,
                                   bias=negmax[:, s % 4:s % 4 + 1], accum_out=rowsum[:, s % 4:s % 4 + 1]).then_inc(exp_done, 1)

                def attended_hi(chunk):
                    act.wait_ge(att_mm, chunk + 1)
                    if chunk == 4:
                        act.wait_ge(out_mm, 4)
                    act.activation(att.hi[:, chunk // 2 % 2, chunk % 2 * BANK:(chunk % 2 + 1) * BANK], p_att[:, :], ACT.Copy).then_inc(att_hi, 1)

                load_table(act, m, ACT.Exp, 1)
                for n, job in jobs_of(-1):
                    job_high(n, *job)
                for s in range(HS + LAG):
                    if s >= LAG:
                        probs_hi(s - LAG)
                    if s < HS:
                        exp(s)
                    if s > ATT and (s - ATT) % 4 == 3:
                        attended_hi((s - ATT) // 4)
                    for n, job in jobs_of(s):
                        job_high(n, *job)
                for chunk in range((HS + LAG - ATT) // 4, 2 * H1):
                    attended_hi(chunk)

            @block.vector
            def _(dve):
                def job_low(n, kind, index, c):
                    dve.wait_ge(job_hi, n + 1)
                    cols, bank = slice(c * BANK, (c + 1) * BANK), bank_of(n)
                    if kind == "v":
                        for g in range(G1):
                            out = v[g][:, 4 * c:4 * c + 4, :, :]
                            ins = dve.tensor_tensor(out[:, :, 1, :], bank.rearrange("p (t g d) -> p t g d", g=G1, d=D1)[:, :, g, :],
                                                    as_f32(out[:, :, 0, :]), ALU.subtract)
                    elif kind == "k":
                        ins = dve.tensor_tensor(klo[index][:, cols], bank, as_f32(khi[index][:, cols]), ALU.subtract)
                    else:
                        for h in range(2 if kind == "qq" else 1):
                            out = q[(index + h) % 2]
                            ins = dve.tensor_tensor(out[D1:P, cols], bank[h * D1:(h + 1) * D1, :], as_f32(out[0:D1, cols]), ALU.subtract)
                    ins.then_inc(proj_free, 1)

                def maximum(s):
                    dve.wait_ge(scores_mm, s + 1)
                    dve.tensor_reduce(negmax[:, s % 4:s % 4 + 1], p_scores[s % 2][:, :], AX.X, ALU.max, negate=True).then_inc(max_done, 1)

                def inverse_sum(s):
                    dve.wait_ge(exp_done, s + 1)
                    dve.reciprocal(rinv[:, s % 4:s % 4 + 1], rowsum[:, s % 4:s % 4 + 1]).then_inc(rinv_done, 1)

                def probs_lo(s):
                    for n in range(2):
                        out = pT[s // 4 % 2][:, 4 * n:4 * n + 4, (s % 4) * P:(s % 4 + 1) * P]
                        dve.wait_ge(turn_hi, 2 * s + n + 1)
                        dve.tensor_tensor(out.lo, p_turn[n][:, :, :], as_f32(out.hi), ALU.subtract).then_inc(turn_lo, 1)

                def attended_lo(chunk):
                    out = att[:, chunk // 2 % 2, chunk % 2 * BANK:(chunk % 2 + 1) * BANK]
                    dve.wait_ge(att_hi, chunk + 1)
                    dve.tensor_tensor(out.lo, p_att[:, :], as_f32(out.hi), ALU.subtract).then_inc(att_lo, 1)

                def add_out(pair_index, j):
                    dve.wait_ge(out_mm, 4 * pair_index + j + 1)
                    dve.wait_ge(residual, 2 * NT)
                    rows = m.x[:, 2 * j:2 * j + 2, :]
                    dve.tensor_tensor(rows, out_bank(pair_index, j).rearrange("p (n d) -> p n d", n=2), rows, ALU.add)\
                       .then_inc(proj_free, 1)

                for n, job in jobs_of(-1):
                    job_low(n, *job)
                for s in range(HS + LAG):
                    if s < HS:
                        maximum(s)
                    if 1 <= s <= HS:
                        inverse_sum(s - 1)
                    if s >= LAG:
                        probs_lo(s - LAG)
                    if s > ATT and (s - ATT) % 4 == 3:
                        attended_lo((s - ATT) // 4)
                    for n, job in jobs_of(s):
                        job_low(n, *job)
                    for j in out_slots.get(s, ()):
                        add_out(0, j)
                for chunk in range((HS + LAG - ATT) // 4, 2 * H1):
                    attended_lo(chunk)
                for j in range(4):
                    add_out(1, j)

            @block.gpsimd
            def _(pool):
                chain = Chain(pool, sem("wo_chain"))
                pool.wait_ge(m.staged1, 80)
                for h in range(H1):
                    chain.step(pool.tensor_tensor(wo_in[:, h, :], wo_in[:, h, :], m.gate[:, 1, 0, :], ALU.mult))
                chain.settle()
                chain.run(pool.tensor_scalar(wo.hi, wo_in[:, :, :], 1.0, 1.0, ALU.mult, ALU.mult))
                pool.tensor_tensor(wo.lo, wo_in[:, :, :], as_f32(wo.hi), ALU.subtract).then_inc(wo_ready, 1)
                for s in range(HS):
                    pool.wait_ge(rinv_done, s + 1)
                    pool.tensor_scalar(probs[s % 4], probs[s % 4], rinv[:, s % 4:s % 4 + 1], 1.0, ALU.mult, ALU.mult)\
                        .then_inc(normed, 1)
                    n, odd = divmod(s - FIRST_RESIDUAL, 2)
                    if 0 <= n < NT and not odd:
                        gated, rows = h_row[:, n, :], m.x[:, n, :]
                        pool.tensor_tensor(gated, gated, m.gate[:, 1, 0, :], ALU.mult).then_inc(residual, 1)
                        pool.wait_ge(residual, 2 * n + 1)
                        pool.tensor_tensor(rows, rows, gated, ALU.add).then_inc(residual, 1)
                    e = s - FIRST_GATED
                    if 0 <= e < NE + 1:
                        if e == 0:
                            pool.wait_ge(m.staged, 48 + 160)
                        expert_w2 = m.staging[:, 4096 + e * DM:4096 + (e + 1) * DM]
                        pool.tensor_tensor(expert_w2, expert_w2, m.gate[:, 1, 1, :], ALU.mult).then_inc(m.w2_gated, 1)


def ffn1(nc, a, m, sems, sb, split):
    transposed_rows(nc, m, sems, sb, 1, 6, "ln3")
    E8 = NE + 1
    with ExitStack() as ctx:
        def buf(name, shape, dt=F32):
            return sb("ff1_" + name, shape, dt, ctx)

        def sem(name):
            return sems("ff1_" + name)

        w1_in = m.staging[:, 0:4096].rearrange("p (e kn) -> p e kn", e=E8)
        w2_in = m.staging[:, 4096:6144].rearrange("p (e n) -> p e n", e=E8)
        w1, w2 = split("ff1_w1", [P, E8, KD * 2 * FE], ctx), split("ff1_w2", [P, E8, DM], ctx)
        aff, marked = buf("aff", [P, NT, 16]), buf("marked", [P, NT, 16])
        best, best2 = buf("best", [P, NT, 8]), buf("best2", [P, NT, 8])
        mask, score = buf("mask", [P, NT, E8]), buf("score", [P, NT, E8])
        PAD = 8
        ranks = [buf(f"ranks{n}", [E8, S + PAD]) for n in range(2)]
        logits = ranks[1][0:NE, 0:S]
        positive, weight = m.staging1[0:E8, 0:S], m.staging1[0:E8, S:2 * S]
        row_best, row_last = buf("row_best", [E8, 8]), buf("row_last", [E8, 8])
        row_weight = buf("row_weight", [P, NT, E8])
        x1, act2, mid = (buf(n, [P, 2, BANK]) for n in ("x1", "act2", "mid"))
        fed = [split(f"ff1_fed{n}", [P, S], ctx) for n in range(2)]
        y = buf("y", [P, NE - 1, NT, DM])
        scaled = x1[:, :, 0:DM]
        p_y = [ctx.enter_context(nc.psum_tensor(f"ff1_y{n}", [P, 2, DM], F32)) for n in range(4)]
        p_x1, p_x2 = ([ctx.enter_context(nc.psum_tensor(f"ff1_{s}{n}", [P, BANK], F32)) for n in range(2)] for s in ("px1", "px2"))
        by_expert = [p_y[n][0:E8, :, :].rearrange("e a b -> e (a b)") for n in range(2)]
        by_row = p_y[2][:, 0, 0:NT * E8].rearrange("p (t e) -> p t e", e=E8)
        p_weight = p_x1[0][:, 0:NT * E8].rearrange("p (t e) -> p t e", e=E8)
        logits_mm, logits_read, logits_turned, aff_done, score_done, ranks_mm, ranks_read, positive_done = (
            sem(n) for n in ("logits_mm", "logits_read", "logits_turned", "aff_done", "score_done", "ranks_mm", "ranks_read", "positive_done"))
        rank_chain, w1_hi, w1_ready, w2_hi, w2_ready = (
            sem(n) for n in ("rank_chain", "w1_hi", "w1_ready", "w2_hi", "w2_ready"))
        up_mm, x1_read, x2_read, mid_done = (sem(n) for n in ("up_mm", "x1_read", "x2_read", "mid_done"))
        fed_hi, down_mm, y_read, shared_added = (sem(n) for n in ("fed_hi", "down_mm", "y_read", "shared_added"))
        fed_lo = [sem(f"fed_lo{n}") for n in range(2)]
        weight_done, weight_mm, weight_read, routed_added = (sem(n) for n in ("weight_done", "weight_mm", "weight_read", "routed_added"))
        aff_cleared, scaled_done, pool_added, stored = sem("aff_cleared"), sem("scaled_done"), sem("pool_added"), sem("stored")
        PAIRS = NT // 2
        VECTOR_FEEDS = (0,)
        FEED_ROUNDS, SHARED_AT = {0: 0}, 3
        POOL_PAIR = PAIRS - 1

        def of_expert(e, t):
            return p_y[t // 2][:, t % 2, :] if e == NE else y[:, e - 1, t, :]

        def returned(engine, e, t):
            if e == NE:
                engine.wait_ge(down_mm, PAIRS * NE + t // 2 + 1)
            else:
                engine.wait_ge(y_read, PAIRS * (e - 1) + t // 2 + 1)

        with nc.Block() as block:
            @block.sync
            def _(sp):
                rows = a["out"].rearrange("o (n p) d -> p (o n) d", p=P)
                for j in range(PAIRS):
                    if j == POOL_PAIR:
                        sp.wait_ge(pool_added, 2 * NE)
                    else:
                        sp.wait_ge(routed_added, 2 * POOL_PAIR * (NE - 1) + 2 * (j + 1))
                    sp.dma_start(rows[:, 2 * j:2 * j + 2, :], m.x[:, 2 * j:2 * j + 2, :]).then_inc(stored, 16)
                sp.wait_ge(stored, 16 * PAIRS)

            @block.tensor
            def _(pe):
                def up(e, c):
                    pe.wait_ge(w1_ready, e + 1)
                    n = 2 * e + c
                    for half, (bank, read) in enumerate(((p_x1, x1_read), (p_x2, x2_read))):
                        if n >= 2:
                            pe.wait_ge(read, n - 1)
                        for k in range(KD):
                            at = k * 2 * FE + half * FE
                            mm = product(pe, bank[c][:, :], w1[:, e, at:at + FE], m.hT[:, k, c * BANK:(c + 1) * BANK], k == 0, k == KD - 1)
                        mm.then_inc(up_mm, 1)

                def down(e):
                    pe.wait_ge(w2_ready, e + 1)
                    for n in range(2):
                        pe.wait_ge(fed_lo[n], e + 1)
                    if e == 0:
                        pe.wait_ge(positive_done, 2)
                        pe.wait_ge(aff_done, 1)
                    for j in range(PAIRS):
                        if e == 1:
                            pe.wait_ge(shared_added, j + 1)
                        elif e:
                            pe.wait_ge(y_read, PAIRS * (e - 2) + j + 1)
                        for n in range(2):
                            rows = slice((2 * j + n) * P, (2 * j + n + 1) * P)
                            mm = product(pe, p_y[j][:, n, :], fed[e % 2][:, rows], w2[:, e, :], True, True)
                        mm.then_inc(down_mm, 1)

                for c in range(2):
                    for k in range(KD):
                        mm = product(pe, by_expert[c][0:NE, :], m.gate_w[:, k, :], m.hT[:, k, c * BANK:(c + 1) * BANK], k == 0, k == KD - 1)
                    mm.then_inc(logits_mm, 1)
                up(0, 0)
                pe.wait_ge(logits_read, 2)
                for t in range(NT):
                    mm = pe.transpose(by_row[:, t, 0:NE], logits[:, t * P:(t + 1) * P], m.ident[0:NE, 0:NE])
                mm.then_inc(logits_turned, 1)
                up(0, 1)
                pe.wait_ge(score_done, 1)
                for t in range(NT):
                    mm = pe.transpose(by_expert[t // 4][:, t % 4 * P:(t % 4 + 1) * P], score[:, t, :], m.ident[:, :])
                mm.then_inc(ranks_mm, 1)
                for e in range(1, E8):
                    for c in range(2):
                        up(e, c)
                    if e == NE:
                        pe.wait_ge(x1_read, 2 * NE + 1)
                        pe.wait_ge(weight_done, 1)
                        for t in range(NT):
                            mm = pe.transpose(p_weight[:, t, :], weight[:, t * P:(t + 1) * P], m.ident[0:E8, 0:E8])
                        mm.then_inc(weight_mm, 1)
                    down(e - 1)
                down(NE)

            @block.scalar
            def _(act):
                def split_hi(e):
                    act.activation(w1.hi[:, e, :], w1_in[:, e, :], ACT.Copy).then_inc(w1_hi, 1)

                def halves(e, c):
                    n = 2 * e + c
                    act.wait_ge(up_mm, 2 * n + 1)
                    if n >= 2:
                        act.wait_ge(mid_done, n - 1)
                    act.activation(x1[:, c, :], p_x1[c][:, :], ACT.Copy).then_inc(x1_read, 1)
                    act.wait_ge(up_mm, 2 * n + 2)
                    act.activation(act2[:, c, :], p_x2[c][:, :], ACT.Silu).then_inc(x2_read, 1)

                def feed_hi(e, c):
                    act.wait_ge(mid_done, 2 * e + c + 1)
                    if e >= 2 and c == 0:
                        act.wait_ge(down_mm, PAIRS * (e - 1))
                    act.activation(fed[e % 2].hi[:, c * BANK:(c + 1) * BANK], mid[:, c, :], ACT.Copy).then_inc(fed_hi, 1)

                def keep(e):
                    for j in range(PAIRS):
                        act.wait_ge(down_mm, PAIRS * e + j + 1)
                        act.activation(y[:, e - 1, 2 * j:2 * j + 2, :], p_y[j][:, :, :], ACT.Copy).then_inc(y_read, 1)

                act.wait_ge(m.staged, 48 + 160)
                split_hi(0)
                split_hi(1)
                load_table(act, m, ACT.Sigmoid, 2)
                for c in range(2):
                    act.wait_ge(logits_mm, c + 1)
                    act.activation(logits[:, c * BANK:(c + 1) * BANK], by_expert[c][0:NE, :], ACT.Identity, bias=m.expert_bias[:, :])\
                       .then_inc(logits_read, 1)
                act.wait_ge(aff_cleared, 1)
                act.wait_ge(logits_turned, 1)
                act.activation(aff[:, :, 0:NE], by_row[:, :, 0:NE], ACT.Sigmoid).then_inc(aff_done, 1)
                for e in range(E8):
                    halves(e, 0)
                    halves(e, 1)
                    feed_hi(e, 0)
                    if e + 2 < E8:
                        split_hi(e + 2)
                    feed_hi(e, 1)
                    if e == 0:
                        for c in range(2):
                            act.wait_ge(ranks_read, c + 1)
                            act.activation(positive[:, c * BANK:(c + 1) * BANK], by_expert[c], ACT.Relu).then_inc(positive_done, 1)
                    if e >= 2:
                        keep(e - 1)
                act.wait_ge(weight_read, 1)
                for e in range(1, E8):
                    for n in range(2):
                        t = 2 * POOL_PAIR + n
                        if e > 1:
                            act.wait_ge(pool_added, 2 * (e - 2) + n + 1)
                        returned(act, e, t)
                        act.activation(scaled[:, n, :], of_expert(e, t), ACT.Copy, scale=row_weight[:, t, e - 1:e]).then_inc(scaled_done, 1)

            @block.vector
            def _(dve):
                def feed_lo(e):
                    dve.wait_ge(fed_hi, 2 * e + 2)
                    out = fed[e % 2][:, BANK:S]
                    dve.tensor_tensor(out.lo, mid[:, 1, :], as_f32(out.hi), ALU.subtract).then_inc(fed_lo[1], 1)

                def add_shared():
                    for j in range(PAIRS):
                        dve.wait_ge(down_mm, j + 1)
                        rows = m.x[:, 2 * j:2 * j + 2, :]
                        dve.tensor_tensor(rows, p_y[j][:, :, :], rows, ALU.add).then_inc(shared_added, 1)

                chain = Chain(dve, rank_chain)
                for e in range(2):
                    dve.wait_ge(w1_hi, e + 1)
                    dve.tensor_tensor(w1.lo[:, e, :], w1_in[:, e, :], as_f32(w1.hi[:, e, :]), ALU.subtract).then_inc(w1_ready, 1)
                dve.memset(aff[:], -1.0).then_inc(aff_cleared, 1)
                for tile, value in ((best2, -1.0), (row_last, -1.0), (score, -1.0), (ranks[0], -1.0)):
                    chain.step(dve.memset(tile[:], value))

                chain.settle()
                dve.wait_ge(aff_done, 1)
                for t in range(NT):
                    chain.step(dve.max(best[:, t, :], aff[:, t, :]))
                chain.settle()
                chain.run(dve.tensor_copy(best2[:, :, 0:TOPK], best[:, :, 0:TOPK]))
                for t in range(NT):
                    chain.step(dve.match_replace(marked[:, t, :], best2[:, t, :], aff[:, t, :], -5.0))
                chain.settle()
                chain.run(dve.tensor_scalar(mask[:, :, 0:NE], marked[:, :, 0:NE], -5.0, None, ALU.is_equal))
                chain.run(dve.tensor_tensor(marked[:, :, 0:NE], aff[:, :, 0:NE], mask[:, :, 0:NE], ALU.mult))
                dve.scalar_tensor_tensor(out=score[:, :, 0:NE], in0=mask[:, :, 0:NE], scalar=-1.0, in1=marked[:, :, 0:NE],
                                         op0=ALU.add, op1=ALU.add).then_inc(score_done, 1)
                dve.memset(ranks[1][:, S:S + PAD], -1.0)
                dve.wait_ge(ranks_mm, 1)
                for n in range(2):
                    dve.tensor_copy(ranks[0][:, n * BANK:(n + 1) * BANK], by_expert[n]).then_inc(ranks_read, 1)
                dve.wait_ge(ranks_read, 2)

                full, rest = divmod(CAPACITY, 8)
                for r in range(full):
                    src, dst = ranks[r % 2], ranks[1 - r % 2]
                    chain.run(dve.max(row_best[:, :], src[:, :]))
                    chain.run(dve.match_replace(dst[:, :], row_best[:, :], src[:, :], -3.0))
                    if r in FEED_ROUNDS:
                        feed_lo(FEED_ROUNDS[r])
                    if r == SHARED_AT:
                        add_shared()
                src, dst = ranks[full % 2], ranks[1 - full % 2]
                chain.run(dve.max(row_best[:, :], src[:, :]))
                chain.run(dve.tensor_copy(row_last[:, 0:rest], row_best[:, 0:rest]))
                chain.run(dve.match_replace(dst[:, :], row_last[:, :], src[:, :], -3.0))
                dve.wait_ge(positive_done, 2)
                dve.scalar_tensor_tensor(out=weight, in0=dst[:, 0:S], scalar=-3.0, in1=positive,
                                         op0=ALU.is_equal, op1=ALU.mult).then_inc(weight_done, 1)
                dve.wait_ge(weight_mm, 1)
                dve.tensor_copy(row_weight[:, :, :], p_weight).then_inc(weight_read, 1)
                dve.wait_ge(weight_read, 1)
                dve.wait_ge(shared_added, PAIRS)
                for e in range(1, E8):
                    for t in range(2 * POOL_PAIR):
                        returned(dve, e, t)
                        if e > 1:
                            dve.wait_ge(routed_added, 2 * POOL_PAIR * (e - 2) + t + 1)
                        dve.scalar_tensor_tensor(out=m.x[:, t, :], in0=of_expert(e, t), scalar=row_weight[:, t, e - 1:e], in1=m.x[:, t, :],
                                                 op0=ALU.mult, op1=ALU.add).then_inc(routed_added, 1)

            @block.gpsimd
            def _(pool):
                def w1_low(e):
                    pool.wait_ge(w1_hi, e + 1)
                    if e == 2:
                        pool.wait_ge(w1_ready, 2)
                    pool.tensor_tensor(w1.lo[:, e, :], w1_in[:, e, :], as_f32(w1.hi[:, e, :]), ALU.subtract).then_inc(w1_ready, 1)

                def middle(e, c):
                    n = 2 * e + c
                    pool.wait_ge(x2_read, n + 1)
                    pool.wait_ge(x1_read, n + 1)
                    if e:
                        pool.wait_ge(fed_lo[c], e)
                    pool.tensor_tensor(mid[:, c, :], x1[:, c, :], act2[:, c, :], ALU.mult).then_inc(mid_done, 1)

                def feed_lo(e, c):
                    pool.wait_ge(fed_hi, 2 * e + c + 1)
                    out = fed[e % 2][:, c * BANK:(c + 1) * BANK]
                    pool.tensor_tensor(out.lo, mid[:, c, :], as_f32(out.hi), ALU.subtract).then_inc(fed_lo[c], 1)

                def split_w2(e):
                    pool.wait_ge(m.w2_gated, e + 1)
                    pool.tensor_scalar(w2.hi[:, e, :], w2_in[:, e, :], 1.0, 1.0, ALU.mult, ALU.mult).then_inc(w2_hi, 1)
                    pool.wait_ge(w2_hi, e + 1)
                    pool.tensor_tensor(w2.lo[:, e, :], w2_in[:, e, :], as_f32(w2.hi[:, e, :]), ALU.subtract).then_inc(w2_ready, 1)

                pool.wait_ge(m.staged, 48 + 160)
                split_w2(0)
                for e in range(E8):
                    middle(e, 0)
                    middle(e, 1)
                    feed_lo(e, 0)
                    if e not in VECTOR_FEEDS:
                        feed_lo(e, 1)
                    if e + 2 < E8:
                        w1_low(e + 2)
                    if e + 1 < E8:
                        split_w2(e + 1)
                pool.wait_ge(shared_added, PAIRS)
                for e in range(1, E8):
                    for n in range(2):
                        rows = m.x[:, 2 * POOL_PAIR + n, :]
                        pool.wait_ge(scaled_done, 2 * (e - 1) + n + 1)
                        pool.tensor_tensor(rows, scaled[:, n, :], rows, ALU.add).then_inc(pool_added, 1)


def constants():
    freqs = (np.float32(1.0) / np.float32(10000.0) ** (np.arange(0, D0, 2, dtype=np.float32) / np.float32(D0))).astype(np.float32)
    ang = (np.arange(S, dtype=np.float32)[:, None] * freqs[None, :]).astype(np.float32)
    root = np.float64(D0) ** -0.25
    c, s = (np.cos(ang.astype(np.float64)) * root).T, (np.sin(ang.astype(np.float64)) * root).T
    causal = np.where(np.arange(P)[None, :] > np.arange(P)[:, None], MASK_NEG, 0.0)
    return {
        "cos": np.concatenate([c, c]).astype(np.float32),
        "sin": np.concatenate([-s, s]).astype(np.float32),
        "mask": causal.astype(np.float32),
        "ident": np.eye(P, dtype=np.float32),
    }


INPUTS = ["L0_attn_x", "L0_attn_Wqkv", "L0_attn_Wo", "L0_ffn_w_gate", "L0_ffn_w_up", "L0_ffn_w_down", "L0_c", "L0_wmod",
          "L1_attn_norm_scale", "L1_attn_split_scale", "L1_attn_Wq", "L1_attn_Wk", "L1_attn_Wv", "L1_attn_Wo",
          "L1_ffn_gate_w", "L1_ffn_expert_bias", "L1_ffn_shared_w1", "L1_ffn_shared_w2", "L1_ffn_routed_w1",
          "L1_ffn_routed_w2", "L1_c", "L1_wmod"]


def columns(v):
    return np.asarray(v).reshape(-1, P).T


LAYOUTS = {
    "L0_c": columns, "L1_c": columns,
    "L1_attn_norm_scale": columns, "L1_attn_split_scale": columns,
    "L1_attn_Wq": np.transpose, "L1_attn_Wk": np.transpose, "L1_attn_Wv": np.transpose, "L1_attn_Wo": np.transpose,
    "L1_ffn_expert_bias": lambda v: np.asarray(v).reshape(-1, 1),
}


def kernel(**inputs):
    import concourse.bacc as bacc
    from concourse.bass_utils import run_bass_kernel_spmd

    nc = bacc.Bacc("TRN2", target_bir_lowering=False, num_devices=1)
    arrays, aps = {}, {}
    for name, value in [(n, inputs[n]) for n in INPUTS] + list(constants().items()):
        if name in LAYOUTS:
            value = LAYOUTS[name](value)
        value = np.ascontiguousarray(value)
        arrays[name] = value
        aps[name] = nc.dram_tensor(name, value.shape, mybir.dt.from_np(value.dtype), kind="ExternalInput").ap()
    aps["out"] = nc.dram_tensor("out", (1, S, DM), F32, kind="ExternalOutput").ap()
    build(nc, aps)
    result = run_bass_kernel_spmd(nc, [arrays], core_ids=[0])
    return result.results[0]["out"]
```
